# Optimizing a Trainium2 kernel written in Bass

```python
import numpy as np
import jax
import jax.numpy as jnp

def _softmax(x, axis=-1):
    return jax.nn.softmax(x, axis=axis)

def _gelu(x):
    return jax.nn.gelu(x, approximate=True)

def _silu(x):
    return jax.nn.silu(x)

def _sigmoid(x):
    return jax.nn.sigmoid(x)

def _layernorm(x, axis=-1, eps=1e-05):
    m = jnp.mean(x, axis=axis, keepdims=True)
    v = jnp.var(x, axis=axis, keepdims=True)
    return (x - m) / jnp.sqrt(v + eps)

def _scatter_add(tgt, idx, src, axis=0):
    return tgt.at[idx].add(src)

def _segment_sum(src, seg, n):
    return jax.ops.segment_sum(src, seg, n)
kernel_name = 'mk_gps_d1_gnn_r8_370fe0'

def setup_inputs(seed: int=0):
    np.random.seed(seed)
    _w = jnp.asarray

    def _rec_inputs():
        import jax
        import jax.numpy as jnp
        _gk = jax.random.key(seed)
        x = -0.0006008 + 1.001 * jax.random.normal(jax.random.fold_in(_gk, 1), (6250, 256), jnp.float32)
        _s = jax.random.randint(jax.random.fold_in(_gk, 2), (50000,), 0, 6250, jnp.int32)
        _d = jax.random.randint(jax.random.fold_in(_gk, 3), (50000,), 0, 6250, jnp.int32)
        _loop = jnp.arange(6250, dtype=jnp.int32)
        src = jnp.concatenate([_s, _d, _loop])
        dst = jnp.concatenate([_d, _s, _loop])
        _o = jnp.argsort(dst, stable=True)
        src = src[_o]
        dst = dst[_o]
        return (x, src, dst)
    x, src, dst = _rec_inputs()

    def _L0_gnn_setup():
        import jax, jax.numpy as jnp
        import numpy as np
        N_NODES = 1250
        N_RAND_EDGES = 40000
        IN_DIM = 256
        HIDDEN = 64
        HEADS = 8
        OUT_DIM = 256
        NEG_SLOPE = 0.2

        def gat_conv(x, W, attn_l, attn_r, src, dst, n_nodes):
            H, D = attn_l.shape
            feat = (x @ W).reshape(n_nodes, H, D)
            el = jnp.einsum('nhd,hd->nh', feat, attn_l)
            er = jnp.einsum('nhd,hd->nh', feat, attn_r)
            e = jax.nn.leaky_relu(el[src] + er[dst], NEG_SLOPE)
            m = jax.ops.segment_max(e, dst, num_segments=n_nodes)
            ex = jnp.exp(e - m[dst])
            denom = jax.ops.segment_sum(ex, dst, num_segments=n_nodes)
            alpha = ex / denom[dst]
            out = jax.ops.segment_sum(alpha[:, :, None] * feat[src], dst, num_segments=n_nodes)
            return out.reshape(n_nodes, H * D)
        key = jax.random.key(seed)
        ks = jax.random.split(key, 9)
        h = jax.random.normal(ks[0], (N_NODES, IN_DIM), dtype=jnp.float32)
        src = jnp.concatenate([jax.random.randint(ks[1], (N_RAND_EDGES,), 0, N_NODES, dtype=jnp.int32), jnp.arange(N_NODES, dtype=jnp.int32)])
        dst = jnp.concatenate([jax.random.randint(ks[2], (N_RAND_EDGES,), 0, N_NODES, dtype=jnp.int32), jnp.arange(N_NODES, dtype=jnp.int32)])

        def glorot(k, shape):
            fan = shape[0] + shape[-1]
            s = jnp.sqrt(2.0 / fan).astype(jnp.float32)
            return jax.random.normal(k, shape, dtype=jnp.float32) * s
        W1 = glorot(ks[3], (IN_DIM, HEADS * HIDDEN))
        attn_l1 = glorot(ks[4], (HEADS, HIDDEN))
        attn_r1 = glorot(ks[5], (HEADS, HIDDEN))
        W2 = glorot(ks[6], (HEADS * HIDDEN, OUT_DIM))
        attn_l2 = glorot(ks[7], (1, OUT_DIM))
        attn_r2 = glorot(ks[8], (1, OUT_DIM))
        return {'h': h, 'W1': W1, 'attn_l1': attn_l1, 'attn_r1': attn_r1, 'W2': W2, 'attn_l2': attn_l2, 'attn_r2': attn_r2, 'src': src, 'dst': dst}
    _L0_gnn_all = _L0_gnn_setup()
    _L0_gnn_in = {k: v for k, v in _L0_gnn_all.items() if k in ('W1', 'attn_l1', 'attn_r1', 'W2', 'attn_l2', 'attn_r2')}
    del _L0_gnn_all

    def _L0_mix_setup():
        import jax, jax.numpy as jnp
        import numpy as np
        NUM_HEADS = 8
        key = jax.random.key(seed)
        ks = jax.random.split(key, 5)
        B, N, C = (8, 2048, 256)
        x = jax.random.normal(ks[0], (B, N, C), dtype=jnp.float32)
        Wq = jax.random.normal(ks[1], (C, C), dtype=jnp.float32) * 0.02
        Wkv = jax.random.normal(ks[2], (2 * C, C), dtype=jnp.float32) * 0.02
        Wproj = jax.random.normal(ks[3], (C, C), dtype=jnp.float32) * 0.02
        bproj = jnp.zeros((C,), dtype=jnp.float32)
        return {'x': x, 'Wq': Wq, 'Wkv': Wkv, 'Wproj': Wproj, 'bproj': bproj}
    _L0_mix_all = _L0_mix_setup()
    _L0_mix_in = {k: v for k, v in _L0_mix_all.items() if k in ('Wq', 'Wkv', 'Wproj', 'bproj')}
    del _L0_mix_all

    def _L0_ffn_setup():
        import jax, jax.numpy as jnp
        import numpy as np
        BN_EPS = 0.001

        def _bn(h, g, b, m, v):
            return g * (h - m) * jax.lax.rsqrt(v + BN_EPS) + b
        key = jax.random.key(seed)
        ks = jax.random.split(key, 8)
        B, F, Df = (256, 64, 256)
        E, H, D = (8, 256, 256)
        s1 = 1.0 / np.sqrt(Df)
        s2 = 1.0 / np.sqrt(H)
        return {'x': jax.random.normal(ks[0], (B, F, Df), jnp.float32), 'Wr': jax.random.normal(ks[1], (Df, E), jnp.float32) * s1, 'br': jnp.zeros((E,), jnp.float32), 'W1': jax.random.normal(ks[2], (E, Df, H), jnp.float32) * s1, 'b1': jnp.zeros((E, H), jnp.float32), 'g1': jnp.ones((E, H), jnp.float32), 'be1': jnp.zeros((E, H), jnp.float32), 'm1': jnp.zeros((E, H), jnp.float32), 'v1': jnp.ones((E, H), jnp.float32), 'W2': jax.random.normal(ks[3], (E, H, H), jnp.float32) * s2, 'b2': jnp.zeros((E, H), jnp.float32), 'g2': jnp.ones((E, H), jnp.float32), 'be2': jnp.zeros((E, H), jnp.float32), 'm2': jnp.zeros((E, H), jnp.float32), 'v2': jnp.ones((E, H), jnp.float32), 'Wo': jax.random.normal(ks[4], (E, H, D), jnp.float32) * s2, 'bo': jnp.zeros((E, D), jnp.float32)}
    _L0_ffn_all = _L0_ffn_setup()
    _L0_ffn_in = {k: v for k, v in _L0_ffn_all.items() if k in ('Wr', 'br', 'W1', 'b1', 'g1', 'be1', 'm1', 'v1', 'W2', 'b2', 'g2', 'be2', 'm2', 'v2', 'Wo', 'bo')}
    del _L0_ffn_all
    return {'x': x, 'src': src, 'dst': dst, 'L0_gnn_W1': _L0_gnn_in['W1'], 'L0_gnn_attn_l1': _L0_gnn_in['attn_l1'], 'L0_gnn_attn_r1': _L0_gnn_in['attn_r1'], 'L0_gnn_W2': _L0_gnn_in['W2'], 'L0_gnn_attn_l2': _L0_gnn_in['attn_l2'], 'L0_gnn_attn_r2': _L0_gnn_in['attn_r2'], 'L0_mix_Wq': _L0_mix_in['Wq'], 'L0_mix_Wkv': _L0_mix_in['Wkv'], 'L0_mix_Wproj': _L0_mix_in['Wproj'], 'L0_mix_bproj': _L0_mix_in['bproj'], 'L0_ffn_Wr': _L0_ffn_in['Wr'], 'L0_ffn_br': _L0_ffn_in['br'], 'L0_ffn_W1': _L0_ffn_in['W1'], 'L0_ffn_b1': _L0_ffn_in['b1'], 'L0_ffn_g1': _L0_ffn_in['g1'], 'L0_ffn_be1': _L0_ffn_in['be1'], 'L0_ffn_m1': _L0_ffn_in['m1'], 'L0_ffn_v1': _L0_ffn_in['v1'], 'L0_ffn_W2': _L0_ffn_in['W2'], 'L0_ffn_b2': _L0_ffn_in['b2'], 'L0_ffn_g2': _L0_ffn_in['g2'], 'L0_ffn_be2': _L0_ffn_in['be2'], 'L0_ffn_m2': _L0_ffn_in['m2'], 'L0_ffn_v2': _L0_ffn_in['v2'], 'L0_ffn_Wo': _L0_ffn_in['Wo'], 'L0_ffn_bo': _L0_ffn_in['bo']}

def reference(x, src, dst, L0_gnn_W1, L0_gnn_attn_l1, L0_gnn_attn_r1, L0_gnn_W2, L0_gnn_attn_l2, L0_gnn_attn_r2, L0_mix_Wq, L0_mix_Wkv, L0_mix_Wproj, L0_mix_bproj, L0_ffn_Wr, L0_ffn_br, L0_ffn_W1, L0_ffn_b1, L0_ffn_g1, L0_ffn_be1, L0_ffn_m1, L0_ffn_v1, L0_ffn_W2, L0_ffn_b2, L0_ffn_g2, L0_ffn_be2, L0_ffn_m2, L0_ffn_v2, L0_ffn_Wo, L0_ffn_bo):
    import jax
    import jax.numpy as jnp

    def _L0_gnn_ref(h, W1, attn_l1, attn_r1, W2, attn_l2, attn_r2, src, dst):
        import jax, jax.numpy as jnp
        import numpy as np
        N_NODES = 1250
        N_RAND_EDGES = 40000
        IN_DIM = 256
        HIDDEN = 64
        HEADS = 8
        OUT_DIM = 256
        NEG_SLOPE = 0.2

        def gat_conv(x, W, attn_l, attn_r, src, dst, n_nodes):
            H, D = attn_l.shape
            feat = (x @ W).reshape(n_nodes, H, D)
            el = jnp.einsum('nhd,hd->nh', feat, attn_l)
            er = jnp.einsum('nhd,hd->nh', feat, attn_r)
            e = jax.nn.leaky_relu(el[src] + er[dst], NEG_SLOPE)
            m = jax.ops.segment_max(e, dst, num_segments=n_nodes)
            ex = jnp.exp(e - m[dst])
            denom = jax.ops.segment_sum(ex, dst, num_segments=n_nodes)
            alpha = ex / denom[dst]
            out = jax.ops.segment_sum(alpha[:, :, None] * feat[src], dst, num_segments=n_nodes)
            return out.reshape(n_nodes, H * D)
        n = h.shape[0]
        x = gat_conv(h, W1, attn_l1, attn_r1, src, dst, n)
        x = jax.nn.elu(x)
        out = gat_conv(x, W2, attn_l2, attn_r2, src, dst, n)
        return out

    def _L0_mix_ref(x, Wq, Wkv, Wproj, bproj):
        import jax, jax.numpy as jnp
        import numpy as np
        NUM_HEADS = 8
        B, N, C = x.shape
        h = NUM_HEADS
        d = C // h
        q = jnp.einsum('bnc,oc->bno', x, Wq).reshape(B, N, h, d).transpose(0, 2, 1, 3)
        kv = jnp.einsum('bnc,oc->bno', x, Wkv).reshape(B, N, 2, h, d)
        k = kv[:, :, 0].transpose(0, 2, 1, 3)
        v = kv[:, :, 1].transpose(0, 2, 1, 3)
        q = jax.nn.elu(q) + 1.0
        k = jax.nn.elu(k) + 1.0
        k_sum = k.sum(axis=2)
        D_inv = 1.0 / jnp.maximum(jnp.einsum('bhnd,bhd->bhn', q, k_sum), 1e-06)
        context = jnp.einsum('bhnd,bhne->bhde', k, v)
        attn = jnp.einsum('bhnd,bhde->bhne', q, context) * D_inv[..., None]
        out = attn.transpose(0, 2, 1, 3).reshape(B, N, C)
        out = jnp.einsum('bnc,oc->bno', out, Wproj) + bproj
        return out

    def _L0_ffn_ref(x, Wr, br, W1, b1, g1, be1, m1, v1, W2, b2, g2, be2, m2, v2, Wo, bo):
        import jax, jax.numpy as jnp
        import numpy as np
        BN_EPS = 0.001

        def _bn(h, g, b, m, v):
            return g * (h - m) * jax.lax.rsqrt(v + BN_EPS) + b
        feat = jnp.mean(x, axis=0)
        w = jax.nn.softmax(feat @ Wr + br, axis=-1)
        h = jnp.einsum('bfd,edh->bfeh', x, W1) + b1
        h = jax.nn.relu(_bn(h, g1, be1, m1, v1))
        h = jnp.einsum('bfeh,ehk->bfek', h, W2) + b2
        h = jax.nn.relu(_bn(h, g2, be2, m2, v2))
        y = jnp.einsum('bfeh,ehd->bfed', h, Wo) + bo
        return jnp.einsum('bfed,fe->bfd', y, w)
    xn = _layernorm(x, axis=-1)
    x = x + _L0_gnn_ref(xn, L0_gnn_W1, L0_gnn_attn_l1, L0_gnn_attn_r1, L0_gnn_W2, L0_gnn_attn_l2, L0_gnn_attn_r2, src, dst) + _L0_mix_ref(xn[None], L0_mix_Wq, L0_mix_Wkv, L0_mix_Wproj, L0_mix_bproj)[0]
    x = x + _L0_ffn_ref(_layernorm(x, axis=-1)[None], L0_ffn_Wr, L0_ffn_br, L0_ffn_W1, L0_ffn_b1, L0_ffn_g1, L0_ffn_be1, L0_ffn_m1, L0_ffn_v1, L0_ffn_W2, L0_ffn_b2, L0_ffn_g2, L0_ffn_be2, L0_ffn_m2, L0_ffn_v2, L0_ffn_Wo, L0_ffn_bo)[0]
    return x

_drawn_inputs = setup_inputs


def setup_inputs(seed=0):
    import zlib

    import numpy as np

    out = dict(_drawn_inputs(seed))
    spreads = {'L0_mix_bproj': (0.0, 0.1),
     'L0_ffn_br': (0.0, 0.1),
     'L0_ffn_b1': (0.0, 0.321),
     'L0_ffn_g1': (1.0, 0.2),
     'L0_ffn_be1': (0.0, 0.332),
     'L0_ffn_m1': (0.0, 0.325),
     'L0_ffn_v1': (1.0, 0.6),
     'L0_ffn_b2': (0.0, 0.1),
     'L0_ffn_g2': (1.0, 0.2),
     'L0_ffn_be2': (0.0, 0.1),
     'L0_ffn_m2': (0.0, 0.1),
     'L0_ffn_v2': (1.0, 0.559),
     'L0_ffn_bo': (0.0, 0.1)}
    factors = {'L0_gnn_attn_r1': 3.377,
     'L0_gnn_attn_l2': 3.061,
     'L0_gnn_attn_r2': 8.0,
     'L0_mix_Wq': 8.0,
     'L0_mix_Wkv': 8.0,
     'L0_mix_Wproj': 8.0}
    for name, (base, spread) in spreads.items():
        noise = np.random.default_rng([zlib.crc32(name.encode()), seed]).standard_normal(out[name].shape)
        drawn = base * np.exp(spread * noise) if base else spread * noise
        out[name] = jnp.asarray(drawn.astype(out[name].dtype))
    for name, factor in factors.items():
        out[name] = (out[name] * factor).astype(out[name].dtype)
    return out
```

```python
import concourse.bass as bass
from concourse import mybir
from contextlib import ExitStack

F32 = mybir.dt.float32
BF16 = mybir.dt.bfloat16
I32 = mybir.dt.int32
ALU = mybir.AluOpType
ACT = mybir.ActivationFunctionType
AX = mybir.AxisListType

P = 128
NODES = 6250
D = 256
NB = 49
NP = NB * P
EDGES = 106250
G = 17
T = NB * G
E = 8
HEADS = 8
MH = D // HEADS
BIG = 1.0e30
ROUND = 12582912.0
NONE = 4.0e6
HALVES = [(0, 9), (9, 17)]
LENGTH = [c1 - c0 for c0, c1 in HALVES]
GB = 7
GN = GB * P // 2

assert P * T >= EDGES and NP >= NODES and NB % GB == 0


class Layer:

    def __init__(self, name, heads, width, act_heads):
        self.name, self.heads, self.width = name, heads, width
        self.dim = width // heads
        self.table = width + 8
        self.row = width + 2 * heads
        self.den = width
        self.max = width + heads
        self.act_heads = act_heads


L1 = Layer("l1", 8, 512, 6)
L2 = Layer("l2", 1, 256, 1)


def wait(eng, sem, value):
    if not isinstance(value, int) or value > 0:
        eng.wait_ge(sem, value)


def sweep(eng, body, first=None):
    body(0, 0, 0)
    body(1, 1, 0)
    with eng.Fori(1, NB // 2, 1) as t:
        body(t * 2, 0, t)
        body(t * 2 + 1, 1, t)
    body(NB - 1, 0, NB // 2)


def wait_apart(eng, own, sem, value, passed):
    eng.wait_ge(sem, value)
    own.sem_inc(passed)


class Steps:

    def __init__(self, eng, sem, passed=None):
        self.eng, self.sem, self.base, self.n = eng, sem, 0, 0
        self.passed = passed

    def __call__(self, ins):
        ins.then_inc(self.sem, 1)
        self.n += 1
        return ins

    def done(self):
        self.eng.wait_ge(self.sem, self.base + self.n)

    def block(self, n, per):
        self.base, self.n, self.per = n * per, 0, per

    def end(self):
        assert self.n == self.per, (self.n, self.per)


def broad(ap, n):
    return ap.unsqueeze(len(ap.shape)).to_broadcast([*ap.shape, n])


class Scope:

    def __init__(self, nc, tag):
        self.nc, self.tag, self.stack, self.held = nc, tag, ExitStack(), []

    def __enter__(self):
        self.stack.__enter__()
        return self

    def __exit__(self, *a):
        out = self.stack.__exit__(*a)
        if self.held and a[0] is None:
            self.nc.clear_and_free_semaphores(self.held)
            self.nc.all_engine_barrier()
        return out

    def sb(self, name, shape, dt=F32):
        return self.stack.enter_context(self.nc.sbuf_tensor(f"{self.tag}_{name}", shape, dt))

    def ps(self, name, shape, dt=F32):
        return self.stack.enter_context(self.nc.psum_tensor(f"{self.tag}_{name}", shape, dt))

    def sem(self, name):
        self.held.append(self.nc.alloc_semaphore(f"{self.tag}_{name}"))
        return self.held[-1]

    def sems(self, name, n=2):
        return [self.sem(f"{name}{i}") for i in range(n)]

    def block(self):
        return self.stack.enter_context(self.nc.Block())


def node_pass(nc, a, k):
    with Scope(nc, "na") as s:
        w1 = s.sb("w1", [P, 2, 512])
        wkv = s.sb("wkv", [P, 2, 512])
        wq = s.sb("wq", [P, 2, D])
        alr = s.sb("alr", [P, 2, 512])
        prod = s.sb("prod", [P, 512])
        wlr = s.sb("wlr", [P, 2, 16])
        io_i = s.sb("io_i", [P, P], I32)
        iop_i = s.sb("iop_i", [P, 1], I32)
        zero = s.sb("zero", [P, 2 * (P + 1) + P])
        hi_i = s.sb("hi_i", [P, T], I32)
        lo_i = s.sb("lo_i", [P, T], I32)
        hi = s.sb("hi", [P, T])
        lo = s.sb("lo", [P, T])
        oneh = s.sb("oneh", [P, 2, G, NB], BF16)
        onel = s.sb("onel", [P, 2, G, P], BF16)
        x = k.x
        blank = s.sb("blank", [P, T // GB * 8])
        stats = s.sb("stats", [P, NB, 6])
        mv = s.sb("mv", [P, NB, 2])
        sd = s.sb("sd", [P, NB])
        rstd = s.sb("rstd", [P, NB])
        xn = s.sb("xn", [P, 2, D])
        xt = s.sb("xt", [P, 2, 2, P])
        frow = s.sb("frow", [P, 2, L1.table])
        kmin = s.sb("kmin", [P, 2, D])
        kexp = s.sb("kexp", [P, 2, D])
        kphi = s.sb("kphi", [P, 2, D])
        vext = s.sb("vext", [P, 2, 2, P + 1])
        qmin = s.sb("qmin", [P, 2, D])
        qexp = s.sb("qexp", [P, 2, D])
        p_t = [s.ps(f"p_t{i}", [P, 512]) for i in range(2)]
        p_f = [s.ps(f"p_f{i}", [P, 512]) for i in range(2)]
        p_kv = [s.ps(f"p_kv{i}", [P, 512]) for i in range(2)]
        p_q = s.ps("p_q", [P, 512])
        p_acc = s.ps("p_acc", [P, 512])
        CW = 2 * (P + 1)
        p_c, p_h = p_acc[:, 0:CW], p_acc[0:NB, CW:CW + P]
        loaded, edges_in = s.sem("loaded"), s.sem("edges_in")
        iota_made, step = s.sem("iota_made"), s.sem("step")
        const_ready, wlr_ready = s.sem("const_ready"), s.sem("wlr_ready")
        x_in = s.sems("x_in", GB)
        passed, mv_ready, rstd_ready = s.sem("passed"), s.sem("mv_ready"), s.sem("rstd_ready")
        xn_ready, t_ready, xt_ready = s.sem("xn_ready"), s.sem("t_ready"), s.sem("xt_ready")
        proj_ready, q_ready = s.sem("proj_ready"), s.sem("q_ready")
        row_copied, row_out = s.sem("row_copied"), s.sems("row_out")
        kmin_ready, kexp_ready, kv_ready = s.sem("kmin_ready"), s.sem("kexp_ready"), s.sem("kv_ready")
        qmin_ready, qexp_ready, q_kept = s.sem("qmin_ready"), s.sem("qexp_ready"), s.sem("q_kept")
        ctx_added, onehot_ready, counted = s.sem("ctx_added"), s.sem("onehot_ready"), s.sem("counted")
        lr_copied, acc_ready, er_out = s.sem("lr_copied"), s.sem("acc_ready"), s.sem("er_out")
        blanked, blank_out = s.sem("blanked"), s.sem("blank_out")
        block = s.block()

        @block.sync
        def _(sp):
            for i in range(GB):
                n = i * GB
                sp.dma_start(x[:, n:n + GB, :], a["x"][n * P:(n + GB) * P, :].rearrange("(n p) d -> p n d", p=P)
                             ).then_inc(x_in[i], 16)
            sp.dma_start(k.dst[:, :], a["dst"]).then_inc(edges_in, 16)
            sp.dma_start(k.src[:, :], a["src"]).then_inc(edges_in, 16)
            sp.dma_start(w1[:, :, :], a["w1"].rearrange("(k p) n -> p k n", p=P)).then_inc(loaded, 16)
            sp.dma_start(wkv[:, :, :], a["wkv"].rearrange("(k p) n -> p k n", p=P)).then_inc(loaded, 16)
            sp.dma_start(wq[:, :, :], a["wq"].rearrange("(k p) n -> p k n", p=P)).then_inc(loaded, 16)
            sp.dma_start(alr[:, 0, :], a["al1"].to_broadcast([P, 512])).then_inc(loaded, 16)
            sp.dma_start(alr[:, 1, :], a["ar1"].to_broadcast([P, 512])).then_inc(loaded, 16)
            sp.wait_ge(blanked, 1)
            starts = a["starts"].rearrange("(p c t) h -> p c (t h)", p=P, c=GB)
            for i in range(GB):
                sp.dma_start(starts[:, i, :], blank[:, :]).then_inc(blank_out, 16)
            sp.wait_ge(blank_out, 16 * GB)


        @block.gpsimd
        def _(pool):
            nc.gpsimd.iota(io_i[:, :], [[1, P]], base=0, channel_multiplier=0).then_inc(iota_made, 1)
            nc.gpsimd.iota(iop_i[:, :], [[0, 1]], base=0, channel_multiplier=1).then_inc(iota_made, 1)
            nc.gpsimd.memset(blank[:, :], 0.0).then_inc(blanked, 1)

        @block.vector
        def _(dve):
            c = Steps(dve, step, passed)
            dve.wait_ge(iota_made, 2)
            c(nc.vector.tensor_copy(k.iota[:, :], io_i[:, :]))
            c(nc.vector.tensor_copy(k.iop[:, :], iop_i[:, :]))
            c(nc.vector.memset(zero[:, :], 0.0))
            c(nc.vector.memset(vext[:, :, :, P:P + 1], 1.0))
            c.done()
            nc.vector.tensor_scalar(k.ident[:, :], k.iota[:, :], k.iop[:, 0:1], None, ALU.is_equal).then_inc(const_ready, 1)
            dve.wait_ge(edges_in, 32)
            c(nc.vector.tensor_scalar(hi_i[:, :], k.dst[:, :], 7, None, ALU.logical_shift_right))
            c(nc.vector.tensor_scalar(lo_i[:, :], k.dst[:, :], 127, None, ALU.bitwise_and))
            c.done()
            c(nc.vector.tensor_copy(hi[:, :], hi_i[:, :]))
            c(nc.vector.tensor_copy(lo[:, :], lo_i[:, :]))
            dve.wait_ge(loaded, 5 * 16)
            for kt in range(2):
                for lr in range(2):
                    c(nc.vector.tensor_tensor(prod[:, :], w1[:, kt, :], alr[:, lr, :], ALU.mult))
                    c.done()
                    c(nc.vector.tensor_reduce(wlr[:, kt, 8 * lr:8 * lr + 8],
                                              prod[:, :].rearrange("p (h d) -> p h d", h=8), AX.X, ALU.add))
                    c.done()
            nc.vector.memset(prod[:, 0:1], 0.0).then_inc(wlr_ready, 1)
            for n in range(NB):
                if n % GB == 0:
                    dve.wait_ge(x_in[n // GB], 16)
                c(nc.vector.bn_stats(stats[:, n, :], x[:, n, :]))
            c.done()
            nc.vector.sem_inc(passed)
            for n in range(NB):
                c(nc.vector.bn_aggr(mv[:, n, :], stats[:, n, :]))
            c.done()
            nc.vector.tensor_scalar(rstd[:, :], mv[:, :, 1], 1e-5, None, ALU.add).then_inc(mv_ready, 1)
            dve.wait_ge(rstd_ready, 1)
            c(nc.vector.reciprocal(rstd[:, :], sd[:, :]))
            c.done()
            start = c.n

            def norm(n, b):
                wait(dve, t_ready, n - 1)
                nc.vector.tensor_scalar(xn[:, b, :], x[:, bass.ds(n, 1), :].rearrange("p a d -> p (a d)"),
                                        mv[:, bass.ds(n, 1), 0:1].rearrange("p a d -> p (a d)"),
                                        rstd[:, bass.ds(n, 1)], ALU.subtract, ALU.mult).then_inc(xn_ready, 1)

            norm(0, 0)

            def vec(n, b, use):
                if not (isinstance(n, int) and n == NB - 1):
                    norm(n + 1, 1 - b)
                wait(dve, counted, n - 1)
                nc.vector.tensor_tensor(oneh[:, b, :, :], broad(hi[:, bass.ds(n * G, G)], NB),
                                        k.iota[:, 0:NB].unsqueeze(1).to_broadcast([P, G, NB]), ALU.is_equal)
                nc.vector.tensor_tensor(onel[:, b, :, :], broad(lo[:, bass.ds(n * G, G)], P),
                                        k.iota[:, :].unsqueeze(1).to_broadcast([P, G, P]),
                                        ALU.is_equal).then_inc(onehot_ready, 1)
                dve.wait_ge(proj_ready, n + 1)
                wait(dve, ctx_added, n - 1)
                if isinstance(n, int) and n == NB - 1:
                    nc.vector.tensor_scalar(vext[:, b, :, P:P + 1], k.iop[:, :].unsqueeze(1).to_broadcast([P, 2, 1]),
                                            float(NODES - n * P), None, ALU.is_lt)
                nc.vector.tensor_scalar(kmin[:, b, :], p_kv[b][:, 0:D], 0.0, None, ALU.min).then_inc(kmin_ready, 1)
                dve.wait_ge(q_ready, n + 1)
                nc.vector.tensor_scalar(qmin[:, b, :], p_q[:, 0:D], 0.0, None, ALU.min).then_inc(qmin_ready, 1)
                nc.vector.tensor_copy(vext[:, b, :, 0:P], p_kv[b][:, D:2 * D].rearrange("p (m v) -> p m v", m=2))
                wait(dve, row_out[b], use * 16)
                nc.vector.tensor_copy(frow[:, b, 512:520], p_q[:, D:D + 8])
                nc.vector.tensor_copy(k.er[:, bass.ds(n, 1), :].rearrange("p a h -> p (a h)"),
                                      p_q[:, D + 8:D + 16]).then_inc(lr_copied, 1)
                dve.wait_ge(kexp_ready, n + 1)
                nc.vector.scalar_tensor_tensor(kphi[:, b, :], p_kv[b][:, 0:D], 0.0, kexp[:, b, :],
                                               ALU.max, ALU.add).then_inc(kv_ready, 1)
                dve.wait_ge(qexp_ready, n + 1)
                nc.vector.scalar_tensor_tensor(
                    k.qt[:, :, bass.ds(n * P, P)], p_q[:, 0:D].rearrange("p (m v) -> p m v", m=2), 0.0,
                    qexp[:, b, :].rearrange("p (m v) -> p m v", m=2), ALU.max, ALU.add).then_inc(q_kept, 1)

            sweep(dve, vec)
            dve.wait_ge(acc_ready, 1)
            c.base, c.n = start, 0
            c(nc.vector.memset(k.cbd[:, :, :], 0.0))
            c(nc.vector.memset(k.kbd[:, :, :], 0.0))
            c.done()
            for m in range(2):
                at = m * (P + 1)
                for h in range(P // MH):
                    r = slice(h * MH, (h + 1) * MH)
                    nc.vector.tensor_copy(k.cbd[r, m, r], p_c[r, at + h * MH:at + (h + 1) * MH])
                    c(nc.vector.tensor_copy(k.kbd[r, m, r], p_c[r, at + P:at + P + 1].to_broadcast([MH, MH])))
            c(nc.vector.tensor_copy(k.hist[:, :], p_h))
            c.done()

        @block.scalar
        def _(act):
            act.wait_ge(mv_ready, 1)
            nc.scalar.activation(sd[:, :], rstd[:, :], ACT.Sqrt).then_inc(rstd_ready, 1)

            def sca(n, b, use):
                act.wait_ge(t_ready, n + 1)
                wait(act, proj_ready, n - 1)
                nc.scalar.copy(xt[:, b, :, :], p_t[b][:, 0:D].rearrange("p (m v) -> p m v", m=2)).then_inc(xt_ready, 1)
                act.wait_ge(kmin_ready, n + 1)
                nc.scalar.activation(kexp[:, b, :], kmin[:, b, :], ACT.Exp).then_inc(kexp_ready, 1)
                act.wait_ge(qmin_ready, n + 1)
                nc.scalar.activation(qexp[:, b, :], qmin[:, b, :], ACT.Exp).then_inc(qexp_ready, 1)
                wait(act, row_out[b], use * 16)
                nc.scalar.copy(frow[:, b, 0:512], p_f[b][:, :]).then_inc(row_copied, 1)
                act.wait_ge(row_copied, n + 1)
                act.wait_ge(lr_copied, n + 1)
                act.dma_start(a["table1"][bass.ds(n * P, P), :], frow[:, b, :]).then_inc(row_out[b], 16)

            sweep(act, sca)
            act.dma_start(a["er1"].rearrange("(n p) h -> p n h", p=P), k.er[:, :, :]).then_inc(er_out, 16)
            act.wait_ge(er_out, 16)
            act.wait_ge(row_out[0], 16 * (NB // 2 + 1))
            act.wait_ge(row_out[1], 16 * (NB // 2))

        @block.tensor
        def _(pe):
            def transposes(n, b):
                pe.wait_ge(xn_ready, n + 1)
                wait(pe, xt_ready, n - 1)
                for m in range(2):
                    last = nc.tensor.transpose(p_t[b][:, m * P:(m + 1) * P], xn[:, b, m * P:(m + 1) * P], k.ident[:, :])
                last.then_inc(t_ready, 1)

            def products(n, b):
                pe.wait_ge(xt_ready, n + 1)
                wait(pe, row_copied, n - 1)
                for kt in range(2):
                    nc.tensor.matmul(p_f[b][:, :], xt[:, b, kt, :], w1[:, kt, :], start=kt == 0, stop=kt == 1)
                wait(pe, kv_ready, n - 1)
                for kt in range(2):
                    last = nc.tensor.matmul(p_kv[b][:, :], xt[:, b, kt, :], wkv[:, kt, :], start=kt == 0, stop=kt == 1)
                last.then_inc(proj_ready, 1)
                wait(pe, q_kept, n)
                wait(pe, lr_copied, n)
                for m in range(2):
                    for kt in range(2):
                        nc.tensor.matmul(p_q[:, m * P:(m + 1) * P], wq[:, kt, m * P:(m + 1) * P], xt[:, b, kt, :],
                                         start=kt == 0, stop=kt == 1)
                for kt in range(2):
                    last = nc.tensor.matmul(p_q[:, D:D + 16], xt[:, b, kt, :], wlr[:, kt, :], start=kt == 0, stop=kt == 1)
                last.then_inc(q_ready, 1)

            def context(n, b):
                pe.wait_ge(kv_ready, n + 1)
                pe.wait_ge(lr_copied, n + 1)
                for m in range(2):
                    last = nc.tensor.matmul(p_c[:, m * (P + 1):(m + 1) * (P + 1)], kphi[:, b, m * P:(m + 1) * P],
                                            vext[:, b, m, :], start=False, stop=False, skip_group_check=True)
                last.then_inc(ctx_added, 1)

            def count(n, b):
                pe.wait_ge(onehot_ready, n + 1)
                for g in range(G):
                    last = nc.tensor.matmul(p_h, oneh[:, b, g, :], onel[:, b, g, :],
                                            start=False, stop=False, skip_group_check=True)
                last.then_inc(counted, 1)

            pe.wait_ge(const_ready, 1)
            pe.wait_ge(wlr_ready, 1)
            pe.wait_ge(loaded, 5 * 16)
            nc.tensor.matmul(p_acc[:, 0:CW + P], zero[:, 0:P], zero[:, :], start=True, stop=False, skip_group_check=True)
            transposes(0, 0)

            def mat(n, b, use):
                if not (isinstance(n, int) and n == NB - 1):
                    transposes(n + 1, 1 - b)
                products(n, b)
                count(n, b)
                if not (isinstance(n, int) and n == 0):
                    context(n - 1, 1 - b)

            sweep(pe, mat)
            context(NB - 1, 0)
            nc.tensor.matmul(p_acc[:, 0:CW + P], zero[:, 0:P], zero[:, :], start=False, stop=True,
                             skip_group_check=True).then_inc(acc_ready, 1)


def scatter_starts(nc, a, k, pool, done):
    for n in range(NB):
        nc.gpsimd.indirect_dma_start(
            out=a["starts"], out_offset=bass.IndirectOffsetOnAxis(ap=k.first[:, n:n + 1], axis=0),
            in_=k.er[:, n, :], in_offset=None, bounds_check=P * T - 1, oob_is_err=False).then_inc(done, 16)
    pool.wait_ge(done, 16 * NB)


def attention_pass(nc, a, k):
    with Scope(nc, "at") as s:
        wproj = s.sb("wproj", [P, 2, D])
        bproj = s.sb("bproj", [P, D])
        nxt = s.sb("nxt", [P, 1], I32)
        own = s.sb("own", [P, 1])
        own_row = s.sb("own_row", [P, P])
        ones = s.sb("ones", [P, P])
        below = s.sb("below", [NB, NB])
        cum = s.sb("cum", [NB, P])
        lead = s.sb("lead", [NB, 1])
        place = s.sb("place", [NB, 3, P])
        pl = s.sb("pl", [P, 3, NB])
        strip = s.sb("strip", [P, 2, NB])
        cross = s.sb("cross", [P, NB])
        xb = s.sb("xb", [P, 2, D])
        dmax = s.sb("dmax", [P, 2, D])
        drec = s.sb("drec", [P, 2, D])
        att = s.sb("att", [P, 2, 2, P])
        res = s.sb("res", [P, 2, D])
        p_ad = [s.ps(f"p_ad{i}", [P, 512]) for i in range(2)]
        p_o = [s.ps(f"p_o{i}", [P, 512]) for i in range(2)]
        p_s = s.ps("p_s", [P, 512])
        p_r = s.ps("p_r", [P, 512])
        loaded, step, nxt_in, nxt_set = s.sem("loaded"), s.sem("step"), s.sem("nxt_in"), s.sem("nxt_set")
        sum_asked, summed = s.sem("sum_asked"), s.sem("summed")
        turn_asked, turned = s.sem("turn_asked"), s.sem("turned")
        index_ready, scattered = s.sem("index_ready"), s.sem("scattered")
        ad_ready, att_ready, o_ready = s.sem("ad_ready"), s.sem("att_ready"), s.sem("o_ready")
        xb_ready, res_ready, res_out, passed = s.sem("xb_ready"), s.sem("res_ready"), s.sems("res_out"), s.sem("passed")
        block = s.block()

        @block.sync
        def _(sp):
            sp.wait_ge(nxt_set, 1)
            sp.dma_start(nxt[0:P - 1, :], a["dst"][1:P, 0:1],
                         allow_slow_non_contiguous=True).then_inc(nxt_in, 16)
            sp.dma_start(wproj[:, :, :], a["wproj"].rearrange("(k p) n -> p k n", p=P)).then_inc(loaded, 16)
            sp.dma_start(bproj[:, :], a["bproj"].to_broadcast([P, D])).then_inc(loaded, 16)

            def store(n, b, use):
                wait_apart(sp, nc.sync, res_ready, n + 1, passed)
                sp.dma_start(a["res"][bass.ds(n * P, P), :], res[:, b, :]).then_inc(res_out[b], 16)

            sweep(sp, store)
            sp.wait_ge(res_out[0], 16 * (NB // 2 + 1))
            sp.wait_ge(res_out[1], 16 * (NB // 2))

        @block.gpsimd
        def _(pool):
            pool.wait_ge(index_ready, 1)
            scatter_starts(nc, a, k, pool, scattered)

        @block.vector
        def _(dve):
            c = Steps(dve, step)
            nc.vector.memset(nxt[:, :], -1).then_inc(nxt_set, 1)
            c(nc.vector.memset(ones[:, :], 1.0))
            c(nc.vector.tensor_scalar(below[:, :], k.iota[0:NB, 0:NB], k.iop[0:NB, 0:1], None, ALU.is_gt))
            c.done()
            c(nc.vector.tensor_tensor_scan(cum[:, :], ones[0:NB, :], k.hist[:, :], 0.0, ALU.mult, ALU.add))
            c.done()
            c(nc.vector.tensor_copy(own[:, :], k.dst[:, T - 1:T]))
            c(nc.vector.memset(k.same[:, 0:1], 0.0))
            c(nc.vector.tensor_tensor(k.same[:, 1:T], k.dst[:, 1:T], k.dst[:, 0:T - 1], ALU.is_equal))
            c.done()
            c(nc.vector.tensor_scalar(k.restart[:, :], k.same[:, :], -1.0, BIG, ALU.add, ALU.mult))
            nc.vector.tensor_scalar(own_row[:, :], k.ident[:, :], own[:, 0:1], None, ALU.mult).then_inc(sum_asked, 1)
            dve.wait_ge(nxt_in, 16)
            c(nc.vector.tensor_tensor(k.open[:, :], k.dst[:, T - 1:T], nxt[:, :], ALU.is_equal))
            dve.wait_ge(summed, 1)
            c(nc.vector.tensor_scalar(k.group[:, :], p_s[:, 0:P], own[:, 0:1], None, ALU.is_equal))
            c(nc.vector.tensor_copy(lead[:, :], p_s[0:NB, P:P + 1]))
            c.done()
            c(nc.vector.tensor_scalar(cum[:, :], cum[:, :], lead[:, 0:1], None, ALU.add))
            c(nc.vector.tensor_copy(place[:, 0, :], k.hist[:, :]))
            c.done()
            c(nc.vector.tensor_tensor(place[:, 1, :], cum[:, :], k.hist[:, :], ALU.subtract))
            nc.vector.tensor_scalar(place[:, 2, :], cum[:, :], -1.0, None, ALU.add).then_inc(turn_asked, 1)
            dve.wait_ge(turned, 1)
            c(nc.vector.tensor_copy(pl[:, :, :], p_r[:, 0:3 * NB].rearrange("p (a n) -> p a n", a=3)))
            c.done()
            c(nc.vector.tensor_scalar(k.has[:, :], pl[:, 0, :], 1.0, None, ALU.min))
            c.done()
            c(nc.vector.tensor_scalar(cross[:, :], k.has[:, :], -NONE, NONE, ALU.mult, ALU.add))
            c(nc.vector.tensor_tensor(pl[:, 2, :], pl[:, 2, :], k.has[:, :], ALU.mult))
            c.done()
            c(nc.vector.tensor_tensor(k.first[:, :], pl[:, 1, :], cross[:, :], ALU.add))
            c(nc.vector.tensor_copy(k.last[:, :], pl[:, 2, :]))
            c(nc.vector.tensor_scalar(strip[:, :, :], pl[:, 1:3, :], 0.5, 1.0 / T, ALU.add, ALU.mult))
            c.done()
            c(nc.vector.tensor_scalar(strip[:, :, :], strip[:, :, :], -0.5, ROUND, ALU.add, ALU.add))
            c.done()
            c(nc.vector.tensor_scalar(strip[:, :, :], strip[:, :, :], -ROUND, None, ALU.add))
            c.done()
            c(nc.vector.tensor_tensor(cross[:, :], strip[:, 0, :], strip[:, 1, :], ALU.is_lt))
            c.done()
            c(nc.vector.tensor_tensor(cross[:, :], cross[:, :], k.has[:, :], ALU.mult))
            c(nc.vector.tensor_scalar(strip[:, 0, :], strip[:, 0, :], -float(P), None, ALU.add))
            c.done()
            c(nc.vector.tensor_tensor(strip[:, 0, :], strip[:, 0, :], cross[:, :], ALU.mult))
            c.done()
            nc.vector.tensor_scalar(k.tail[:, :], strip[:, 0, :], float(P), None, ALU.add).then_inc(index_ready, 1)
            start = c.n
            dve.wait_ge(loaded, 32)

            def vec(n, b, use):
                c.base, c.n = n * 3 + start, 0
                dve.wait_ge(ad_ready, n + 1)
                c(nc.vector.tensor_scalar(dmax[:, b, :], p_ad[b][:, D:2 * D], 1e-6, None, ALU.max))
                c(nc.vector.tensor_tensor(xb[:, b, :], k.x[:, bass.ds(n, 1), :].rearrange("p a d -> p (a d)"),
                                          bproj[:, :], ALU.add))
                c.done()
                c(nc.vector.reciprocal(drec[:, b, :], dmax[:, b, :]))
                c.done()
                wait(dve, o_ready, n - 1)
                nc.vector.tensor_tensor(att[:, b, :, :].rearrange("p m v -> p (m v)"), p_ad[b][:, 0:D], drec[:, b, :],
                                        ALU.mult).then_inc(att_ready, 1)
                dve.wait_ge(o_ready, n + 1)
                wait(dve, res_out[b], use * 16)
                nc.vector.tensor_tensor(res[:, b, :], p_o[b][:, 0:D], xb[:, b, :], ALU.add).then_inc(res_ready, 1)

            sweep(dve, vec)

        @block.tensor
        def _(pe):
            pe.wait_ge(sum_asked, 1)
            nc.tensor.matmul(p_s[:, 0:P], ones[:, :], own_row[:, :], start=True, stop=True)
            nc.tensor.matmul(p_s[0:NB, P:P + 1], below[:, :], cum[:, P - 1:P], start=True, stop=True).then_inc(summed, 1)
            pe.wait_ge(turn_asked, 1)
            for i in range(3):
                last = nc.tensor.transpose(p_r[:, i * NB:(i + 1) * NB], place[:, i, :], k.ident[0:NB, 0:NB])
            last.then_inc(turned, 1)
            pe.wait_ge(loaded, 32)

            def sums(n, b):
                wait(pe, att_ready, n - 1)
                for m in range(2):
                    q = k.qt[:, m:m + 1, bass.ds(n * P, P)].rearrange("p a v -> p (a v)")
                    nc.tensor.matmul(p_ad[b][:, m * P:(m + 1) * P], k.cbd[:, m, :], q, start=True, stop=True)
                    last = nc.tensor.matmul(p_ad[b][:, D + m * P:D + (m + 1) * P], k.kbd[:, m, :], q, start=True, stop=True)
                last.then_inc(ad_ready, 1)

            sums(0, 0)

            def mat(n, b, use):
                if not (isinstance(n, int) and n == NB - 1):
                    sums(n + 1, 1 - b)
                pe.wait_ge(att_ready, n + 1)
                wait(pe, res_ready, n - 1)
                for m in range(2):
                    last = nc.tensor.matmul(p_o[b][:, 0:D], att[:, b, m, :], wproj[:, m, :], start=m == 0, stop=m == 1)
                last.then_inc(o_ready, 1)

            sweep(pe, mat)


def edge_pass(nc, a, k, L):
    H, W, R, dim, AH = L.heads, L.width, L.row, L.dim, L.act_heads
    U = min(2, H)
    i_ = L.name[1]
    table, er_table, sums, tails = a["table" + i_], a["er" + i_], a["sums" + i_], a["tails" + i_]
    G1 = G + 1
    with Scope(nc, "e" + i_) as s:
        er = s.sb("er", [P, T, 8])
        er0 = s.sb("er0", [P, 8])
        idx = s.sb("idx", [P, 2, G], I32)
        rows = s.sb("rows", [P, 2, G, L.table])
        ring = s.sb("ring", [P, 2, 9, R])
        z = s.sb("z", [P, H, G])
        eext = s.sb("eext", [P, H, G1])
        rext = s.sb("rext", [P, H, G1])
        mext = s.sb("mext", [P, 2, H, G1])
        d = s.sb("d", [P, 2, H, G])
        wr = s.sb("wr", [P, 2, 2, H, G1])
        dext = s.sb("dext", [P, 2, H, G1])
        om = s.sb("om", [P, 1])
        pen = s.sb("pen", [P, P])
        mm = s.sb("mm", [P, H])
        diag = s.sb("diag", [P, H, P])
        cand = s.sb("cand", [P, H, P])
        gm = s.sb("gm", [P, H])
        ts = s.sb("ts", [P, R])
        sc = s.sb("sc", [P, 2, H])
        tl = s.sb("tl", [P, R])
        none = s.sb("none", [1, R])
        ones = s.sb("ones", [P, P])
        p_m = [s.ps(f"p_m{i}", [P, 512]) for i in range(2)]
        p_t = s.ps("p_t", [P, 512])
        p_d = s.ps("p_d", [P, 512])
        er_in, er0_in, step, er_ready = s.sem("er_in"), s.sem("er0_in"), s.sem("step"), s.sem("er_ready")
        idx_ready, rows_in = s.sem("idx_ready"), s.sems("rows_in")
        passed, passed_sp, d_ready, wr_ready = s.sem("passed"), s.sem("passed_sp"), s.sem("d_ready"), s.sem("wr_ready")
        scaled, summed = s.sem("scaled"), s.sem("summed")
        dm_ready, den_ready = s.sems("dm_ready"), s.sem("den_ready")
        stored = s.sems("stored")
        max_asked, max_spread = s.sem("max_asked"), s.sem("max_spread")
        exp_asked, exp_done = s.sem("exp_asked"), s.sem("exp_done")
        tail_asked, tail_summed = s.sem("tail_asked"), s.sem("tail_summed")
        tail_ready, tail_out = s.sem("tail_ready"), s.sem("tail_out")
        block = s.block()

        @block.sync
        def _(sp):
            sp.dma_start(er[:, :, :], a["starts"].rearrange("(p t) h -> p t h", p=P)).then_inc(er_in, 16)
            out = sums.rearrange("(p t) r -> p t r", p=P)

            def store(n, b, use):
                for i, (c0, c1) in enumerate(HALVES):
                    wait_apart(sp, nc.sync, summed, (n * G + c1) * U, passed_sp)
                    wait_apart(sp, nc.sync, dm_ready[i], n + 1, passed_sp)
                    sp.dma_start(out[:, bass.ds(n * G + c0, c1 - c0), :], ring[:, i, 0:c1 - c0, :]).then_inc(stored[i], 16)

            sweep(sp, store)
            sp.wait_ge(tail_ready, 1)
            sp.dma_start(tails[0:P, :], tl[:, :]).then_inc(tail_out, 16)
            sp.dma_start(tails[P:P + 1, :], none[:, :]).then_inc(tail_out, 16)
            sp.wait_ge(tail_out, 32)
            sp.wait_ge(stored[0], 16 * NB)
            sp.wait_ge(stored[1], 16 * NB)

        @block.gpsimd
        def _(pool):
            nc.gpsimd.indirect_dma_start(out=er0[:, :], out_offset=None, in_=er_table,
                                         in_offset=bass.IndirectOffsetOnAxis(ap=k.dst[:, 0:1], axis=0)).then_inc(er0_in, 16)

            def gather(n, b, use):
                wait(pool, summed, (n - 1) * (G * U))
                nc.gpsimd.sem_inc(passed)
                nc.gpsimd.tensor_copy(idx[:, b, :], k.src[:, bass.ds(n * G, G)]).then_inc(idx_ready, 1)
                pool.wait_ge(idx_ready, n + 1)
                nc.gpsimd.sem_inc(passed)
                for g in range(G):
                    nc.gpsimd.indirect_dma_start(out=rows[:, b, g, :], out_offset=None, in_=table,
                                                 in_offset=bass.IndirectOffsetOnAxis(ap=idx[:, b, g:g + 1], axis=0)
                                                 ).then_inc(rows_in[b], 16)

            sweep(pool, gather)

        @block.vector
        def _(dve):
            c = Steps(dve, step)
            c(nc.vector.memset(ring[:, :, :, :], 0.0))
            c(nc.vector.memset(mext[:, 1, :, G:G1], -BIG))
            c(nc.vector.memset(dext[:, 1, :, G:G1], 0.0))
            c(nc.vector.memset(rext[:, :, :], -BIG))
            c(nc.vector.memset(wr[:, :, :, :, 0:1], 0.0))
            c(nc.vector.memset(ones[:, :], 1.0))
            c(nc.vector.memset(none[:, :], 0.0))
            c.done()
            c(nc.vector.memset(none[:, L.max:R], -BIG))
            dve.wait_ge(er_in, 16)
            dve.wait_ge(er0_in, 16)
            c(nc.vector.tensor_copy(er[:, 0, 0:H], er0[:, 0:H]))
            c.done()
            for h in range(H):
                c(nc.vector.tensor_tensor_scan(er[:, :, h], k.same[:, :], er[:, :, h], 0.0, ALU.mult, ALU.add))
            c.done()
            nc.vector.memset(om[:, :], 0.0).then_inc(er_ready, 1)
            start = c.n

            per = 8 if AH < H else 7

            def batch(n, b, use):
                c.base, c.n, c.per = n * per + start, 0, per
                dve.wait_ge(rows_in[b], use * (16 * G) + 16 * G)
                c(nc.vector.tensor_tensor(z[:, :, :], rows[:, b, :, W:W + H].rearrange("p j h -> p h j"),
                                          er[:, bass.ds(n * G, G), 0:H].rearrange("p j h -> p h j"), ALU.add))
                c(nc.vector.tensor_copy(eext[:, :, 0:1], mext[:, 1 - b, :, G:G1]))
                c(nc.vector.tensor_copy(rext[:, :, 1:G1],
                                        k.restart[:, bass.ds(n * G, G)].unsqueeze(1).to_broadcast([P, H, G])))
                c.done()
                c(nc.vector.scalar_tensor_tensor(eext[:, :, 1:G1], z[:, :, :], 0.2, z[:, :, :], ALU.mult, ALU.max))
                c.done()
                wait(dve, dm_ready[1], n - 1)
                c(nc.vector.tensor_tensor_scan(mext[:, b, :, :].rearrange("p h j -> p (h j)"),
                                               rext[:, :, :].rearrange("p h j -> p (h j)"),
                                               eext[:, :, :].rearrange("p h j -> p (h j)"), 0.0, ALU.add, ALU.max))
                c.done()
                wait(dve, wr_ready, n)
                c(nc.vector.tensor_tensor(d[:, 1, :, :], mext[:, b, :, 0:G], rext[:, :, 1:G1], ALU.add))
                nc.vector.tensor_tensor(d[:, 0, :, :], eext[:, :, 1:G1], mext[:, b, :, 1:G1], ALU.subtract)
                c.done()
                nc.vector.tensor_tensor(d[:, 1, :, :], d[:, 1, :, :], mext[:, b, :, 1:G1], ALU.subtract).then_inc(d_ready, 1)
                wait(dve, den_ready, n)
                c(nc.vector.tensor_copy(wr[:, b, 0, :, 0:1], dext[:, 1 - b, :, G:G1]))
                c.done()
                dve.wait_ge(wr_ready, n + 1)
                nc.vector.tensor_tensor_scan(dext[:, b, :, :].rearrange("p h j -> p (h j)"),
                                             wr[:, b, 1, :, :].rearrange("p h j -> p (h j)"),
                                             wr[:, b, 0, :, :].rearrange("p h j -> p (h j)"), 0.0,
                                             ALU.mult, ALU.add).then_inc(den_ready, 1)
                if AH < H:
                    v = rows[:, b, :, AH * dim:W].rearrange("p j (h e) -> p j h e", h=H - AH)
                    c(nc.vector.tensor_tensor(v, v, broad(wr[:, b, 0, AH:H, 1:G1].rearrange("p h j -> p j h"), dim), ALU.mult))
                    c.done()
                for i, (c0, c1) in enumerate(HALVES):
                    wait(dve, stored[i], n * 16)
                    for j in range(c0, c1):
                        prev = ring[:, i, j - c0 - 1, :] if j > c0 else ring[:, 1 - i, LENGTH[1 - i] - 1, :]
                        dve.wait_ge(scaled, n * G + (j + 1))
                        for h in range(H):
                            if h % (H // U) == 0:
                                wait(dve, summed, n * (G * U) + ((j - 1) * U + h * U // H + 1))
                            at = slice(h * dim, (h + 1) * dim)
                            ins = nc.vector.scalar_tensor_tensor(ring[:, i, j - c0, at], prev[:, at],
                                                                 wr[:, b, 1, h, j + 1:j + 2], rows[:, b, j, at],
                                                                 ALU.mult, ALU.add)
                            if (h + 1) % (H // U) == 0:
                                ins.then_inc(summed, 1)
                c.end()

            sweep(dve, batch)
            c.base, c.n = NB * per + start, 0
            final = ring[:, 1, LENGTH[1] - 1, :]
            dve.wait_ge(dm_ready[1], NB)
            dve.wait_ge(summed, T * U)
            c(nc.vector.tensor_scalar(om[:, :], k.open[:, :], -1.0, BIG, ALU.add, ALU.mult))
            c(nc.vector.tensor_scalar(pen[:, :], k.group[:, :], -1.0, BIG, ALU.add, ALU.mult))
            c.done()
            c(nc.vector.tensor_scalar(mm[:, :], final[:, L.max:R], om[:, 0:1], None, ALU.add))
            c.done()
            for h in range(H):
                last = nc.vector.tensor_scalar(diag[:, h, :], k.ident[:, :], mm[:, h:h + 1], None, ALU.mult)
            last.then_inc(max_asked, 1)
            dve.wait_ge(max_spread, 1)
            for h in range(H):
                c(nc.vector.tensor_tensor(cand[:, h, :], p_m[h // 4][:, h % 4 * P:(h % 4 + 1) * P], pen[:, :], ALU.add))
            c.done()
            c(nc.vector.tensor_reduce(gm[:, :], cand[:, :, :], AX.X, ALU.max))
            c.done()
            nc.vector.tensor_tensor(sc[:, 0, :], mm[:, :], gm[:, :], ALU.subtract).then_inc(exp_asked, 1)
            dve.wait_ge(exp_done, 1)
            c(nc.vector.tensor_scalar(sc[:, 1, :], sc[:, 1, :], k.open[:, 0:1], None, ALU.mult))
            c.done()
            nc.vector.tensor_tensor(ts[:, 0:W].rearrange("p (h e) -> p h e", h=H),
                                    final[:, 0:W].rearrange("p (h e) -> p h e", h=H), broad(sc[:, 1, :], dim), ALU.mult)
            nc.vector.tensor_tensor(ts[:, W:W + H], final[:, W:W + H], sc[:, 1, :], ALU.mult).then_inc(tail_asked, 1)
            dve.wait_ge(tail_summed, 1)
            nc.vector.tensor_copy(tl[:, 0:W], p_t[:, 0:W])
            nc.vector.tensor_copy(tl[:, W:W + H], p_d[:, 0:H])
            nc.vector.tensor_copy(tl[:, L.max:R], gm[:, :]).then_inc(tail_ready, 1)

        @block.scalar
        def _(act):
            def weights(n, b, use):
                act.wait_ge(d_ready, n + 1)
                wait(act, summed, (n - 1) * (G * U))
                nc.scalar.activation(wr[:, b, :, :, 1:G1].rearrange("p a h j -> p (a h) j"),
                                     d[:, :, :, :].rearrange("p a h j -> p (a h) j"), ACT.Exp).then_inc(wr_ready, 1)
                act.wait_ge(wr_ready, n + 1)
                for i, (c0, c1) in enumerate(HALVES):
                    for j in range(c0, c1):
                        for h in range(AH):
                            at = slice(h * dim, (h + 1) * dim)
                            last = nc.scalar.activation(rows[:, b, j, at], rows[:, b, j, at], ACT.Copy,
                                                        scale=wr[:, b, 0, h, j + 1:j + 2])
                        last.then_inc(scaled, 1)
                    act.wait_ge(den_ready, n + 1)
                    wait(act, stored[i], n * 16)
                    nc.scalar.copy(ring[:, i, 0:c1 - c0, W:W + H], dext[:, b, :, 1 + c0:1 + c1].rearrange("p h j -> p j h"))
                    nc.scalar.copy(ring[:, i, 0:c1 - c0, L.max:R],
                                   mext[:, b, :, 1 + c0:1 + c1].rearrange("p h j -> p j h")).then_inc(dm_ready[i], 1)

            act.wait_ge(er_ready, 1)
            sweep(act, weights)
            act.wait_ge(exp_asked, 1)
            nc.scalar.activation(sc[:, 1, :], sc[:, 0, :], ACT.Exp).then_inc(exp_done, 1)

        @block.tensor
        def _(pe):
            pe.wait_ge(max_asked, 1)
            for i in range((H + 3) // 4):
                w = min(4, H) * P
                last = nc.tensor.matmul(p_m[i][:, 0:w], ones[:, :], diag[:, 4 * i:min(4 * i + 4, H), :].rearrange("p h v -> p (h v)"),
                                        start=True, stop=True)
            last.then_inc(max_spread, 1)
            pe.wait_ge(tail_asked, 1)
            nc.tensor.matmul(p_t[:, 0:W], k.group[:, :], ts[:, 0:W], start=True, stop=True)
            nc.tensor.matmul(p_d[:, 0:H], k.group[:, :], ts[:, W:W + H], start=True, stop=True).then_inc(tail_summed, 1)


def join_maxima(nc, c, L, rows, m, d):
    c(nc.vector.tensor_tensor(m, rows[:, 0, L.max:L.row], rows[:, 1, L.max:L.row], ALU.max))
    c.done()
    return nc.vector.tensor_tensor(d, rows[:, :, L.max:L.row], m.unsqueeze(1).to_broadcast([P, 2, L.heads]), ALU.subtract)


JOIN_STEPS = 7


def join_sums(nc, c, L, rows, s, q, rec, has, out):
    H, W = L.heads, L.width
    c(nc.vector.tensor_tensor(q, rows[:, :, W:W + H], s, ALU.mult))
    c.done()
    c(nc.vector.tensor_tensor(rec, q[:, 0, :], q[:, 1, :], ALU.add))
    c.done()
    c(nc.vector.reciprocal(rec, rec))
    c.done()
    c(nc.vector.tensor_scalar(rec, rec, has, None, ALU.mult))
    c.done()
    c(nc.vector.tensor_tensor(q, s, rec.unsqueeze(1).to_broadcast([P, 2, H]), ALU.mult))
    c.done()
    for i in range(2):
        v = rows[:, i, 0:W].rearrange("p (h e) -> p h e", h=H)
        c(nc.vector.tensor_tensor(v, v, broad(q[:, i, :], L.dim), ALU.mult))
    c.done()
    return nc.vector.tensor_tensor(out, rows[:, 0, 0:W], rows[:, 1, 0:W], ALU.add)


def hidden_pass(nc, a, k):
    L = L1
    with Scope(nc, "hi") as s:
        w2 = s.sb("w2", [P, 4, D])
        alr = s.sb("alr", [P, 2, D])
        prod = s.sb("prod", [P, 4, D])
        wlr = s.sb("wlr", [P, 4, 16])
        rows = s.sb("rows", [P, 2, 2, L.row])
        m = s.sb("m", [P, 2, 8])
        d = s.sb("d", [P, 2, 2, 8])
        sc = s.sb("sc", [P, 2, 2, 8])
        q = s.sb("q", [P, 2, 2, 8])
        rec = s.sb("rec", [P, 2, 8])
        agg = s.sb("agg", [P, 2, 512])
        pos = s.sb("pos", [P, 2, 512])
        neg = s.sb("neg", [P, 2, 512])
        ex = s.sb("ex", [P, 2, 512])
        hid = s.sb("hid", [P, 2, 512])
        ht = s.sb("ht", [P, 2, 4, P])
        frow = s.sb("frow", [P, 2, L2.table])
        p_t = [s.ps(f"p_t{i}", [P, 512]) for i in range(2)]
        p_f = [s.ps(f"p_f{i}", [P, 512]) for i in range(2)]
        loaded, step, wlr_ready = s.sem("loaded"), s.sem("step"), s.sem("wlr_ready")
        rows_in, d_ready, sc_ready = s.sems("rows_in"), s.sem("d_ready"), s.sem("sc_ready")
        agg_ready, neg_ready, pos_ready, ex_ready = s.sem("agg_ready"), s.sem("neg_ready"), s.sem("pos_ready"), s.sem("ex_ready")
        hid_ready, t_ready, ht_ready, f_ready = s.sem("hid_ready"), s.sem("t_ready"), s.sem("ht_ready"), s.sem("f_ready")
        er_kept, row_copied, row_out, er_out = s.sem("er_kept"), s.sem("row_copied"), s.sems("row_out"), s.sem("er_out")
        scattered, step1, step2 = s.sem("scattered"), s.sem("step1"), s.sem("step2")
        block = s.block()

        @block.sync
        def _(sp):
            sp.dma_start(w2[:, :, :], a["w2"].rearrange("(k p) n -> p k n", p=P)).then_inc(loaded, 16)
            sp.dma_start(alr[:, 0, :], a["al2"].to_broadcast([P, D])).then_inc(loaded, 16)
            sp.dma_start(alr[:, 1, :], a["ar2"].to_broadcast([P, D])).then_inc(loaded, 16)

        def scatter(pool, n):
            pool.wait_ge(er_kept, n + 1)
            nc.gpsimd.indirect_dma_start(
                out=a["starts"], out_offset=bass.IndirectOffsetOnAxis(ap=k.first[:, n:n + 1], axis=0),
                in_=k.er[:, n, :], in_offset=None, bounds_check=P * T - 1, oob_is_err=False).then_inc(scattered, 16)

        @block.gpsimd
        def _(pool):
            for n in range(NB):
                b = n % 2
                wait(pool, agg_ready, n - 1)
                for i, (at, src) in enumerate([(k.last, a["sums1"]), (k.tail, a["tails1"])]):
                    nc.gpsimd.indirect_dma_start(out=rows[:, b, i, :], out_offset=None, in_=src,
                                                 in_offset=bass.IndirectOffsetOnAxis(ap=at[:, n:n + 1], axis=0)
                                                 ).then_inc(rows_in[b], 16)
                if n >= 4:
                    scatter(pool, n - 4)
            for n in range(NB - 4, NB):
                scatter(pool, n)
            pool.wait_ge(scattered, 16 * NB)

        @block.vector
        def _(dve):
            c, c1, c2 = Steps(dve, step), Steps(dve, step1), Steps(dve, step2)
            c(nc.vector.memset(wlr[:, :, :], 0.0))
            c.done()
            dve.wait_ge(loaded, 48)
            for lr in range(2):
                c(nc.vector.tensor_tensor(prod[:, :, :], w2[:, :, :], alr[:, lr:lr + 1, :].to_broadcast([P, 4, D]), ALU.mult))
                c.done()
                last = c(nc.vector.tensor_reduce(wlr[:, :, 8 * lr:8 * lr + 1], prod[:, :, :], AX.X, ALU.add))
                c.done()
            nc.vector.memset(prod[:, 0, 0:1], 0.0).then_inc(wlr_ready, 1)

            def maxima(n, b, use):
                c1.base, c1.n = n, 0
                dve.wait_ge(rows_in[b], use * 32 + 32)
                wait(dve, sc_ready, n - 1)
                join_maxima(nc, c1, L, rows[:, b, :, :], m[:, b, :], d[:, b, :, :]).then_inc(d_ready, 1)

            def elu(n, b):
                dve.wait_ge(ex_ready, n + 1)
                wait(dve, t_ready, n - 1)
                nc.vector.scalar_tensor_tensor(hid[:, b, :], ex[:, b, :], -1.0, pos[:, b, :], ALU.add,
                                               ALU.add).then_inc(hid_ready, 1)

            def vec(n, b, use):
                if not (isinstance(n, int) and n == NB - 1):
                    maxima(n + 1, 1 - b, use + b)
                c2.block(n, JOIN_STEPS)
                dve.wait_ge(sc_ready, n + 1)
                wait(dve, ex_ready, n - 1)
                join_sums(nc, c2, L, rows[:, b, :, :], sc[:, b, :, :], q[:, b, :, :], rec[:, b, :],
                          k.has[:, bass.ds(n, 1)], agg[:, b, :]).then_inc(agg_ready, 1)
                c2.end()
                dve.wait_ge(agg_ready, n + 1)
                nc.vector.tensor_scalar(neg[:, b, :], agg[:, b, :], 0.0, None, ALU.min).then_inc(neg_ready, 1)
                if not (isinstance(n, int) and n == 0):
                    elu(n - 1, 1 - b)

            maxima(0, 0, 0)
            sweep(dve, vec)
            elu(NB - 1, 0)

        @block.scalar
        def _(act):
            def exponents(n, b):
                act.wait_ge(d_ready, n + 1)
                wait(act, agg_ready, n - 1)
                nc.scalar.activation(sc[:, b, :, :], d[:, b, :, :], ACT.Exp).then_inc(sc_ready, 1)

            def out(n, b, use):
                act.wait_ge(t_ready, n + 1)
                wait(act, f_ready, n - 1)
                nc.scalar.copy(ht[:, b, :, :].rearrange("p k v -> p (k v)"), p_t[b][:, :]).then_inc(ht_ready, 1)
                act.wait_ge(f_ready, n + 1)
                wait(act, row_out[b], use * 16)
                nc.scalar.copy(frow[:, b, :], p_f[b][:, 0:L2.table]).then_inc(row_copied, 1)
                nc.scalar.copy(k.er[:, bass.ds(n, 1), :].rearrange("p a h -> p (a h)"),
                               p_f[b][:, D + 8:D + 16]).then_inc(er_kept, 1)
                act.wait_ge(row_copied, n + 1)
                act.dma_start(a["table2"][bass.ds(n * P, P), :], frow[:, b, :]).then_inc(row_out[b], 16)

            def sca(n, b, use):
                if not (isinstance(n, int) and n == NB - 1):
                    exponents(n + 1, 1 - b)
                act.wait_ge(agg_ready, n + 1)
                wait(act, hid_ready, n - 1)
                nc.scalar.activation(pos[:, b, :], agg[:, b, :], ACT.Relu)
                act.wait_ge(neg_ready, n + 1)
                nc.scalar.activation(ex[:, b, :], neg[:, b, :], ACT.Exp).then_inc(ex_ready, 1)
                if not (isinstance(n, int) and n == 0):
                    out(n - 1, 1 - b, use - 1 + b)

            exponents(0, 0)
            sweep(act, sca)
            out(NB - 1, 0, NB // 2)
            act.wait_ge(er_kept, NB)
            act.dma_start(a["er2"].rearrange("(n p) h -> p n h", p=P), k.er[:, :, :]).then_inc(er_out, 16)
            act.wait_ge(er_out, 16)
            act.wait_ge(row_out[0], 16 * (NB // 2 + 1))
            act.wait_ge(row_out[1], 16 * (NB // 2))

        @block.tensor
        def _(pe):
            pe.wait_ge(loaded, 48)
            pe.wait_ge(wlr_ready, 1)

            def mat(n, b, use):
                pe.wait_ge(hid_ready, n + 1)
                wait(pe, ht_ready, n - 1)
                for kt in range(4):
                    last = nc.tensor.transpose(p_t[b][:, kt * P:(kt + 1) * P], hid[:, b, kt * P:(kt + 1) * P], k.ident[:, :])
                last.then_inc(t_ready, 1)
                pe.wait_ge(ht_ready, n + 1)
                wait(pe, er_kept, n - 1)
                for kt in range(4):
                    nc.tensor.matmul(p_f[b][:, 0:D], ht[:, b, kt, :], w2[:, kt, :], start=kt == 0, stop=kt == 3)
                for kt in range(4):
                    last = nc.tensor.matmul(p_f[b][:, D:D + 16], ht[:, b, kt, :], wlr[:, kt, :], start=kt == 0, stop=kt == 3)
                last.then_inc(f_ready, 1)

            sweep(pe, mat)


def final_pass(nc, a, k):
    L = L2
    GR = NB // GB
    FILLS = 9 * 4
    with Scope(nc, "fi") as s:
        wf = [s.sb(f"wf{i}", [P, E, 2, D]) for i in range(3)]
        bn = s.sb("bn", [P, 10, E * 2])
        scale = s.sb("scale", [P, 2, E * 2])
        shift = s.sb("shift", [P, 2, E * 2])
        wr = s.sb("wr", [P, 2, E])
        br = s.sb("br", [P, E])
        bo = s.sb("bo", [E, D])
        rows = s.sb("rows", [P, GB, 2, L.row])
        m = s.sb("m", [P, GB, 1])
        d = s.sb("d", [P, GB, 2, 1])
        sc = s.sb("sc", [P, GB, 2, 1])
        q = s.sb("q", [P, GB, 2, 1])
        rec = s.sb("rec", [P, GB, 1])
        agg = s.sb("agg", [P, GB, D])
        res = s.sb("res", [P, GB, D])
        y = s.sb("y", [P, 2, GB, D])
        stats = s.sb("stats", [P, GB, 6])
        mv = s.sb("mv", [P, GB, 2])
        var = s.sb("var", [P, GB])
        sd = s.sb("sd", [P, GB])
        rstd = s.sb("rstd", [P, GB])
        xn = s.sb("xn", [P, GB, D])
        xt = s.sb("xt", [P, 2, 2, GB * P])
        lg = s.sb("lg", [P, GB, E])
        top = s.sb("top", [P, GB])
        lge = s.sb("lge", [P, GB, E])
        tot = s.sb("tot", [P, GB])
        w = s.sb("w", [P, 2, GB, E])
        wt = s.sb("wt", [E, 2, GB * P])
        h1 = s.sb("h1", [P, 2, GB * P])
        h2 = s.sb("h2", [P, 2, GB * P])
        p_h = [s.ps(f"p_h{i}", [P, 512]) for i in range(4)]
        p_y = [s.ps(f"p_y{i}", [P, 512]) for i in range(2)]
        p_t = [s.ps(f"p_t{i}", [P, 512]) for i in range(2)]
        loaded, bn_in, step, bn_ready = s.sem("loaded"), s.sem("bn_in"), s.sem("step"), s.sem("bn_ready")
        sd_asked, sd_done, passed = s.sem("sd_asked"), s.sem("sd_done"), s.sem("passed")
        rows_in, res_in, joined = s.sems("rows_in", GB), s.sem("res_in"), s.sem("joined")
        d_ready, sc_ready, x_ready = s.sem("d_ready"), s.sem("sc_ready"), s.sem("x_ready")
        xn_ready, t_ready, xt_ready = s.sem("xn_ready"), s.sem("t_ready"), s.sem("xt_ready")
        gate_ready, lg_ready, lge_ready = s.sem("gate_ready"), s.sem("lg_ready"), s.sem("lge_ready")
        w_ready, wt_turned, wt_ready = s.sem("w_ready"), s.sem("wt_turned"), s.sem("wt_ready")
        h_filled, h_kept = s.sem("h_filled"), s.sem("h_kept")
        y_filled, y_added, y_out = s.sem("y_filled"), s.sem("y_added"), s.sems("y_out")
        block = s.block()

        def groups(eng, first, main):
            first()
            main(0, 0, 0, True)
            with eng.Fori(0, (GR - 3) // 2, 1) as t:
                main(t * 2 + 1, 1, t, True)
                main(t * 2 + 2, 0, t + 1, True)
            main(GR - 2, 1, (GR - 2) // 2, True)
            main(GR - 1, 0, (GR - 1) // 2, False)

        @block.sync
        def _(sp):
            def load(g, b, use):
                sp.dma_start(res[:, :, :], a["res"][bass.ds(g * (GB * P), GB * P), :].rearrange("(n p) d -> p n d", p=P)
                             ).then_inc(res_in, 16)

            def first():
                load(0, 0, 0)
                for i, name in enumerate(("b1", "g1", "be1", "m1", "v1", "b2", "g2", "be2", "m2", "v2")):
                    sp.dma_start(bn[:, i, :], a[name].rearrange("p e k -> p (e k)")).then_inc(bn_in, 16)
                for i, name in enumerate(("f1", "f2", "fo")):
                    sp.dma_start(wf[i][:, :, :, :], a[name].rearrange("e (k p) n -> p e k n", p=P)).then_inc(loaded, 16)
                sp.dma_start(wr[:, :, :], a["wr"].rearrange("(k p) n -> p k n", p=P)).then_inc(loaded, 16)
                sp.dma_start(br[:, :], a["br"].to_broadcast([P, E])).then_inc(loaded, 16)
                sp.dma_start(bo[:, :], a["bo"]).then_inc(loaded, 16)

            def main(g, b, use, more):
                if more:
                    wait_apart(sp, nc.sync, x_ready, g + 1, passed)
                    load(g + 1, 1 - b, use + b)
                wait_apart(sp, nc.sync, y_added, (g + 1) * FILLS, passed)
                sp.dma_start(a["out"][bass.ds(g * (GB * P), GB * P), :].rearrange("(n p) d -> p n d", p=P),
                             y[:, b, :, :]).then_inc(y_out[b], 16)

            groups(sp, first, main)
            sp.wait_ge(y_out[0], 16 * (GR // 2 + 1))
            sp.wait_ge(y_out[1], 16 * (GR // 2))

        @block.gpsimd
        def _(pool):
            for n in range(NB):
                wait(pool, joined, n - GB + 1)
                for i, (at, src) in enumerate([(k.last, a["sums2"]), (k.tail, a["tails2"])]):
                    nc.gpsimd.indirect_dma_start(out=rows[:, n % GB, i, :], out_offset=None, in_=src,
                                                 in_offset=bass.IndirectOffsetOnAxis(ap=at[:, n:n + 1], axis=0)
                                                 ).then_inc(rows_in[n % GB], 16)

        @block.vector
        def _(dve):
            c = Steps(dve, step, passed)
            dve.wait_ge(bn_in, 160)
            for i in range(2):
                last = nc.vector.tensor_scalar(shift[:, i, :], bn[:, 5 * i + 4, :], 1e-3, None, ALU.add)
            last.then_inc(sd_asked, 1)
            dve.wait_ge(sd_done, 1)
            c(nc.vector.reciprocal(scale[:, :, :], scale[:, :, :]))
            c.done()
            for i in range(2):
                c(nc.vector.tensor_tensor(scale[:, i, :], scale[:, i, :], bn[:, 5 * i + 1, :], ALU.mult))
                c(nc.vector.tensor_tensor(shift[:, i, :], bn[:, 5 * i, :], bn[:, 5 * i + 3, :], ALU.subtract))
            c.done()
            for i in range(2):
                c(nc.vector.tensor_tensor(shift[:, i, :], shift[:, i, :], scale[:, i, :], ALU.mult))
            c.done()
            for i in range(2):
                last = nc.vector.tensor_tensor(shift[:, i, :], shift[:, i, :], bn[:, 5 * i + 2, :], ALU.add)
            last.then_inc(bn_ready, 1)
            dve.wait_ge(loaded, 96)
            start = c.n
            PER = GB * (1 + JOIN_STEPS + 1 + 1 + 1) - 1 + 1 + 4

            def maxima(g):
                for i in range(GB):
                    dve.wait_ge(rows_in[i], g * 32 + 32)
                    join_maxima(nc, c, L, rows[:, i, :, :], m[:, i, :], d[:, i, :, :]).then_inc(d_ready, 1)

            def sums(g, b, use, blocks):
                for i in blocks:
                    dve.wait_ge(sc_ready, g * GB + (i + 1))
                    join_sums(nc, c, L, rows[:, i, :, :], sc[:, i, :, :], q[:, i, :, :], rec[:, i, :],
                              k.has[:, bass.ds(g * GB + i, 1)], agg[:, i, :]).then_inc(joined, 1)
                    dve.wait_ge(joined, g * GB + (i + 1))
                    if i == 0:
                        dve.wait_ge(res_in, g * 16 + 16)
                        wait(dve, y_out[b], use * 16)
                    c(nc.vector.tensor_tensor(y[:, b, i, :], agg[:, i, :], res[:, i, :], ALU.add))
                    c.done()
                    ins = nc.vector.bn_stats(stats[:, i, :], y[:, b, i, :])
                    if i < GB - 1:
                        c(ins)
                    else:
                        ins.then_inc(x_ready, 1)

            def spread(g):
                dve.wait_ge(x_ready, g + 1)
                nc.vector.sem_inc(passed)
                for i in range(GB):
                    c(nc.vector.bn_aggr(mv[:, i, :], stats[:, i, :]))
                c.done()
                nc.vector.tensor_scalar(var[:, :], mv[:, :, 1], 1e-5, None, ALU.add).then_inc(sd_asked, 1)

            def norm(g, b):
                dve.wait_ge(sd_done, g + 2)
                c(nc.vector.reciprocal(rstd[:, :], sd[:, :]))
                c.done()
                wait(dve, t_ready, g * GB)
                for i in range(GB):
                    nc.vector.tensor_scalar(xn[:, i, :], y[:, b, i, :], mv[:, i, 0:1], rstd[:, i:i + 1],
                                            ALU.subtract, ALU.mult).then_inc(xn_ready, 1)

            def gate_logits(g):
                dve.wait_ge(gate_ready, g + 1)
                c(nc.vector.tensor_tensor(lg[:, :, :], p_t[0][:, 0:GB * E].rearrange("p (n e) -> p n e", n=GB),
                                          br[:, :].unsqueeze(1).to_broadcast([P, GB, E]), ALU.add))
                c.done()
                c(nc.vector.tensor_reduce(top[:, :], lg[:, :, :], AX.X, ALU.max))
                c.done()
                nc.vector.tensor_tensor(lg[:, :, :], lg[:, :, :], broad(top[:, :], E), ALU.subtract).then_inc(lg_ready, 1)

            def gate_weights(g, b):
                dve.wait_ge(lge_ready, g + 1)
                c(nc.vector.tensor_reduce(tot[:, :], lge[:, :, :], AX.X, ALU.add))
                c.done()
                c(nc.vector.reciprocal(tot[:, :], tot[:, :]))
                c.done()
                nc.vector.tensor_tensor(w[:, b, :, :], lge[:, :, :], broad(tot[:, :], E), ALU.mult).then_inc(w_ready, 1)

            def add(g, b, e):
                for i in range(GB):
                    v = i // 2
                    if i % 2 == 0:
                        dve.wait_ge(y_filled, g * FILLS + ((e + 1) * 4 + v + 1))
                        wait(dve, y_added, g * FILLS + e * 4 + v + 1 if e >= 0 else 0)
                    out = p_y[v % 2][:, i % 2 * D:(i % 2 + 1) * D]
                    if e < 0:
                        ins = nc.vector.tensor_tensor(y[:, b, i, :], out, y[:, b, i, :], ALU.add)
                    else:
                        ins = nc.vector.scalar_tensor_tensor(y[:, b, i, :], out, w[:, b, i, e:e + 1], y[:, b, i, :],
                                                             ALU.mult, ALU.add)
                    if i % 2 == 1 or i == GB - 1:
                        ins.then_inc(y_added, 1)

            def prepare(g):
                c.base, c.n = g * PER + start, 0

            def first():
                prepare(0)
                maxima(0)
                sums(0, 0, 0, range(GB))
                spread(0)
                norm(0, 0)
                gate_logits(0)
                gate_weights(0, 0)
                assert c.n == PER, c.n

            def main(g, b, use, more):
                add(g, b, -1)
                if more:
                    prepare(g + 1)
                    maxima(g + 1)
                for e in range(E):
                    add(g, b, e)
                    if more:
                        if e < 4:
                            sums(g + 1, 1 - b, use + b, [i for i in (2 * e, 2 * e + 1) if i < GB])
                        elif e == 4:
                            spread(g + 1)
                            norm(g + 1, 1 - b)
                        elif e == 6:
                            gate_logits(g + 1)
                if more:
                    gate_weights(g + 1, 1 - b)

            groups(dve, first, main)

        @block.scalar
        def _(act):
            act.wait_ge(sd_asked, 1)
            nc.scalar.activation(scale[:, :, :], shift[:, :, :], ACT.Sqrt).then_inc(sd_done, 1)
            act.wait_ge(bn_ready, 1)

            def exponents(g):
                for i in range(GB):
                    act.wait_ge(d_ready, g * GB + (i + 1))
                    wait(act, joined, g * GB + (i + 1 - GB))
                    nc.scalar.activation(sc[:, i, :, :], d[:, i, :, :], ACT.Exp).then_inc(sc_ready, 1)

            def root(g):
                act.wait_ge(sd_asked, g + 2)
                nc.scalar.activation(sd[:, :], var[:, :], ACT.Sqrt).then_inc(sd_done, 1)

            def turned(g, b):
                for i in range(GB):
                    act.wait_ge(t_ready, g * GB + (i + 1))
                    nc.scalar.copy(xt[:, b, :, i * P:(i + 1) * P],
                                   p_t[i % 2][:, 0:D].rearrange("p (m v) -> p m v", m=2)).then_inc(xt_ready, 1)

            def gates(g):
                act.wait_ge(lg_ready, g + 1)
                wait(act, w_ready, g)
                nc.scalar.activation(lge[:, :, :], lg[:, :, :], ACT.Exp).then_inc(lge_ready, 1)

            def weights(g, b):
                act.wait_ge(wt_turned, g + 1)
                nc.scalar.copy(wt[:, b, 0:4 * P], p_t[0][0:E, 0:4 * P])
                nc.scalar.copy(wt[:, b, 4 * P:GB * P], p_t[1][0:E, 0:(GB - 4) * P]).then_inc(wt_ready, 1)

            def keep(g, e, layer):
                out = (h1, h2)[layer]
                for r in range(4):
                    mt, half = r // 2, r % 2
                    fill = (e * 2 + layer) * 4 + r
                    act.wait_ge(h_filled, g * (E * 8) + (fill + 1))
                    nc.scalar.activation(out[:, mt, half * GN:(half + 1) * GN], p_h[r][:, 0:GN], ACT.Relu,
                                         bias=shift[:, layer, 2 * e + mt:2 * e + mt + 1],
                                         scale=scale[:, layer, 2 * e + mt:2 * e + mt + 1]).then_inc(h_kept, 1)

            def first():
                exponents(0)
                root(0)
                turned(0, 0)
                gates(0)
                weights(0, 0)

            def main(g, b, use, more):
                if more:
                    exponents(g + 1)
                keep(g, 0, 0)
                for e in range(E):
                    keep(g, e, 1)
                    if more and e == 5:
                        root(g + 1)
                    if more and e == 6:
                        turned(g + 1, 1 - b)
                    if more and e == 7:
                        gates(g + 1)
                    if e < E - 1:
                        keep(g, e + 1, 0)
                if more:
                    weights(g + 1, 1 - b)

            groups(act, first, main)

        @block.tensor
        def _(pe):
            pe.wait_ge(loaded, 96)

            def transposes(g, b):
                for i in range(GB):
                    pe.wait_ge(xn_ready, g * GB + (i + 1))
                    if i > 1:
                        pe.wait_ge(xt_ready, g * GB + (i - 1))
                    for mt in range(2):
                        last = nc.tensor.transpose(p_t[i % 2][:, mt * P:(mt + 1) * P], xn[:, i, mt * P:(mt + 1) * P],
                                                   k.ident[:, :])
                    last.then_inc(t_ready, 1)

            def gate(g, b):
                pe.wait_ge(xt_ready, g * GB + GB)
                for i in range(GB):
                    for kt in range(2):
                        last = nc.tensor.matmul(p_t[0][:, i * E:(i + 1) * E], xt[:, b, kt, i * P:(i + 1) * P],
                                                wr[:, kt, :], start=kt == 0, stop=kt == 1)
                last.then_inc(gate_ready, 1)

            def turn_weights(g, b):
                pe.wait_ge(w_ready, g + 1)
                for i in range(GB):
                    last = nc.tensor.transpose(p_t[i // 4][0:E, i % 4 * P:(i % 4 + 1) * P], w[:, b, i, :], k.ident[:, :])
                last.then_inc(wt_turned, 1)

            def layer(g, b, e, lay):
                src = xt[:, b, :, :] if lay == 0 else h1[:, :, :]
                if lay == 1:
                    pe.wait_ge(h_kept, g * (E * 8) + (e * 8 + 4))
                for r in range(4):
                    mt, half = r // 2, r % 2
                    fill = (e * 2 + lay) * 4 + r
                    wait(pe, h_kept, g * (E * 8) + (fill - 3))
                    for kt in range(2):
                        last = nc.tensor.matmul(p_h[r][:, 0:GN], wf[lay][:, e, kt, mt * P:(mt + 1) * P],
                                                src[:, kt, half * GN:(half + 1) * GN], start=kt == 0, stop=kt == 1)
                    last.then_inc(h_filled, 1)

            def outputs(g, b, e):
                if e >= 0:
                    pe.wait_ge(h_kept, g * (E * 8) + (e * 8 + 8))
                else:
                    pe.wait_ge(wt_ready, g + 1)
                for i in range(GB):
                    v = i // 2
                    if i % 2 == 0:
                        wait(pe, y_added, g * FILLS + ((e + 1) * 4 + v - 1))
                    out = p_y[v % 2][:, i % 2 * D:(i % 2 + 1) * D]
                    if e < 0:
                        last = nc.tensor.matmul(out, wt[:, b, i * P:(i + 1) * P], bo[:, :], start=True, stop=True)
                    else:
                        for kt in range(2):
                            last = nc.tensor.matmul(out, h2[:, kt, i * P:(i + 1) * P], wf[2][:, e, kt, :],
                                                    start=kt == 0, stop=kt == 1)
                    if i % 2 == 1 or i == GB - 1:
                        last.then_inc(y_filled, 1)

            def first():
                transposes(0, 0)
                gate(0, 0)
                turn_weights(0, 0)

            def main(g, b, use, more):
                outputs(g, b, -1)
                layer(g, b, 0, 0)
                for e in range(E):
                    layer(g, b, e, 1)
                    if more and e == 6:
                        transposes(g + 1, 1 - b)
                    if more and e == 7:
                        gate(g + 1, 1 - b)
                    if e < E - 1:
                        layer(g, b, e + 1, 0)
                    outputs(g, b, e)
                if more:
                    turn_weights(g + 1, 1 - b)

            groups(pe, first, main)


def gps_kernel(nc, a):
    with Scope(nc, "k") as k:
        k.iota = k.sb("iota", [P, P])
        k.iop = k.sb("iop", [P, 1])
        k.ident = k.sb("ident", [P, P])
        k.src = k.sb("src", [P, T], I32)
        k.dst = k.sb("dst", [P, T], I32)
        k.er = k.sb("er", [P, NB, 8])
        k.hist = k.sb("hist", [NB, P])
        k.restart = k.sb("restart", [P, T])
        k.same = k.sb("same", [P, T])
        k.first = k.sb("first", [P, NB], I32)
        k.last = k.sb("last", [P, NB], I32)
        k.tail = k.sb("tail", [P, NB], I32)
        k.has = k.sb("has", [P, NB])
        k.group = k.sb("group", [P, P])
        k.open = k.sb("open", [P, 1])
        with Scope(nc, "kq") as q:
            k.x = q.sb("x", [P, NB, D])
            k.qt = q.sb("qt", [P, 2, NP])
            k.cbd = q.sb("cbd", [P, 2, P])
            k.kbd = q.sb("kbd", [P, 2, P])
            node_pass(nc, a, k)
            attention_pass(nc, a, k)
        edge_pass(nc, a, k, L1)
        hidden_pass(nc, a, k)
        edge_pass(nc, a, k, L2)
        final_pass(nc, a, k)


_SHAPES = {
    "table1": (NP, L1.table), "table2": (NP, L2.table), "er1": (NP, 8), "er2": (NP, 8), "res": (NP, D),
    "starts": (P * T, 8), "sums1": (P * T, L1.row), "sums2": (P * T, L2.row),
    "tails1": (P + 1, L1.row), "tails2": (P + 1, L2.row),
}


def kernel(**inputs):
    import numpy as np
    import concourse.bacc as bacc
    from concourse.bass_utils import run_bass_kernel_spmd as run

    v = {name: np.asarray(x) for name, x in inputs.items()}

    def edges(name, fill):
        out = np.full(P * T, fill, np.int32)
        out[:EDGES] = v[name]
        return out.reshape(P, T)

    def by_feature(name):
        return np.ascontiguousarray(v["L0_ffn_" + name].reshape(E, 2, P).transpose(2, 0, 1))

    x = np.zeros((NP, D), np.float32)
    x[:NODES] = v["x"]
    given = {
        "x": x, "src": edges("src", 0), "dst": edges("dst", NODES),
        "w1": v["L0_gnn_W1"], "al1": v["L0_gnn_attn_l1"].reshape(1, -1), "ar1": v["L0_gnn_attn_r1"].reshape(1, -1),
        "w2": v["L0_gnn_W2"], "al2": v["L0_gnn_attn_l2"], "ar2": v["L0_gnn_attn_r2"],
        "wq": v["L0_mix_Wq"].T, "wkv": v["L0_mix_Wkv"].T, "wproj": v["L0_mix_Wproj"].T,
        "bproj": v["L0_mix_bproj"].reshape(1, -1),
        "wr": v["L0_ffn_Wr"], "br": v["L0_ffn_br"].reshape(1, -1),
        "f1": v["L0_ffn_W1"], "f2": v["L0_ffn_W2"], "fo": v["L0_ffn_Wo"], "bo": v["L0_ffn_bo"],
        **{name: by_feature(name) for name in ("b1", "g1", "be1", "m1", "v1", "b2", "g2", "be2", "m2", "v2")},
    }
    nc = bacc.Bacc("TRN2", target_bir_lowering=False, num_devices=1)
    arrays, a = {}, {}
    for name, array in given.items():
        array = np.ascontiguousarray(array)
        arrays[f"in_{name}"] = array
        a[name] = nc.dram_tensor(f"in_{name}", array.shape, mybir.dt.from_np(array.dtype), kind="ExternalInput").ap()
    for name, shape in _SHAPES.items():
        a[name] = nc.dram_tensor(f"scratch_{name}", shape, F32, kind="Internal").ap()
    a["out"] = nc.dram_tensor("out", (NP, D), F32, kind="ExternalOutput").ap()
    gps_kernel(nc, a)
    r = run(nc, [arrays], core_ids=[0])
    return r.results[0]["out"][:NODES]
```

```python
import concourse.bass as bass
from concourse import mybir
from contextlib import ExitStack

F32 = mybir.dt.float32
BF16 = mybir.dt.bfloat16
I32 = mybir.dt.int32
ALU = mybir.AluOpType
ACT = mybir.ActivationFunctionType
AX = mybir.AxisListType

P = 128
NODES = 6250
D = 256
NB = 49
NP = NB * P
EDGES = 106250
G = 17
T = NB * G
E = 8
HEADS = 8
MH = D // HEADS
BIG = 1.0e30
ROUND = 12582912.0
NONE = 4.0e6
HALVES = [(0, 9), (9, 17)]
LENGTH = [c1 - c0 for c0, c1 in HALVES]
GB = 7
GN = GB * P // 2

assert P * T >= EDGES and NP >= NODES and NB % GB == 0


class Layer:

    def __init__(self, name, heads, width, act_heads):
        self.name, self.heads, self.width = name, heads, width
        self.dim = width // heads
        self.table = width + 8
        self.row = width + 2 * heads
        self.den = width
        self.max = width + heads
        self.act_heads = act_heads


L1 = Layer("l1", 8, 512, 5)
L2 = Layer("l2", 1, 256, 1)


def wait(eng, sem, value):
    if not isinstance(value, int) or value > 0:
        eng.wait_ge(sem, value)


def sweep(eng, body, first=None):
    body(0, 0, 0)
    body(1, 1, 0)
    with eng.Fori(1, NB // 2, 1) as t:
        body(t * 2, 0, t)
        body(t * 2 + 1, 1, t)
    body(NB - 1, 0, NB // 2)


def wait_apart(eng, own, sem, value, passed):
    eng.wait_ge(sem, value)
    own.sem_inc(passed)


def groups(eng, first, main):
    last = NB // GB - 1
    first()
    main(0, 0, 0, True)
    with eng.Fori(0, (last - 2) // 2, 1) as t:
        main(t * 2 + 1, 1, t, True)
        main(t * 2 + 2, 0, t + 1, True)
    main(last - 1, 1, (last - 1) // 2, True)
    main(last, 0, last // 2, False)


class Steps:

    def __init__(self, eng, sem, passed=None):
        self.eng, self.sem, self.base, self.n = eng, sem, 0, 0
        self.passed = passed

    def __call__(self, ins):
        ins.then_inc(self.sem, 1)
        self.n += 1
        return ins

    def done(self):
        self.eng.wait_ge(self.sem, self.base + self.n)

    def block(self, n, per):
        self.base, self.n, self.per = n * per, 0, per

    def end(self):
        assert self.n == self.per, (self.n, self.per)


def broad(ap, n):
    return ap.unsqueeze(len(ap.shape)).to_broadcast([*ap.shape, n])


class Scope:

    def __init__(self, nc, tag):
        self.nc, self.tag, self.stack, self.held = nc, tag, ExitStack(), []

    def __enter__(self):
        self.stack.__enter__()
        return self

    def __exit__(self, *a):
        out = self.stack.__exit__(*a)
        if self.held and a[0] is None:
            self.nc.clear_and_free_semaphores(self.held)
            self.nc.all_engine_barrier()
        return out

    def sb(self, name, shape, dt=F32):
        return self.stack.enter_context(self.nc.sbuf_tensor(f"{self.tag}_{name}", shape, dt))

    def ps(self, name, shape, dt=F32):
        return self.stack.enter_context(self.nc.psum_tensor(f"{self.tag}_{name}", shape, dt))

    def sem(self, name):
        self.held.append(self.nc.alloc_semaphore(f"{self.tag}_{name}"))
        return self.held[-1]

    def sems(self, name, n=2):
        return [self.sem(f"{name}{i}") for i in range(n)]

    def block(self):
        return self.stack.enter_context(self.nc.Block())


def node_pass(nc, a, k):
    with Scope(nc, "na") as s:
        w1 = s.sb("w1", [P, 2, 512])
        wkv = s.sb("wkv", [P, 2, 512])
        wq = s.sb("wq", [P, 2, D])
        alr = s.sb("alr", [P, 2, 512])
        prod = s.sb("prod", [P, 512])
        wlr = s.sb("wlr", [P, 2, 16])
        io_i = s.sb("io_i", [P, P], I32)
        iop_i = s.sb("iop_i", [P, 1], I32)
        zero = s.sb("zero", [P, 2 * (P + 1) + P])
        hi_i = s.sb("hi_i", [P, T], I32)
        lo_i = s.sb("lo_i", [P, T], I32)
        hi = s.sb("hi", [P, T])
        lo = s.sb("lo", [P, T])
        oneh = s.sb("oneh", [P, 2, G, NB], BF16)
        onel = s.sb("onel", [P, 2, G, P], BF16)
        x = s.sb("x", [P, NB, D])
        qt = s.sb("qt", [P, 2, D])
        q_out, passed_sp = s.sems("q_out"), s.sem("passed_sp")
        blank = s.sb("blank", [P, T // GB * 8])
        stats = s.sb("stats", [P, NB, 6])
        mv = s.sb("mv", [P, NB, 2])
        sd = s.sb("sd", [P, NB])
        rstd = s.sb("rstd", [P, NB])
        xn = s.sb("xn", [P, 2, D])
        xt = s.sb("xt", [P, 2, 2, P])
        frow = s.sb("frow", [P, 2, L1.table])
        kmin = s.sb("kmin", [P, 2, D])
        kexp = s.sb("kexp", [P, 2, D])
        kphi = s.sb("kphi", [P, 2, D])
        vext = s.sb("vext", [P, 2, 2, P + 1])
        qmin = s.sb("qmin", [P, 2, D])
        qexp = s.sb("qexp", [P, 2, D])
        p_t = [s.ps(f"p_t{i}", [P, 512]) for i in range(2)]
        p_f = [s.ps(f"p_f{i}", [P, 512]) for i in range(2)]
        p_kv = [s.ps(f"p_kv{i}", [P, 512]) for i in range(2)]
        p_q = s.ps("p_q", [P, 512])
        p_acc = s.ps("p_acc", [P, 512])
        CW = 2 * (P + 1)
        p_c, p_h = p_acc[:, 0:CW], p_acc[0:NB, CW:CW + P]
        loaded, edges_in = s.sem("loaded"), s.sem("edges_in")
        iota_made, step = s.sem("iota_made"), s.sem("step")
        const_ready, wlr_ready = s.sem("const_ready"), s.sem("wlr_ready")
        x_in = s.sems("x_in", GB)
        passed, mv_ready, rstd_ready = s.sem("passed"), s.sem("mv_ready"), s.sem("rstd_ready")
        xn_ready, t_ready, xt_ready = s.sem("xn_ready"), s.sem("t_ready"), s.sem("xt_ready")
        proj_ready, q_ready = s.sem("proj_ready"), s.sem("q_ready")
        row_copied, row_out = s.sem("row_copied"), s.sems("row_out")
        kmin_ready, kexp_ready, kv_ready = s.sem("kmin_ready"), s.sem("kexp_ready"), s.sem("kv_ready")
        qmin_ready, qexp_ready, q_kept = s.sem("qmin_ready"), s.sem("qexp_ready"), s.sem("q_kept")
        ctx_added, onehot_ready, counted = s.sem("ctx_added"), s.sem("onehot_ready"), s.sem("counted")
        lr_copied, acc_ready, er_out = s.sem("lr_copied"), s.sem("acc_ready"), s.sem("er_out")
        blanked, blank_out = s.sem("blanked"), s.sem("blank_out")
        block = s.block()

        @block.sync
        def _(sp):
            for i in range(GB):
                n = i * GB
                sp.dma_start(x[:, n:n + GB, :], a["x"][n * P:(n + GB) * P, :].rearrange("(n p) d -> p n d", p=P)
                             ).then_inc(x_in[i], 16)
            sp.dma_start(k.dst[:, :], a["dst"]).then_inc(edges_in, 16)
            sp.dma_start(k.src[:, :], a["src"]).then_inc(edges_in, 16)
            sp.dma_start(w1[:, :, :], a["w1"].rearrange("(k p) n -> p k n", p=P)).then_inc(loaded, 16)
            sp.dma_start(wkv[:, :, :], a["wkv"].rearrange("(k p) n -> p k n", p=P)).then_inc(loaded, 16)
            sp.dma_start(wq[:, :, :], a["wq"].rearrange("(k p) n -> p k n", p=P)).then_inc(loaded, 16)
            sp.dma_start(alr[:, 0, :], a["al1"].to_broadcast([P, 512])).then_inc(loaded, 16)
            sp.dma_start(alr[:, 1, :], a["ar1"].to_broadcast([P, 512])).then_inc(loaded, 16)
            sp.wait_ge(blanked, 1)
            starts = a["starts"].rearrange("(p c t) h -> p c (t h)", p=P, c=GB)
            for i in range(GB):
                sp.dma_start(starts[:, i, :], blank[:, :]).then_inc(blank_out, 16)
            sp.wait_ge(blank_out, 16 * GB)

            def keep_queries(n, b, use):
                wait_apart(sp, nc.sync, q_kept, n + 1, passed_sp)
                sp.dma_start(a["qt"][bass.ds(n * P, P), :], qt[:, b, :]).then_inc(q_out[b], 16)

            sweep(sp, keep_queries)
            sp.wait_ge(q_out[0], 16 * (NB // 2 + 1))
            sp.wait_ge(q_out[1], 16 * (NB // 2))


        @block.gpsimd
        def _(pool):
            nc.gpsimd.iota(io_i[:, :], [[1, P]], base=0, channel_multiplier=0).then_inc(iota_made, 1)
            nc.gpsimd.iota(iop_i[:, :], [[0, 1]], base=0, channel_multiplier=1).then_inc(iota_made, 1)
            nc.gpsimd.memset(blank[:, :], 0.0).then_inc(blanked, 1)

        @block.vector
        def _(dve):
            c = Steps(dve, step, passed)
            dve.wait_ge(iota_made, 2)
            c(nc.vector.tensor_copy(k.iota[:, :], io_i[:, :]))
            c(nc.vector.tensor_copy(k.iop[:, :], iop_i[:, :]))
            c(nc.vector.memset(zero[:, :], 0.0))
            c(nc.vector.memset(vext[:, :, :, P:P + 1], 1.0))
            c.done()
            nc.vector.tensor_scalar(k.ident[:, :], k.iota[:, :], k.iop[:, 0:1], None, ALU.is_equal).then_inc(const_ready, 1)
            dve.wait_ge(edges_in, 32)
            c(nc.vector.tensor_scalar(hi_i[:, :], k.dst[:, :], 7, None, ALU.logical_shift_right))
            c(nc.vector.tensor_scalar(lo_i[:, :], k.dst[:, :], 127, None, ALU.bitwise_and))
            c.done()
            c(nc.vector.tensor_copy(hi[:, :], hi_i[:, :]))
            c(nc.vector.tensor_copy(lo[:, :], lo_i[:, :]))
            dve.wait_ge(loaded, 5 * 16)
            for kt in range(2):
                for lr in range(2):
                    c(nc.vector.tensor_tensor(prod[:, :], w1[:, kt, :], alr[:, lr, :], ALU.mult))
                    c.done()
                    c(nc.vector.tensor_reduce(wlr[:, kt, 8 * lr:8 * lr + 8],
                                              prod[:, :].rearrange("p (h d) -> p h d", h=8), AX.X, ALU.add))
                    c.done()
            nc.vector.memset(prod[:, 0:1], 0.0).then_inc(wlr_ready, 1)
            for n in range(NB):
                if n % GB == 0:
                    dve.wait_ge(x_in[n // GB], 16)
                c(nc.vector.bn_stats(stats[:, n, :], x[:, n, :]))
            c.done()
            nc.vector.sem_inc(passed)
            for n in range(NB):
                c(nc.vector.bn_aggr(mv[:, n, :], stats[:, n, :]))
            c.done()
            nc.vector.tensor_scalar(rstd[:, :], mv[:, :, 1], 1e-5, None, ALU.add).then_inc(mv_ready, 1)
            dve.wait_ge(rstd_ready, 1)
            c(nc.vector.reciprocal(rstd[:, :], sd[:, :]))
            c.done()
            start = c.n

            def norm(n, b):
                wait(dve, t_ready, n - 1)
                nc.vector.tensor_scalar(xn[:, b, :], x[:, bass.ds(n, 1), :].rearrange("p a d -> p (a d)"),
                                        mv[:, bass.ds(n, 1), 0:1].rearrange("p a d -> p (a d)"),
                                        rstd[:, bass.ds(n, 1)], ALU.subtract, ALU.mult).then_inc(xn_ready, 1)

            norm(0, 0)

            def vec(n, b, use):
                if not (isinstance(n, int) and n == NB - 1):
                    norm(n + 1, 1 - b)
                wait(dve, counted, n - 1)
                nc.vector.tensor_tensor(oneh[:, b, :, :], broad(hi[:, bass.ds(n * G, G)], NB),
                                        k.iota[:, 0:NB].unsqueeze(1).to_broadcast([P, G, NB]), ALU.is_equal)
                nc.vector.tensor_tensor(onel[:, b, :, :], broad(lo[:, bass.ds(n * G, G)], P),
                                        k.iota[:, :].unsqueeze(1).to_broadcast([P, G, P]),
                                        ALU.is_equal).then_inc(onehot_ready, 1)
                dve.wait_ge(proj_ready, n + 1)
                wait(dve, ctx_added, n - 1)
                if isinstance(n, int) and n == NB - 1:
                    nc.vector.tensor_scalar(vext[:, b, :, P:P + 1], k.iop[:, :].unsqueeze(1).to_broadcast([P, 2, 1]),
                                            float(NODES - n * P), None, ALU.is_lt)
                nc.vector.tensor_scalar(kmin[:, b, :], p_kv[b][:, 0:D], 0.0, None, ALU.min).then_inc(kmin_ready, 1)
                dve.wait_ge(q_ready, n + 1)
                nc.vector.tensor_scalar(qmin[:, b, :], p_q[:, 0:D], 0.0, None, ALU.min).then_inc(qmin_ready, 1)
                nc.vector.tensor_copy(vext[:, b, :, 0:P], p_kv[b][:, D:2 * D].rearrange("p (m v) -> p m v", m=2))
                wait(dve, row_out[b], use * 16)
                nc.vector.tensor_copy(frow[:, b, 512:520], p_q[:, D:D + 8])
                nc.vector.tensor_copy(k.er[:, bass.ds(n, 1), :].rearrange("p a h -> p (a h)"),
                                      p_q[:, D + 8:D + 16]).then_inc(lr_copied, 1)
                dve.wait_ge(kexp_ready, n + 1)
                nc.vector.scalar_tensor_tensor(kphi[:, b, :], p_kv[b][:, 0:D], 0.0, kexp[:, b, :],
                                               ALU.max, ALU.add).then_inc(kv_ready, 1)
                dve.wait_ge(qexp_ready, n + 1)
                wait(dve, q_out[b], use * 16)
                nc.vector.scalar_tensor_tensor(
                    qt[:, b, :], p_q[:, 0:D], 0.0, qexp[:, b, :], ALU.max, ALU.add).then_inc(q_kept, 1)

            sweep(dve, vec)
            dve.wait_ge(acc_ready, 1)
            c.base, c.n = start, 0
            c(nc.vector.memset(k.cbd[:, :, :], 0.0))
            c(nc.vector.memset(k.kbd[:, :, :], 0.0))
            c.done()
            for m in range(2):
                at = m * (P + 1)
                for h in range(P // MH):
                    r = slice(h * MH, (h + 1) * MH)
                    nc.vector.tensor_copy(k.cbd[r, m, r], p_c[r, at + h * MH:at + (h + 1) * MH])
                    c(nc.vector.tensor_copy(k.kbd[r, m, r], p_c[r, at + P:at + P + 1].to_broadcast([MH, MH])))
            c(nc.vector.tensor_copy(k.hist[:, :], p_h))
            c.done()

        @block.scalar
        def _(act):
            act.wait_ge(mv_ready, 1)
            nc.scalar.activation(sd[:, :], rstd[:, :], ACT.Sqrt).then_inc(rstd_ready, 1)

            def sca(n, b, use):
                act.wait_ge(t_ready, n + 1)
                wait(act, proj_ready, n - 1)
                nc.scalar.copy(xt[:, b, :, :], p_t[b][:, 0:D].rearrange("p (m v) -> p m v", m=2)).then_inc(xt_ready, 1)
                act.wait_ge(kmin_ready, n + 1)
                nc.scalar.activation(kexp[:, b, :], kmin[:, b, :], ACT.Exp).then_inc(kexp_ready, 1)
                act.wait_ge(qmin_ready, n + 1)
                nc.scalar.activation(qexp[:, b, :], qmin[:, b, :], ACT.Exp).then_inc(qexp_ready, 1)
                wait(act, row_out[b], use * 16)
                nc.scalar.copy(frow[:, b, 0:512], p_f[b][:, :]).then_inc(row_copied, 1)
                act.wait_ge(row_copied, n + 1)
                act.wait_ge(lr_copied, n + 1)
                act.dma_start(a["table1"][bass.ds(n * P, P), :], frow[:, b, :]).then_inc(row_out[b], 16)

            sweep(act, sca)
            act.dma_start(a["er1"].rearrange("(n p) h -> p n h", p=P), k.er[:, :, :]).then_inc(er_out, 16)
            act.wait_ge(er_out, 16)
            act.wait_ge(row_out[0], 16 * (NB // 2 + 1))
            act.wait_ge(row_out[1], 16 * (NB // 2))

        @block.tensor
        def _(pe):
            def transposes(n, b):
                pe.wait_ge(xn_ready, n + 1)
                wait(pe, xt_ready, n - 1)
                for m in range(2):
                    last = nc.tensor.transpose(p_t[b][:, m * P:(m + 1) * P], xn[:, b, m * P:(m + 1) * P], k.ident[:, :])
                last.then_inc(t_ready, 1)

            def products(n, b):
                pe.wait_ge(xt_ready, n + 1)
                wait(pe, row_copied, n - 1)
                for kt in range(2):
                    nc.tensor.matmul(p_f[b][:, :], xt[:, b, kt, :], w1[:, kt, :], start=kt == 0, stop=kt == 1)
                wait(pe, kv_ready, n - 1)
                for kt in range(2):
                    last = nc.tensor.matmul(p_kv[b][:, :], xt[:, b, kt, :], wkv[:, kt, :], start=kt == 0, stop=kt == 1)
                last.then_inc(proj_ready, 1)
                wait(pe, q_kept, n)
                wait(pe, lr_copied, n)
                for m in range(2):
                    for kt in range(2):
                        nc.tensor.matmul(p_q[:, m * P:(m + 1) * P], wq[:, kt, m * P:(m + 1) * P], xt[:, b, kt, :],
                                         start=kt == 0, stop=kt == 1)
                for kt in range(2):
                    last = nc.tensor.matmul(p_q[:, D:D + 16], xt[:, b, kt, :], wlr[:, kt, :], start=kt == 0, stop=kt == 1)
                last.then_inc(q_ready, 1)

            def context(n, b):
                pe.wait_ge(kv_ready, n + 1)
                pe.wait_ge(lr_copied, n + 1)
                for m in range(2):
                    last = nc.tensor.matmul(p_c[:, m * (P + 1):(m + 1) * (P + 1)], kphi[:, b, m * P:(m + 1) * P],
                                            vext[:, b, m, :], start=False, stop=False, skip_group_check=True)
                last.then_inc(ctx_added, 1)

            def count(n, b):
                pe.wait_ge(onehot_ready, n + 1)
                for g in range(G):
                    last = nc.tensor.matmul(p_h, oneh[:, b, g, :], onel[:, b, g, :],
                                            start=False, stop=False, skip_group_check=True)
                last.then_inc(counted, 1)

            pe.wait_ge(const_ready, 1)
            pe.wait_ge(wlr_ready, 1)
            pe.wait_ge(loaded, 5 * 16)
            nc.tensor.matmul(p_acc[:, 0:CW + P], zero[:, 0:P], zero[:, :], start=True, stop=False, skip_group_check=True)
            transposes(0, 0)

            def mat(n, b, use):
                if not (isinstance(n, int) and n == NB - 1):
                    transposes(n + 1, 1 - b)
                products(n, b)
                count(n, b)
                if not (isinstance(n, int) and n == 0):
                    context(n - 1, 1 - b)

            sweep(pe, mat)
            context(NB - 1, 0)
            nc.tensor.matmul(p_acc[:, 0:CW + P], zero[:, 0:P], zero[:, :], start=False, stop=True,
                             skip_group_check=True).then_inc(acc_ready, 1)


def scatter_starts(nc, a, k, pool, done):
    for n in range(NB):
        nc.gpsimd.indirect_dma_start(
            out=a["starts"], out_offset=bass.IndirectOffsetOnAxis(ap=k.first[:, n:n + 1], axis=0),
            in_=k.er[:, n, :], in_offset=None, bounds_check=P * T - 1, oob_is_err=False).then_inc(done, 16)
    pool.wait_ge(done, 16 * NB)


def index_pass(nc, a, k):
    with Scope(nc, "at") as s:
        nxt = s.sb("nxt", [P, 1], I32)
        own = s.sb("own", [P, 1])
        own_row = s.sb("own_row", [P, P])
        ones = s.sb("ones", [P, P])
        below = s.sb("below", [NB, NB])
        cum = s.sb("cum", [NB, P])
        lead = s.sb("lead", [NB, 1])
        place = s.sb("place", [NB, 3, P])
        pl = s.sb("pl", [P, 3, NB])
        strip = s.sb("strip", [P, 2, NB])
        cross = s.sb("cross", [P, NB])
        p_s = s.ps("p_s", [P, 512])
        p_r = s.ps("p_r", [P, 512])
        step, nxt_in, nxt_set = s.sem("step"), s.sem("nxt_in"), s.sem("nxt_set")
        sum_asked, summed = s.sem("sum_asked"), s.sem("summed")
        turn_asked, turned = s.sem("turn_asked"), s.sem("turned")
        index_ready, scattered = s.sem("index_ready"), s.sem("scattered")
        block = s.block()

        @block.sync
        def _(sp):
            sp.wait_ge(nxt_set, 1)
            sp.dma_start(nxt[0:P - 1, :], a["dst"][1:P, 0:1],
                         allow_slow_non_contiguous=True).then_inc(nxt_in, 16)

        @block.gpsimd
        def _(pool):
            pool.wait_ge(index_ready, 1)
            scatter_starts(nc, a, k, pool, scattered)

        @block.vector
        def _(dve):
            c = Steps(dve, step)
            nc.vector.memset(nxt[:, :], -1).then_inc(nxt_set, 1)
            c(nc.vector.memset(ones[:, :], 1.0))
            c(nc.vector.tensor_scalar(below[:, :], k.iota[0:NB, 0:NB], k.iop[0:NB, 0:1], None, ALU.is_gt))
            c.done()
            c(nc.vector.tensor_tensor_scan(cum[:, :], ones[0:NB, :], k.hist[:, :], 0.0, ALU.mult, ALU.add))
            c.done()
            c(nc.vector.tensor_copy(own[:, :], k.dst[:, T - 1:T]))
            c(nc.vector.memset(k.same[:, 0:1], 0.0))
            c(nc.vector.tensor_tensor(k.same[:, 1:T], k.dst[:, 1:T], k.dst[:, 0:T - 1], ALU.is_equal))
            c.done()
            c(nc.vector.tensor_scalar(k.restart[:, :], k.same[:, :], -1.0, BIG, ALU.add, ALU.mult))
            nc.vector.tensor_scalar(own_row[:, :], k.ident[:, :], own[:, 0:1], None, ALU.mult).then_inc(sum_asked, 1)
            dve.wait_ge(nxt_in, 16)
            c(nc.vector.tensor_tensor(k.open[:, :], k.dst[:, T - 1:T], nxt[:, :], ALU.is_equal))
            dve.wait_ge(summed, 1)
            c(nc.vector.tensor_scalar(k.group[:, :], p_s[:, 0:P], own[:, 0:1], None, ALU.is_equal))
            c(nc.vector.tensor_copy(lead[:, :], p_s[0:NB, P:P + 1]))
            c.done()
            c(nc.vector.tensor_scalar(cum[:, :], cum[:, :], lead[:, 0:1], None, ALU.add))
            c(nc.vector.tensor_copy(place[:, 0, :], k.hist[:, :]))
            c.done()
            c(nc.vector.tensor_tensor(place[:, 1, :], cum[:, :], k.hist[:, :], ALU.subtract))
            nc.vector.tensor_scalar(place[:, 2, :], cum[:, :], -1.0, None, ALU.add).then_inc(turn_asked, 1)
            dve.wait_ge(turned, 1)
            c(nc.vector.tensor_copy(pl[:, :, :], p_r[:, 0:3 * NB].rearrange("p (a n) -> p a n", a=3)))
            c.done()
            c(nc.vector.tensor_scalar(k.has[:, :], pl[:, 0, :], 1.0, None, ALU.min))
            c.done()
            c(nc.vector.tensor_scalar(cross[:, :], k.has[:, :], -NONE, NONE, ALU.mult, ALU.add))
            c(nc.vector.tensor_tensor(pl[:, 2, :], pl[:, 2, :], k.has[:, :], ALU.mult))
            c.done()
            c(nc.vector.tensor_tensor(k.first[:, :], pl[:, 1, :], cross[:, :], ALU.add))
            c(nc.vector.tensor_copy(k.last[:, :], pl[:, 2, :]))
            c(nc.vector.tensor_scalar(strip[:, :, :], pl[:, 1:3, :], 0.5, 1.0 / T, ALU.add, ALU.mult))
            c.done()
            c(nc.vector.tensor_scalar(strip[:, :, :], strip[:, :, :], -0.5, ROUND, ALU.add, ALU.add))
            c.done()
            c(nc.vector.tensor_scalar(strip[:, :, :], strip[:, :, :], -ROUND, None, ALU.add))
            c.done()
            c(nc.vector.tensor_tensor(cross[:, :], strip[:, 0, :], strip[:, 1, :], ALU.is_lt))
            c.done()
            c(nc.vector.tensor_tensor(cross[:, :], cross[:, :], k.has[:, :], ALU.mult))
            c(nc.vector.tensor_scalar(strip[:, 0, :], strip[:, 0, :], -float(P), None, ALU.add))
            c.done()
            c(nc.vector.tensor_tensor(strip[:, 0, :], strip[:, 0, :], cross[:, :], ALU.mult))
            c.done()
            nc.vector.tensor_scalar(k.tail[:, :], strip[:, 0, :], float(P), None, ALU.add).then_inc(index_ready, 1)

        @block.tensor
        def _(pe):
            pe.wait_ge(sum_asked, 1)
            nc.tensor.matmul(p_s[:, 0:P], ones[:, :], own_row[:, :], start=True, stop=True)
            nc.tensor.matmul(p_s[0:NB, P:P + 1], below[:, :], cum[:, P - 1:P], start=True, stop=True).then_inc(summed, 1)
            pe.wait_ge(turn_asked, 1)
            for i in range(3):
                last = nc.tensor.transpose(p_r[:, i * NB:(i + 1) * NB], place[:, i, :], k.ident[0:NB, 0:NB])
            last.then_inc(turned, 1)


class Attention:

    def __init__(self, nc, a, k, s):
        self.nc, self.a, self.k = nc, a, k
        self.wproj = s.sb("wproj", [P, 2, D])
        self.bproj = s.sb("bproj", [P, D])
        self.q = s.sb("q", [P, 2, D])
        self.x = s.sb("x", [P, 2, D])
        self.xb = s.sb("xb", [P, 2, D])
        self.dmax = s.sb("dmax", [P, 2, D])
        self.att = s.sb("att", [P, 2, 2, P])
        self.res = s.sb("res", [P, 2, D])
        self.p_ad = [s.ps(f"p_ad{i}", [P, 512]) for i in range(2)]
        self.p_o = [s.ps(f"p_o{i}", [P, 512]) for i in range(2)]
        self.loaded, self.step, self.passed = s.sem("mix_loaded"), s.sem("mix_step"), s.sem("mix_passed")
        self.q_in, self.x_in, self.res_out = s.sems("q_in"), s.sems("x_in"), s.sems("res_out")
        self.ad_ready, self.att_ready, self.o_ready = s.sem("ad_ready"), s.sem("att_ready"), s.sem("o_ready")
        self.res_ready, self.x_added = s.sem("res_ready"), s.sem("x_added")

    def load_weights(self, sp):
        a = self.a
        sp.dma_start(self.wproj[:, :, :], a["wproj"].rearrange("(k p) n -> p k n", p=P)).then_inc(self.loaded, 16)
        sp.dma_start(self.bproj[:, :], a["bproj"].to_broadcast([P, D])).then_inc(self.loaded, 16)

    def load(self, sp, n, b):
        at = bass.ds(n * P, P)
        if not isinstance(n, int) or n >= 2:
            wait_apart(sp, self.nc.sync, self.ad_ready, n - 1, self.passed)
            wait_apart(sp, self.nc.sync, self.res_ready, n - 1, self.passed)
        sp.dma_start(self.q[:, b, :], self.a["qt"][at, :]).then_inc(self.q_in[b], 16)
        sp.dma_start(self.x[:, b, :], self.a["x"][at, :]).then_inc(self.x_in[b], 16)

    def store(self, sp, n, b):
        wait_apart(sp, self.nc.sync, self.res_ready, n + 1, self.passed)
        sp.dma_start(self.a["res"][bass.ds(n * P, P), :], self.res[:, b, :]).then_inc(self.res_out[b], 16)

    def stored(self, sp):
        sp.wait_ge(self.res_out[0], 16 * (NB // 2 + 1))
        sp.wait_ge(self.res_out[1], 16 * (NB // 2))

    def quotient(self, dve, n, b, use):
        nc, c = self.nc, Steps(dve, self.step)
        c.base = n * 2
        dve.wait_ge(self.ad_ready, n + 1)
        c(nc.vector.tensor_scalar(self.dmax[:, b, :], self.p_ad[b][:, D:2 * D], 1e-6, None, ALU.max))
        c.done()
        c(nc.vector.reciprocal(self.dmax[:, b, :], self.dmax[:, b, :]))
        c.done()
        nc.vector.tensor_tensor(self.att[:, b, :, :].rearrange("p m v -> p (m v)"), self.p_ad[b][:, 0:D],
                                self.dmax[:, b, :], ALU.mult).then_inc(self.att_ready, 1)

    def residual(self, dve, n, b, use):
        nc = self.nc
        if isinstance(n, int) and n == 0:
            dve.wait_ge(self.loaded, 32)
        dve.wait_ge(self.o_ready, n + 1)
        dve.wait_ge(self.x_in[b], use * 16 + 16)
        wait(dve, self.res_out[b], use * 16)
        nc.vector.tensor_tensor(self.xb[:, b, :], self.p_o[b][:, 0:D], self.x[:, b, :], ALU.add).then_inc(self.x_added, 1)
        dve.wait_ge(self.x_added, n + 1)
        nc.vector.tensor_tensor(self.res[:, b, :], self.xb[:, b, :], self.bproj[:, :], ALU.add).then_inc(self.res_ready, 1)

    def products(self, pe, n, b, use):
        nc, k = self.nc, self.k
        if isinstance(n, int) and n == 0:
            pe.wait_ge(self.loaded, 32)
        pe.wait_ge(self.q_in[b], use * 16 + 16)
        wait(pe, self.att_ready, n - 1)
        for m in range(2):
            q = self.q[:, b, m * P:(m + 1) * P]
            nc.tensor.matmul(self.p_ad[b][:, m * P:(m + 1) * P], k.cbd[:, m, :], q, start=True, stop=True)
            last = nc.tensor.matmul(self.p_ad[b][:, D + m * P:D + (m + 1) * P], k.kbd[:, m, :], q, start=True, stop=True)
        last.then_inc(self.ad_ready, 1)
        pe.wait_ge(self.att_ready, n + 1)
        wait(pe, self.res_ready, n - 1)
        for m in range(2):
            last = nc.tensor.matmul(self.p_o[b][:, 0:D], self.att[:, b, m, :], self.wproj[:, m, :], start=m == 0, stop=m == 1)
        last.then_inc(self.o_ready, 1)


def edge_pass(nc, a, k, L):
    H, W, R, dim, AH = L.heads, L.width, L.row, L.dim, L.act_heads
    i_ = L.name[1]
    table, er_table, sums, tails = a["table" + i_], a["er" + i_], a["sums" + i_], a["tails" + i_]
    G1 = G + 1
    with Scope(nc, "e" + i_) as s:
        er = s.sb("er", [P, T, 8])
        er0 = s.sb("er0", [P, 8])
        idx = s.sb("idx", [P, 2, G], I32)
        rows = s.sb("rows", [P, 2, G, L.table])
        ring = s.sb("ring", [P, 2, 9, R])
        z = s.sb("z", [P, H, G])
        eext = s.sb("eext", [P, H, G1])
        rflat = s.sb("rflat", [P, H * G1 + 1])
        rext = rflat[:, 0:H * G1].rearrange("p (h j) -> p h j", h=H)
        kext = s.sb("kext", [P, H, G1])
        fext = s.sb("fext", [P, H, G1])
        mext = s.sb("mext", [P, 2, H, G1])
        d = s.sb("d", [P, H, G1])
        wr = s.sb("wr", [P, 2, H, G1])
        dext = s.sb("dext", [P, 2, H, G1])
        om = s.sb("om", [P, 1])
        pen = s.sb("pen", [P, P])
        mm = s.sb("mm", [P, H])
        diag = s.sb("diag", [P, H, P])
        cand = s.sb("cand", [P, H, P])
        gm = s.sb("gm", [P, H])
        ts = s.sb("ts", [P, R])
        sc = s.sb("sc", [P, 2, H])
        tl = s.sb("tl", [P, R])
        none = s.sb("none", [1, R])
        ones = s.sb("ones", [P, P])
        p_m = [s.ps(f"p_m{i}", [P, 512]) for i in range(2)]
        p_t = s.ps("p_t", [P, 512])
        p_d = s.ps("p_d", [P, 512])
        er_in, er0_in, step, er_ready = s.sem("er_in"), s.sem("er0_in"), s.sem("step"), s.sem("er_ready")
        idx_ready, rows_in = s.sem("idx_ready"), s.sems("rows_in")
        passed, passed_sp, d_ready, wr_ready = s.sem("passed"), s.sem("passed_sp"), s.sem("d_ready"), s.sem("wr_ready")
        scaled, summed = s.sem("scaled"), s.sem("summed")
        dm_ready, den_ready = s.sems("dm_ready"), s.sem("den_ready")
        stored = s.sems("stored")
        max_asked, max_spread = s.sem("max_asked"), s.sem("max_spread")
        exp_asked, exp_done = s.sem("exp_asked"), s.sem("exp_done")
        tail_asked, tail_summed = s.sem("tail_asked"), s.sem("tail_summed")
        tail_ready, tail_out = s.sem("tail_ready"), s.sem("tail_out")
        mix = Attention(nc, a, k, s) if L is L2 else None
        block = s.block()

        @block.sync
        def _(sp):
            sp.dma_start(er[:, :, :], a["starts"].rearrange("(p t) h -> p t h", p=P)).then_inc(er_in, 16)
            out = sums.rearrange("(p t) r -> p t r", p=P)

            if mix:
                mix.load_weights(sp)
                mix.load(sp, 0, 0)

            def store(n, b, use):
                if mix and not (isinstance(n, int) and n == NB - 1):
                    mix.load(sp, n + 1, 1 - b)
                for i, (c0, c1) in enumerate(HALVES):
                    wait_apart(sp, nc.sync, summed, n * G + c1, passed_sp)
                    wait_apart(sp, nc.sync, dm_ready[i], n + 1, passed_sp)
                    sp.dma_start(out[:, bass.ds(n * G + c0, c1 - c0), :], ring[:, i, 0:c1 - c0, :]).then_inc(stored[i], 16)
                if mix:
                    mix.store(sp, n, b)

            sweep(sp, store)
            if mix:
                mix.stored(sp)
            sp.wait_ge(tail_ready, 1)
            sp.dma_start(tails[0:P, :], tl[:, :]).then_inc(tail_out, 16)
            sp.dma_start(tails[P:P + 1, :], none[:, :]).then_inc(tail_out, 16)
            sp.wait_ge(tail_out, 32)
            sp.wait_ge(stored[0], 16 * NB)
            sp.wait_ge(stored[1], 16 * NB)

        @block.gpsimd
        def _(pool):
            nc.gpsimd.indirect_dma_start(out=er0[:, :], out_offset=None, in_=er_table,
                                         in_offset=bass.IndirectOffsetOnAxis(ap=k.dst[:, 0:1], axis=0)).then_inc(er0_in, 16)

            def gather(n, b, use):
                wait(pool, summed, (n - 1) * G)
                nc.gpsimd.sem_inc(passed)
                nc.gpsimd.tensor_copy(idx[:, b, :], k.src[:, bass.ds(n * G, G)]).then_inc(idx_ready, 1)
                pool.wait_ge(idx_ready, n + 1)
                nc.gpsimd.sem_inc(passed)
                for g in range(G):
                    nc.gpsimd.indirect_dma_start(out=rows[:, b, g, :], out_offset=None, in_=table,
                                                 in_offset=bass.IndirectOffsetOnAxis(ap=idx[:, b, g:g + 1], axis=0)
                                                 ).then_inc(rows_in[b], 16)

            sweep(pool, gather)

        @block.vector
        def _(dve):
            c = Steps(dve, step)
            c(nc.vector.memset(ring[:, :, :, :], 0.0))
            c(nc.vector.memset(mext[:, 1, :, G:G1], -BIG))
            c(nc.vector.memset(dext[:, 1, :, G:G1], 0.0))
            c(nc.vector.memset(rflat[:, :], -BIG))
            c(nc.vector.memset(kext[:, :, 0:1], 0.0))
            c(nc.vector.memset(kext[:, :, 1:2], 1.0))
            c(nc.vector.memset(ones[:, :], 1.0))
            c(nc.vector.memset(none[:, :], 0.0))
            c.done()
            c(nc.vector.memset(none[:, L.max:R], -BIG))
            dve.wait_ge(er_in, 16)
            dve.wait_ge(er0_in, 16)
            c(nc.vector.tensor_copy(er[:, 0, 0:H], er0[:, 0:H]))
            c.done()
            for h in range(H):
                c(nc.vector.tensor_tensor_scan(er[:, :, h], k.same[:, :], er[:, :, h], 0.0, ALU.mult, ALU.add))
            c.done()
            nc.vector.memset(om[:, :], 0.0).then_inc(er_ready, 1)
            start = c.n

            per = 11 if AH < H else 10
            flat = "p h j -> p (h j)"

            def batch(n, b, use):
                c.block(n, per)
                c.base = n * per + start
                dve.wait_ge(rows_in[b], use * (16 * G) + 16 * G)
                c(nc.vector.tensor_tensor(z[:, :, :], rows[:, b, :, W:W + H].rearrange("p j h -> p h j"),
                                          er[:, bass.ds(n * G, G), 0:H].rearrange("p j h -> p h j"), ALU.add))
                c(nc.vector.tensor_copy(eext[:, :, 0:1], mext[:, 1 - b, :, G:G1]))
                c(nc.vector.tensor_copy(rext[:, :, 1:G1],
                                        k.restart[:, bass.ds(n * G, G)].unsqueeze(1).to_broadcast([P, H, G])))
                c.done()
                c(nc.vector.scalar_tensor_tensor(eext[:, :, 1:G1], z[:, :, :], 0.2, z[:, :, :], ALU.mult, ALU.max))
                c.done()
                c(nc.vector.tensor_tensor_scan(fext[:, :, :].rearrange(flat), rflat[:, 0:H * G1],
                                               eext[:, :, :].rearrange(flat), 0.0, ALU.add, ALU.max))
                c.done()
                wait(dve, dm_ready[1], n - 1)
                c(nc.vector.tensor_tensor_scan(mext[:, b, :, :].rearrange(flat)[:, ::-1], rflat[:, 1:H * G1 + 1][:, ::-1],
                                               fext[:, :, :].rearrange(flat)[:, ::-1], 0.0, ALU.add, ALU.max))
                c(nc.vector.tensor_tensor(eext[:, :, 0:1], eext[:, :, 0:1], rext[:, :, 1:2], ALU.add))
                c.done()
                wait(dve, wr_ready, n)
                nc.vector.tensor_tensor(d[:, :, 0:1], eext[:, :, 0:1], mext[:, b, :, 1:2], ALU.subtract)
                nc.vector.tensor_tensor(d[:, :, 1:G1], eext[:, :, 1:G1], mext[:, b, :, 1:G1], ALU.subtract).then_inc(d_ready, 1)
                dve.wait_ge(wr_ready, n + 1)
                if AH < H:
                    v = rows[:, b, :, AH * dim:W].rearrange("p j (h e) -> p j h e", h=H - AH)
                    c(nc.vector.tensor_tensor(v, v, broad(wr[:, b, AH:H, 1:G1].rearrange("p h j -> p j h"), dim), ALU.mult))
                wait(dve, stored[0], n * 16)
                wait(dve, summed, n * G)
                c(nc.vector.tensor_copy(kext[:, :, 2:G1],
                                        k.same[:, bass.ds(n * G + 1, G - 1)].unsqueeze(1).to_broadcast([P, H, G - 1])))
                by_head = "p (h e) -> p h e"
                c(nc.vector.tensor_tensor(ring[:, 0, 0, 0:W].rearrange(by_head, h=H),
                                          ring[:, 1, LENGTH[1] - 1, 0:W].rearrange(by_head, h=H),
                                          broad(wr[:, b, :, 0], dim), ALU.mult))
                wait(dve, den_ready, n)
                c.done()
                c(nc.vector.tensor_tensor(wr[:, b, :, 0:1], wr[:, b, :, 0:1], dext[:, 1 - b, :, G:G1], ALU.mult))
                dve.wait_ge(scaled, n * G + 1)
                nc.vector.tensor_tensor(ring[:, 0, 0, 0:W], ring[:, 0, 0, 0:W], rows[:, b, 0, 0:W], ALU.add).then_inc(summed, 1)
                c.done()
                nc.vector.tensor_tensor_scan(dext[:, b, :, :].rearrange(flat), kext[:, :, :].rearrange(flat),
                                             wr[:, b, :, :].rearrange(flat), 0.0, ALU.mult, ALU.add).then_inc(den_ready, 1)
                for i, (c0, c1) in enumerate(HALVES):
                    if i == 1:
                        wait(dve, stored[1], n * 16)
                    for j in range(max(c0, 1), c1):
                        if mix and j == 3:
                            mix.quotient(dve, n, b, use)
                        if mix and j == 12:
                            mix.residual(dve, n, b, use)
                        prev = ring[:, i, j - c0 - 1, 0:W] if j > c0 else ring[:, 1 - i, LENGTH[1 - i] - 1, 0:W]
                        dve.wait_ge(scaled, n * G + (j + 1))
                        dve.wait_ge(summed, n * G + j)
                        nc.vector.scalar_tensor_tensor(ring[:, i, j - c0, 0:W], prev, kext[:, 0, j + 1:j + 2],
                                                       rows[:, b, j, 0:W], ALU.mult, ALU.add).then_inc(summed, 1)
                c.end()

            sweep(dve, batch)
            c.base, c.n = NB * per + start, 0
            final = ring[:, 1, LENGTH[1] - 1, :]
            dve.wait_ge(dm_ready[1], NB)
            dve.wait_ge(summed, T)
            c(nc.vector.tensor_scalar(om[:, :], k.open[:, :], -1.0, BIG, ALU.add, ALU.mult))
            c(nc.vector.tensor_scalar(pen[:, :], k.group[:, :], -1.0, BIG, ALU.add, ALU.mult))
            c.done()
            c(nc.vector.tensor_scalar(mm[:, :], final[:, L.max:R], om[:, 0:1], None, ALU.add))
            c.done()
            for h in range(H):
                last = nc.vector.tensor_scalar(diag[:, h, :], k.ident[:, :], mm[:, h:h + 1], None, ALU.mult)
            last.then_inc(max_asked, 1)
            dve.wait_ge(max_spread, 1)
            for h in range(H):
                c(nc.vector.tensor_tensor(cand[:, h, :], p_m[h // 4][:, h % 4 * P:(h % 4 + 1) * P], pen[:, :], ALU.add))
            c.done()
            c(nc.vector.tensor_reduce(gm[:, :], cand[:, :, :], AX.X, ALU.max))
            c.done()
            nc.vector.tensor_tensor(sc[:, 0, :], mm[:, :], gm[:, :], ALU.subtract).then_inc(exp_asked, 1)
            dve.wait_ge(exp_done, 1)
            c(nc.vector.tensor_scalar(sc[:, 1, :], sc[:, 1, :], k.open[:, 0:1], None, ALU.mult))
            c.done()
            nc.vector.tensor_tensor(ts[:, 0:W].rearrange("p (h e) -> p h e", h=H),
                                    final[:, 0:W].rearrange("p (h e) -> p h e", h=H), broad(sc[:, 1, :], dim), ALU.mult)
            nc.vector.tensor_tensor(ts[:, W:W + H], final[:, W:W + H], sc[:, 1, :], ALU.mult).then_inc(tail_asked, 1)
            dve.wait_ge(tail_summed, 1)
            nc.vector.tensor_copy(tl[:, 0:W], p_t[:, 0:W])
            nc.vector.tensor_copy(tl[:, W:W + H], p_d[:, 0:H])
            nc.vector.tensor_copy(tl[:, L.max:R], gm[:, :]).then_inc(tail_ready, 1)

        @block.scalar
        def _(act):
            def weights(n, b, use):
                act.wait_ge(d_ready, n + 1)
                wait(act, summed, (n - 1) * G)
                nc.scalar.activation(wr[:, b, :, :].rearrange("p h j -> p (h j)"),
                                     d[:, :, :].rearrange("p h j -> p (h j)"), ACT.Exp).then_inc(wr_ready, 1)
                act.wait_ge(wr_ready, n + 1)
                for i, (c0, c1) in enumerate(HALVES):
                    for j in range(c0, c1):
                        for h in range(AH):
                            at = slice(h * dim, (h + 1) * dim)
                            last = nc.scalar.activation(rows[:, b, j, at], rows[:, b, j, at], ACT.Copy,
                                                        scale=wr[:, b, h, j + 1:j + 2])
                        last.then_inc(scaled, 1)
                    act.wait_ge(den_ready, n + 1)
                    wait(act, stored[i], n * 16)
                    nc.scalar.copy(ring[:, i, 0:c1 - c0, W:W + H], dext[:, b, :, 1 + c0:1 + c1].rearrange("p h j -> p j h"))
                    nc.scalar.copy(ring[:, i, 0:c1 - c0, L.max:R],
                                   mext[:, b, :, 1 + c0:1 + c1].rearrange("p h j -> p j h")).then_inc(dm_ready[i], 1)

            act.wait_ge(er_ready, 1)
            sweep(act, weights)
            act.wait_ge(exp_asked, 1)
            nc.scalar.activation(sc[:, 1, :], sc[:, 0, :], ACT.Exp).then_inc(exp_done, 1)

        @block.tensor
        def _(pe):
            if mix:
                sweep(pe, lambda n, b, use: mix.products(pe, n, b, use))
            pe.wait_ge(max_asked, 1)
            for i in range((H + 3) // 4):
                w = min(4, H) * P
                last = nc.tensor.matmul(p_m[i][:, 0:w], ones[:, :], diag[:, 4 * i:min(4 * i + 4, H), :].rearrange("p h v -> p (h v)"),
                                        start=True, stop=True)
            last.then_inc(max_spread, 1)
            pe.wait_ge(tail_asked, 1)
            nc.tensor.matmul(p_t[:, 0:W], k.group[:, :], ts[:, 0:W], start=True, stop=True)
            nc.tensor.matmul(p_d[:, 0:H], k.group[:, :], ts[:, W:W + H], start=True, stop=True).then_inc(tail_summed, 1)


def join_maxima(nc, c, L, rows, m, d):
    c(nc.vector.tensor_tensor(m, rows[:, 0, L.max:L.row], rows[:, 1, L.max:L.row], ALU.max))
    c.done()
    return nc.vector.tensor_tensor(d, rows[:, :, L.max:L.row], m.unsqueeze(1).to_broadcast([P, 2, L.heads]), ALU.subtract)


JOIN_STEPS = 7


def join_sums(nc, c, L, rows, s, q, rec, has, out):
    H, W = L.heads, L.width
    c(nc.vector.tensor_tensor(q, rows[:, :, W:W + H], s, ALU.mult))
    c.done()
    c(nc.vector.tensor_tensor(rec, q[:, 0, :], q[:, 1, :], ALU.add))
    c.done()
    c(nc.vector.reciprocal(rec, rec))
    c.done()
    c(nc.vector.tensor_scalar(rec, rec, has, None, ALU.mult))
    c.done()
    c(nc.vector.tensor_tensor(q, s, rec.unsqueeze(1).to_broadcast([P, 2, H]), ALU.mult))
    c.done()
    for i in range(2):
        v = rows[:, i, 0:W].rearrange("p (h e) -> p h e", h=H)
        c(nc.vector.tensor_tensor(v, v, broad(q[:, i, :], L.dim), ALU.mult))
    c.done()
    return nc.vector.tensor_tensor(out, rows[:, 0, 0:W], rows[:, 1, 0:W], ALU.add)


def hidden_pass(nc, a, k):
    L = L1
    with Scope(nc, "hi") as s:
        w2 = s.sb("w2", [P, 4, D])
        alr = s.sb("alr", [P, 2, D])
        prod = s.sb("prod", [P, 4, D])
        wlr = s.sb("wlr", [P, 4, 16])
        rows = s.sb("rows", [P, 2 * GB, 2, L.row])
        m = s.sb("m", [P, GB, 8])
        d = s.sb("d", [P, GB, 2, 8])
        sc = s.sb("sc", [P, 2, GB, 2, 8])
        q = s.sb("q", [P, 2, GB, 2, 8])
        rec = s.sb("rec", [P, GB, 8])
        agg = s.sb("agg", [P, 2, 512])
        pos = s.sb("pos", [P, 2, 512])
        neg = s.sb("neg", [P, 2, 512])
        ex = s.sb("ex", [P, 2, 512])
        hid = s.sb("hid", [P, 2, 512])
        ht = s.sb("ht", [P, 2, 4, P])
        frow = s.sb("frow", [P, 2, L2.table])
        p_t = [s.ps(f"p_t{i}", [P, 512]) for i in range(2)]
        p_f = [s.ps(f"p_f{i}", [P, 512]) for i in range(2)]
        loaded, step, wlr_ready = s.sem("loaded"), s.sem("step"), s.sem("wlr_ready")
        rows_in, d_ready, sc_ready = s.sems("rows_in", 2 * GB), s.sem("d_ready"), s.sem("sc_ready")
        agg_ready, neg_ready, pos_ready, ex_ready = s.sem("agg_ready"), s.sem("neg_ready"), s.sem("pos_ready"), s.sem("ex_ready")
        hid_ready, t_ready, ht_ready, f_ready = s.sem("hid_ready"), s.sem("t_ready"), s.sem("ht_ready"), s.sem("f_ready")
        er_kept, row_copied, row_out, er_out = s.sem("er_kept"), s.sem("row_copied"), s.sems("row_out"), s.sem("er_out")
        scattered, step1, step2 = s.sem("scattered"), s.sem("step1"), s.sem("step2")
        block = s.block()

        @block.sync
        def _(sp):
            sp.dma_start(w2[:, :, :], a["w2"].rearrange("(k p) n -> p k n", p=P)).then_inc(loaded, 16)
            sp.dma_start(alr[:, 0, :], a["al2"].to_broadcast([P, D])).then_inc(loaded, 16)
            sp.dma_start(alr[:, 1, :], a["ar2"].to_broadcast([P, D])).then_inc(loaded, 16)

        def scatter(pool, n):
            pool.wait_ge(er_kept, n + 1)
            nc.gpsimd.indirect_dma_start(
                out=a["starts"], out_offset=bass.IndirectOffsetOnAxis(ap=k.first[:, n:n + 1], axis=0),
                in_=k.er[:, n, :], in_offset=None, bounds_check=P * T - 1, oob_is_err=False).then_inc(scattered, 16)

        @block.gpsimd
        def _(pool):
            for n in range(NB):
                b = n % (2 * GB)
                wait(pool, agg_ready, n - 2 * GB + 1)
                for i, (at, src) in enumerate([(k.last, a["sums1"]), (k.tail, a["tails1"])]):
                    nc.gpsimd.indirect_dma_start(out=rows[:, b, i, :], out_offset=None, in_=src,
                                                 in_offset=bass.IndirectOffsetOnAxis(ap=at[:, n:n + 1], axis=0)
                                                 ).then_inc(rows_in[b], 16)
                if n >= 2 * GB:
                    scatter(pool, n - 2 * GB)
            for n in range(NB - 2 * GB, NB):
                scatter(pool, n)
            pool.wait_ge(scattered, 16 * NB)

        @block.vector
        def _(dve):
            c, c1, c2 = Steps(dve, step), Steps(dve, step1), Steps(dve, step2)
            c(nc.vector.memset(wlr[:, :, :], 0.0))
            c.done()
            dve.wait_ge(loaded, 48)
            for lr in range(2):
                c(nc.vector.tensor_tensor(prod[:, :, :], w2[:, :, :], alr[:, lr:lr + 1, :].to_broadcast([P, 4, D]), ALU.mult))
                c.done()
                last = c(nc.vector.tensor_reduce(wlr[:, :, 8 * lr:8 * lr + 1], prod[:, :, :], AX.X, ALU.add))
                c.done()
            nc.vector.memset(prod[:, 0, 0:1], 0.0).then_inc(wlr_ready, 1)

            def shares(g, gb):
                c1.block(g, 6)
                at = rows[:, gb * GB:(gb + 1) * GB, :, :]
                for i in range(GB):
                    if not isinstance(g, int):
                        dve.wait_ge(rows_in[gb * GB + i], (g - gb) * 16 + 32)
                    else:
                        dve.wait_ge(rows_in[gb * GB + i], g // 2 * 32 + 32)
                c1(nc.vector.tensor_tensor(m[:, :, :], at[:, :, 0, L.max:L.row], at[:, :, 1, L.max:L.row], ALU.max))
                c1.done()
                wait(dve, sc_ready, g)
                nc.vector.tensor_tensor(d[:, :, :, :], at[:, :, :, L.max:L.row],
                                        m[:, :, :].unsqueeze(2).to_broadcast([P, GB, 2, 8]), ALU.subtract).then_inc(d_ready, 1)
                dve.wait_ge(sc_ready, g + 1)
                c1(nc.vector.tensor_tensor(q[:, gb, :, :, :], at[:, :, :, L.den:L.max], sc[:, gb, :, :, :], ALU.mult))
                c1.done()
                c1(nc.vector.tensor_tensor(rec[:, :, :], q[:, gb, :, 0, :], q[:, gb, :, 1, :], ALU.add))
                c1.done()
                c1(nc.vector.reciprocal(rec[:, :, :], rec[:, :, :]))
                c1.done()
                c1(nc.vector.tensor_tensor(rec[:, :, :], rec[:, :, :], broad(k.has[:, bass.ds(g * GB, GB)], 8), ALU.mult))
                c1.done()
                c1(nc.vector.tensor_tensor(q[:, gb, :, :, :], sc[:, gb, :, :, :],
                                           rec[:, :, :].unsqueeze(2).to_broadcast([P, GB, 2, 8]), ALU.mult))
                c1.done()
                c1.end()

            def elu(n, b):
                dve.wait_ge(ex_ready, n + 1)
                wait(dve, t_ready, n - 1)
                nc.vector.scalar_tensor_tensor(hid[:, b, :], ex[:, b, :], -1.0, pos[:, b, :], ALU.add,
                                               ALU.add).then_inc(hid_ready, 1)

            def main(g, gb, gu, more):
                for i in range(GB):
                    n, b = g * GB + i, (gb + i) % 2
                    at = rows[:, gb * GB + i, :, :]
                    for j in range(2):
                        v = at[:, j, 0:512].rearrange("p (h e) -> p h e", h=8)
                        last = nc.vector.tensor_tensor(v, v, broad(q[:, gb, i, j, :], L.dim), ALU.mult)
                    last.then_inc(step2, 1)
                    dve.wait_ge(step2, n + 1)
                    wait(dve, ex_ready, n - 1)
                    nc.vector.tensor_tensor(agg[:, b, :], at[:, 0, 0:512], at[:, 1, 0:512], ALU.add).then_inc(agg_ready, 1)
                    if not (isinstance(n, int) and n == 0):
                        elu(n - 1, 1 - b)
                    dve.wait_ge(agg_ready, n + 1)
                    nc.vector.tensor_scalar(neg[:, b, :], agg[:, b, :], 0.0, None, ALU.min).then_inc(neg_ready, 1)
                    if more and i == 5:
                        shares(g + 1, 1 - gb)

            groups(dve, lambda: shares(0, 0), main)
            elu(NB - 1, 0)

        @block.scalar
        def _(act):
            def exponents(g, gb):
                act.wait_ge(d_ready, g + 1)
                wait(act, agg_ready, (g - 1) * GB)
                nc.scalar.activation(sc[:, gb, :, :, :], d[:, :, :, :], ACT.Exp).then_inc(sc_ready, 1)

            def out(n, b, use):
                act.wait_ge(t_ready, n + 1)
                wait(act, f_ready, n - 1)
                nc.scalar.copy(ht[:, b, :, :].rearrange("p k v -> p (k v)"), p_t[b][:, :]).then_inc(ht_ready, 1)
                act.wait_ge(f_ready, n + 1)
                wait(act, row_out[b], use * 16)
                nc.scalar.copy(frow[:, b, :], p_f[b][:, 0:L2.table]).then_inc(row_copied, 1)
                nc.scalar.copy(k.er[:, bass.ds(n, 1), :].rearrange("p a h -> p (a h)"),
                               p_f[b][:, D + 8:D + 16]).then_inc(er_kept, 1)
                act.wait_ge(row_copied, n + 1)
                act.dma_start(a["table2"][bass.ds(n * P, P), :], frow[:, b, :]).then_inc(row_out[b], 16)

            def main(g, gb, gu, more):
                for i in range(GB):
                    n, b = g * GB + i, (gb + i) % 2
                    act.wait_ge(agg_ready, n + 1)
                    wait(act, hid_ready, n - 1)
                    nc.scalar.activation(pos[:, b, :], agg[:, b, :], ACT.Relu)
                    act.wait_ge(neg_ready, n + 1)
                    nc.scalar.activation(ex[:, b, :], neg[:, b, :], ACT.Exp).then_inc(ex_ready, 1)
                    if more and i == 5:
                        exponents(g + 1, 1 - gb)
                    if not (isinstance(n, int) and n == 0):
                        out(n - 1, 1 - b, gu * GB + (gb * GB + i - 1) // 2)

            groups(act, lambda: exponents(0, 0), main)
            out(NB - 1, 0, NB // 2)
            act.wait_ge(er_kept, NB)
            act.dma_start(a["er2"].rearrange("(n p) h -> p n h", p=P), k.er[:, :, :]).then_inc(er_out, 16)
            act.wait_ge(er_out, 16)
            act.wait_ge(row_out[0], 16 * (NB // 2 + 1))
            act.wait_ge(row_out[1], 16 * (NB // 2))

        @block.tensor
        def _(pe):
            pe.wait_ge(loaded, 48)
            pe.wait_ge(wlr_ready, 1)

            def mat(n, b, use):
                pe.wait_ge(hid_ready, n + 1)
                wait(pe, ht_ready, n - 1)
                for kt in range(4):
                    last = nc.tensor.transpose(p_t[b][:, kt * P:(kt + 1) * P], hid[:, b, kt * P:(kt + 1) * P], k.ident[:, :])
                last.then_inc(t_ready, 1)
                pe.wait_ge(ht_ready, n + 1)
                wait(pe, er_kept, n - 1)
                for kt in range(4):
                    nc.tensor.matmul(p_f[b][:, 0:D], ht[:, b, kt, :], w2[:, kt, :], start=kt == 0, stop=kt == 3)
                for kt in range(4):
                    last = nc.tensor.matmul(p_f[b][:, D:D + 16], ht[:, b, kt, :], wlr[:, kt, :], start=kt == 0, stop=kt == 3)
                last.then_inc(f_ready, 1)

            sweep(pe, mat)


def final_pass(nc, a, k):
    L = L2
    GR = NB // GB
    FILLS = 9 * 4
    with Scope(nc, "fi") as s:
        wf = [s.sb(f"wf{i}", [P, E, 2, D]) for i in range(3)]
        bn = s.sb("bn", [P, 10, E * 2])
        scale = s.sb("scale", [P, 2, E * 2])
        shift = s.sb("shift", [P, 2, E * 2])
        wr = s.sb("wr", [P, 2, E])
        br = s.sb("br", [P, E])
        bo = s.sb("bo", [E, D])
        rows = s.sb("rows", [P, GB, 2, L.row])
        m = s.sb("m", [P, GB, 1])
        d = s.sb("d", [P, GB, 2, 1])
        sc = s.sb("sc", [P, GB, 2, 1])
        q = s.sb("q", [P, GB, 2, 1])
        rec = s.sb("rec", [P, GB, 1])
        agg = s.sb("agg", [P, GB, D])
        res = s.sb("res", [P, GB, D])
        y = s.sb("y", [P, 2, GB, D])
        stats = s.sb("stats", [P, GB, 6])
        mv = s.sb("mv", [P, GB, 2])
        var = s.sb("var", [P, GB])
        sd = s.sb("sd", [P, GB])
        rstd = s.sb("rstd", [P, GB])
        xn = s.sb("xn", [P, GB, D])
        xt = s.sb("xt", [P, 2, 2, GB * P])
        lg = s.sb("lg", [P, GB, E])
        top = s.sb("top", [P, GB])
        lge = s.sb("lge", [P, GB, E])
        tot = s.sb("tot", [P, GB])
        w = s.sb("w", [P, 2, GB, E])
        wt = s.sb("wt", [E, 2, GB * P])
        h1 = s.sb("h1", [P, 2, GB * P])
        h2 = s.sb("h2", [P, 2, GB * P])
        p_h = [s.ps(f"p_h{i}", [P, 512]) for i in range(4)]
        p_y = [s.ps(f"p_y{i}", [P, 512]) for i in range(2)]
        p_t = [s.ps(f"p_t{i}", [P, 512]) for i in range(2)]
        loaded, bn_in, step, bn_ready = s.sem("loaded"), s.sem("bn_in"), s.sem("step"), s.sem("bn_ready")
        sd_asked, sd_done, passed = s.sem("sd_asked"), s.sem("sd_done"), s.sem("passed")
        rows_in, res_in, joined = s.sems("rows_in", GB), s.sem("res_in"), s.sem("joined")
        d_ready, sc_ready, x_ready = s.sem("d_ready"), s.sem("sc_ready"), s.sem("x_ready")
        xn_ready, t_ready, xt_ready = s.sem("xn_ready"), s.sem("t_ready"), s.sem("xt_ready")
        gate_ready, lg_ready, lge_ready = s.sem("gate_ready"), s.sem("lg_ready"), s.sem("lge_ready")
        w_ready, wt_turned, wt_ready = s.sem("w_ready"), s.sem("wt_turned"), s.sem("wt_ready")
        h_filled, h_kept = s.sem("h_filled"), s.sem("h_kept")
        y_filled, y_added, y_out = s.sem("y_filled"), s.sem("y_added"), s.sems("y_out")
        block = s.block()

        @block.sync
        def _(sp):
            def load(g, b, use):
                sp.dma_start(res[:, :, :], a["res"][bass.ds(g * (GB * P), GB * P), :].rearrange("(n p) d -> p n d", p=P)
                             ).then_inc(res_in, 16)

            def first():
                load(0, 0, 0)
                for i, name in enumerate(("b1", "g1", "be1", "m1", "v1", "b2", "g2", "be2", "m2", "v2")):
                    sp.dma_start(bn[:, i, :], a[name].rearrange("p e k -> p (e k)")).then_inc(bn_in, 16)
                for i, name in enumerate(("f1", "f2", "fo")):
                    sp.dma_start(wf[i][:, :, :, :], a[name].rearrange("e (k p) n -> p e k n", p=P)).then_inc(loaded, 16)
                sp.dma_start(wr[:, :, :], a["wr"].rearrange("(k p) n -> p k n", p=P)).then_inc(loaded, 16)
                sp.dma_start(br[:, :], a["br"].to_broadcast([P, E])).then_inc(loaded, 16)
                sp.dma_start(bo[:, :], a["bo"]).then_inc(loaded, 16)

            def main(g, b, use, more):
                if more:
                    wait_apart(sp, nc.sync, x_ready, g + 1, passed)
                    load(g + 1, 1 - b, use + b)
                wait_apart(sp, nc.sync, y_added, (g + 1) * FILLS, passed)
                sp.dma_start(a["out"][bass.ds(g * (GB * P), GB * P), :].rearrange("(n p) d -> p n d", p=P),
                             y[:, b, :, :]).then_inc(y_out[b], 16)

            groups(sp, first, main)
            sp.wait_ge(y_out[0], 16 * (GR // 2 + 1))
            sp.wait_ge(y_out[1], 16 * (GR // 2))

        @block.gpsimd
        def _(pool):
            for n in range(NB):
                wait(pool, joined, n - GB + 1)
                for i, (at, src) in enumerate([(k.last, a["sums2"]), (k.tail, a["tails2"])]):
                    nc.gpsimd.indirect_dma_start(out=rows[:, n % GB, i, :], out_offset=None, in_=src,
                                                 in_offset=bass.IndirectOffsetOnAxis(ap=at[:, n:n + 1], axis=0)
                                                 ).then_inc(rows_in[n % GB], 16)

        @block.vector
        def _(dve):
            c = Steps(dve, step, passed)
            dve.wait_ge(bn_in, 160)
            for i in range(2):
                last = nc.vector.tensor_scalar(shift[:, i, :], bn[:, 5 * i + 4, :], 1e-3, None, ALU.add)
            last.then_inc(sd_asked, 1)
            dve.wait_ge(sd_done, 1)
            c(nc.vector.reciprocal(scale[:, :, :], scale[:, :, :]))
            c.done()
            for i in range(2):
                c(nc.vector.tensor_tensor(scale[:, i, :], scale[:, i, :], bn[:, 5 * i + 1, :], ALU.mult))
                c(nc.vector.tensor_tensor(shift[:, i, :], bn[:, 5 * i, :], bn[:, 5 * i + 3, :], ALU.subtract))
            c.done()
            for i in range(2):
                c(nc.vector.tensor_tensor(shift[:, i, :], shift[:, i, :], scale[:, i, :], ALU.mult))
            c.done()
            for i in range(2):
                last = nc.vector.tensor_tensor(shift[:, i, :], shift[:, i, :], bn[:, 5 * i + 2, :], ALU.add)
            last.then_inc(bn_ready, 1)
            dve.wait_ge(loaded, 96)
            start = c.n
            PER = GB * (1 + JOIN_STEPS + 1 + 1 + 1) - 1 + 1 + 4

            def maxima(g):
                for i in range(GB):
                    dve.wait_ge(rows_in[i], g * 32 + 32)
                    join_maxima(nc, c, L, rows[:, i, :, :], m[:, i, :], d[:, i, :, :]).then_inc(d_ready, 1)

            def sums(g, b, use, blocks):
                for i in blocks:
                    dve.wait_ge(sc_ready, g * GB + (i + 1))
                    join_sums(nc, c, L, rows[:, i, :, :], sc[:, i, :, :], q[:, i, :, :], rec[:, i, :],
                              k.has[:, bass.ds(g * GB + i, 1)], agg[:, i, :]).then_inc(joined, 1)
                    dve.wait_ge(joined, g * GB + (i + 1))
                    if i == 0:
                        dve.wait_ge(res_in, g * 16 + 16)
                        wait(dve, y_out[b], use * 16)
                    c(nc.vector.tensor_tensor(y[:, b, i, :], agg[:, i, :], res[:, i, :], ALU.add))
                    c.done()
                    ins = nc.vector.bn_stats(stats[:, i, :], y[:, b, i, :])
                    if i < GB - 1:
                        c(ins)
                    else:
                        ins.then_inc(x_ready, 1)

            def spread(g):
                dve.wait_ge(x_ready, g + 1)
                nc.vector.sem_inc(passed)
                for i in range(GB):
                    c(nc.vector.bn_aggr(mv[:, i, :], stats[:, i, :]))
                c.done()
                nc.vector.tensor_scalar(var[:, :], mv[:, :, 1], 1e-5, None, ALU.add).then_inc(sd_asked, 1)

            def norm(g, b):
                dve.wait_ge(sd_done, g + 2)
                c(nc.vector.reciprocal(rstd[:, :], sd[:, :]))
                c.done()
                wait(dve, t_ready, g * GB)
                for i in range(GB):
                    nc.vector.tensor_scalar(xn[:, i, :], y[:, b, i, :], mv[:, i, 0:1], rstd[:, i:i + 1],
                                            ALU.subtract, ALU.mult).then_inc(xn_ready, 1)

            def gate_logits(g):
                dve.wait_ge(gate_ready, g + 1)
                c(nc.vector.tensor_tensor(lg[:, :, :], p_t[0][:, 0:GB * E].rearrange("p (n e) -> p n e", n=GB),
                                          br[:, :].unsqueeze(1).to_broadcast([P, GB, E]), ALU.add))
                c.done()
                c(nc.vector.tensor_reduce(top[:, :], lg[:, :, :], AX.X, ALU.max))
                c.done()
                nc.vector.tensor_tensor(lg[:, :, :], lg[:, :, :], broad(top[:, :], E), ALU.subtract).then_inc(lg_ready, 1)

            def gate_weights(g, b):
                dve.wait_ge(lge_ready, g + 1)
                c(nc.vector.tensor_reduce(tot[:, :], lge[:, :, :], AX.X, ALU.add))
                c.done()
                c(nc.vector.reciprocal(tot[:, :], tot[:, :]))
                c.done()
                nc.vector.tensor_tensor(w[:, b, :, :], lge[:, :, :], broad(tot[:, :], E), ALU.mult).then_inc(w_ready, 1)

            def add(g, b, e):
                for i in range(GB):
                    v = i // 2
                    if i % 2 == 0:
                        dve.wait_ge(y_filled, g * FILLS + ((e + 1) * 4 + v + 1))
                        wait(dve, y_added, g * FILLS + e * 4 + v + 1 if e >= 0 else 0)
                    out = p_y[v % 2][:, i % 2 * D:(i % 2 + 1) * D]
                    if e < 0:
                        ins = nc.vector.tensor_tensor(y[:, b, i, :], out, y[:, b, i, :], ALU.add)
                    else:
                        ins = nc.vector.scalar_tensor_tensor(y[:, b, i, :], out, w[:, b, i, e:e + 1], y[:, b, i, :],
                                                             ALU.mult, ALU.add)
                    if i % 2 == 1 or i == GB - 1:
                        ins.then_inc(y_added, 1)

            def prepare(g):
                c.base, c.n = g * PER + start, 0

            def first():
                prepare(0)
                maxima(0)
                sums(0, 0, 0, range(GB))
                spread(0)
                norm(0, 0)
                gate_logits(0)
                gate_weights(0, 0)
                assert c.n == PER, c.n

            def main(g, b, use, more):
                add(g, b, -1)
                if more:
                    prepare(g + 1)
                    maxima(g + 1)
                for e in range(E):
                    add(g, b, e)
                    if more:
                        if e < 4:
                            sums(g + 1, 1 - b, use + b, [i for i in (2 * e, 2 * e + 1) if i < GB])
                        elif e == 4:
                            spread(g + 1)
                            norm(g + 1, 1 - b)
                        elif e == 6:
                            gate_logits(g + 1)
                if more:
                    gate_weights(g + 1, 1 - b)

            groups(dve, first, main)

        @block.scalar
        def _(act):
            act.wait_ge(sd_asked, 1)
            nc.scalar.activation(scale[:, :, :], shift[:, :, :], ACT.Sqrt).then_inc(sd_done, 1)
            act.wait_ge(bn_ready, 1)

            def exponents(g):
                for i in range(GB):
                    act.wait_ge(d_ready, g * GB + (i + 1))
                    wait(act, joined, g * GB + (i + 1 - GB))
                    nc.scalar.activation(sc[:, i, :, :], d[:, i, :, :], ACT.Exp).then_inc(sc_ready, 1)

            def root(g):
                act.wait_ge(sd_asked, g + 2)
                nc.scalar.activation(sd[:, :], var[:, :], ACT.Sqrt).then_inc(sd_done, 1)

            def turned(g, b):
                for i in range(GB):
                    act.wait_ge(t_ready, g * GB + (i + 1))
                    nc.scalar.copy(xt[:, b, :, i * P:(i + 1) * P],
                                   p_t[i % 2][:, 0:D].rearrange("p (m v) -> p m v", m=2)).then_inc(xt_ready, 1)

            def gates(g):
                act.wait_ge(lg_ready, g + 1)
                wait(act, w_ready, g)
                nc.scalar.activation(lge[:, :, :], lg[:, :, :], ACT.Exp).then_inc(lge_ready, 1)

            def weights(g, b):
                act.wait_ge(wt_turned, g + 1)
                nc.scalar.copy(wt[:, b, 0:4 * P], p_t[0][0:E, 0:4 * P])
                nc.scalar.copy(wt[:, b, 4 * P:GB * P], p_t[1][0:E, 0:(GB - 4) * P]).then_inc(wt_ready, 1)

            def keep(g, e, layer):
                out = (h1, h2)[layer]
                for r in range(4):
                    mt, half = r // 2, r % 2
                    fill = (e * 2 + layer) * 4 + r
                    act.wait_ge(h_filled, g * (E * 8) + (fill + 1))
                    nc.scalar.activation(out[:, mt, half * GN:(half + 1) * GN], p_h[r][:, 0:GN], ACT.Relu,
                                         bias=shift[:, layer, 2 * e + mt:2 * e + mt + 1],
                                         scale=scale[:, layer, 2 * e + mt:2 * e + mt + 1]).then_inc(h_kept, 1)

            def first():
                exponents(0)
                root(0)
                turned(0, 0)
                gates(0)
                weights(0, 0)

            def main(g, b, use, more):
                if more:
                    exponents(g + 1)
                keep(g, 0, 0)
                for e in range(E):
                    keep(g, e, 1)
                    if more and e == 5:
                        root(g + 1)
                    if more and e == 6:
                        turned(g + 1, 1 - b)
                    if more and e == 7:
                        gates(g + 1)
                    if e < E - 1:
                        keep(g, e + 1, 0)
                if more:
                    weights(g + 1, 1 - b)

            groups(act, first, main)

        @block.tensor
        def _(pe):
            pe.wait_ge(loaded, 96)

            def transposes(g, b):
                for i in range(GB):
                    pe.wait_ge(xn_ready, g * GB + (i + 1))
                    if i > 1:
                        pe.wait_ge(xt_ready, g * GB + (i - 1))
                    for mt in range(2):
                        last = nc.tensor.transpose(p_t[i % 2][:, mt * P:(mt + 1) * P], xn[:, i, mt * P:(mt + 1) * P],
                                                   k.ident[:, :])
                    last.then_inc(t_ready, 1)

            def gate(g, b):
                pe.wait_ge(xt_ready, g * GB + GB)
                for i in range(GB):
                    for kt in range(2):
                        last = nc.tensor.matmul(p_t[0][:, i * E:(i + 1) * E], xt[:, b, kt, i * P:(i + 1) * P],
                                                wr[:, kt, :], start=kt == 0, stop=kt == 1)
                last.then_inc(gate_ready, 1)

            def turn_weights(g, b):
                pe.wait_ge(w_ready, g + 1)
                for i in range(GB):
                    last = nc.tensor.transpose(p_t[i // 4][0:E, i % 4 * P:(i % 4 + 1) * P], w[:, b, i, :], k.ident[:, :])
                last.then_inc(wt_turned, 1)

            def layer(g, b, e, lay):
                src = xt[:, b, :, :] if lay == 0 else h1[:, :, :]
                if lay == 1:
                    pe.wait_ge(h_kept, g * (E * 8) + (e * 8 + 4))
                for r in range(4):
                    mt, half = r // 2, r % 2
                    fill = (e * 2 + lay) * 4 + r
                    wait(pe, h_kept, g * (E * 8) + (fill - 3))
                    for kt in range(2):
                        last = nc.tensor.matmul(p_h[r][:, 0:GN], wf[lay][:, e, kt, mt * P:(mt + 1) * P],
                                                src[:, kt, half * GN:(half + 1) * GN], start=kt == 0, stop=kt == 1)
                    last.then_inc(h_filled, 1)

            def outputs(g, b, e):
                if e >= 0:
                    pe.wait_ge(h_kept, g * (E * 8) + (e * 8 + 8))
                else:
                    pe.wait_ge(wt_ready, g + 1)
                for i in range(GB):
                    v = i // 2
                    if i % 2 == 0:
                        wait(pe, y_added, g * FILLS + ((e + 1) * 4 + v - 1))
                    out = p_y[v % 2][:, i % 2 * D:(i % 2 + 1) * D]
                    if e < 0:
                        last = nc.tensor.matmul(out, wt[:, b, i * P:(i + 1) * P], bo[:, :], start=True, stop=True)
                    else:
                        for kt in range(2):
                            last = nc.tensor.matmul(out, h2[:, kt, i * P:(i + 1) * P], wf[2][:, e, kt, :],
                                                    start=kt == 0, stop=kt == 1)
                    if i % 2 == 1 or i == GB - 1:
                        last.then_inc(y_filled, 1)

            def first():
                transposes(0, 0)
                gate(0, 0)
                turn_weights(0, 0)

            def main(g, b, use, more):
                outputs(g, b, -1)
                layer(g, b, 0, 0)
                for e in range(E):
                    layer(g, b, e, 1)
                    if more and e == 6:
                        transposes(g + 1, 1 - b)
                    if more and e == 7:
                        gate(g + 1, 1 - b)
                    if e < E - 1:
                        layer(g, b, e + 1, 0)
                    outputs(g, b, e)
                if more:
                    turn_weights(g + 1, 1 - b)

            groups(pe, first, main)


def gps_kernel(nc, a):
    with Scope(nc, "k") as k:
        k.iota = k.sb("iota", [P, P])
        k.iop = k.sb("iop", [P, 1])
        k.ident = k.sb("ident", [P, P])
        k.src = k.sb("src", [P, T], I32)
        k.dst = k.sb("dst", [P, T], I32)
        k.er = k.sb("er", [P, NB, 8])
        k.hist = k.sb("hist", [NB, P])
        k.restart = k.sb("restart", [P, T])
        k.same = k.sb("same", [P, T])
        k.first = k.sb("first", [P, NB], I32)
        k.last = k.sb("last", [P, NB], I32)
        k.tail = k.sb("tail", [P, NB], I32)
        k.has = k.sb("has", [P, NB])
        k.group = k.sb("group", [P, P])
        k.open = k.sb("open", [P, 1])
        k.cbd = k.sb("cbd", [P, 2, P])
        k.kbd = k.sb("kbd", [P, 2, P])
        node_pass(nc, a, k)
        index_pass(nc, a, k)
        edge_pass(nc, a, k, L1)
        hidden_pass(nc, a, k)
        edge_pass(nc, a, k, L2)
        final_pass(nc, a, k)


_SHAPES = {
    "table1": (NP, L1.table), "table2": (NP, L2.table), "er1": (NP, 8), "er2": (NP, 8), "qt": (NP, D), "res": (NP, D),
    "starts": (P * T, 8), "sums1": (P * T, L1.row), "sums2": (P * T, L2.row),
    "tails1": (P + 1, L1.row), "tails2": (P + 1, L2.row),
}


def kernel(**inputs):
    import numpy as np
    import concourse.bacc as bacc
    from concourse.bass_utils import run_bass_kernel_spmd as run

    v = {name: np.asarray(x) for name, x in inputs.items()}

    def edges(name, fill):
        out = np.full(P * T, fill, np.int32)
        out[:EDGES] = v[name]
        return out.reshape(P, T)

    def by_feature(name):
        return np.ascontiguousarray(v["L0_ffn_" + name].reshape(E, 2, P).transpose(2, 0, 1))

    x = np.zeros((NP, D), np.float32)
    x[:NODES] = v["x"]
    given = {
        "x": x, "src": edges("src", 0), "dst": edges("dst", NODES),
        "w1": v["L0_gnn_W1"], "al1": v["L0_gnn_attn_l1"].reshape(1, -1), "ar1": v["L0_gnn_attn_r1"].reshape(1, -1),
        "w2": v["L0_gnn_W2"], "al2": v["L0_gnn_attn_l2"], "ar2": v["L0_gnn_attn_r2"],
        "wq": v["L0_mix_Wq"].T, "wkv": v["L0_mix_Wkv"].T, "wproj": v["L0_mix_Wproj"].T,
        "bproj": v["L0_mix_bproj"].reshape(1, -1),
        "wr": v["L0_ffn_Wr"], "br": v["L0_ffn_br"].reshape(1, -1),
        "f1": v["L0_ffn_W1"], "f2": v["L0_ffn_W2"], "fo": v["L0_ffn_Wo"], "bo": v["L0_ffn_bo"],
        **{name: by_feature(name) for name in ("b1", "g1", "be1", "m1", "v1", "b2", "g2", "be2", "m2", "v2")},
    }
    nc = bacc.Bacc("TRN2", target_bir_lowering=False, num_devices=1)
    arrays, a = {}, {}
    for name, array in given.items():
        array = np.ascontiguousarray(array)
        arrays[f"in_{name}"] = array
        a[name] = nc.dram_tensor(f"in_{name}", array.shape, mybir.dt.from_np(array.dtype), kind="ExternalInput").ap()
    for name, shape in _SHAPES.items():
        a[name] = nc.dram_tensor(f"scratch_{name}", shape, F32, kind="Internal").ap()
    a["out"] = nc.dram_tensor("out", (NP, D), F32, kind="ExternalOutput").ap()
    gps_kernel(nc, a)
    r = run(nc, [arrays], core_ids=[0])
    return r.results[0]["out"][:NODES]
```

```python
import concourse.bass as bass
from concourse import mybir
from contextlib import ExitStack

F32 = mybir.dt.float32
BF16 = mybir.dt.bfloat16
F32R = mybir.dt.float32r
I32 = mybir.dt.int32
ALU = mybir.AluOpType
ACT = mybir.ActivationFunctionType
AX = mybir.AxisListType

P = 128
NODES = 6250
D = 256
NB = 49
NP = NB * P
EDGES = 106250
G = 17
T = NB * G
E = 8
HEADS = 8
MH = D // HEADS
BIG = 1.0e30
ROUND = 12582912.0
NONE = 4.0e6
HALVES = [(0, 9), (9, 17)]
LENGTH = [c1 - c0 for c0, c1 in HALVES]
GB = 7
GN = GB * P // 2

assert P * T >= EDGES and NP >= NODES and NB % GB == 0


class Layer:

    def __init__(self, name, heads, width, act_heads):
        self.name, self.heads, self.width = name, heads, width
        self.dim = width // heads
        self.table = width + 8
        self.row = width + 2 * heads
        self.den = width
        self.max = width + heads
        self.act_heads = act_heads


L1 = Layer("l1", 8, 512, 5)
L2 = Layer("l2", 1, 256, 1)


def wait(eng, sem, value):
    if not isinstance(value, int) or value > 0:
        eng.wait_ge(sem, value)


def sweep(eng, body):
    body(0, 0, 0)
    body(1, 1, 0)
    with eng.Fori(1, NB // 2, 1) as t:
        body(t * 2, 0, t)
        body(t * 2 + 1, 1, t)
    body(NB - 1, 0, NB // 2)


def wait_apart(eng, own, sem, value, passed):
    eng.wait_ge(sem, value)
    own.sem_inc(passed)


def groups(eng, first, main):
    last = NB // GB - 1
    first()
    main(0, 0, 0, True)
    with eng.Fori(0, (last - 2) // 2, 1) as t:
        main(t * 2 + 1, 1, t, True)
        main(t * 2 + 2, 0, t + 1, True)
    main(last - 1, 1, (last - 1) // 2, True)
    main(last, 0, last // 2, False)


class Steps:

    def __init__(self, eng, sem, passed=None):
        self.eng, self.sem, self.base, self.n = eng, sem, 0, 0
        self.passed = passed

    def __call__(self, ins):
        ins.then_inc(self.sem, 1)
        self.n += 1
        return ins

    def done(self):
        self.eng.wait_ge(self.sem, self.base + self.n)

    def block(self, n, per):
        self.base, self.n, self.per = n * per, 0, per

    def end(self):
        assert self.n == self.per, (self.n, self.per)


def broad(ap, n):
    return ap.unsqueeze(len(ap.shape)).to_broadcast([*ap.shape, n])


class Scope:

    def __init__(self, nc, tag):
        self.nc, self.tag, self.stack, self.held = nc, tag, ExitStack(), []

    def __enter__(self):
        self.stack.__enter__()
        return self

    def __exit__(self, *a):
        out = self.stack.__exit__(*a)
        if self.held and a[0] is None:
            self.nc.clear_and_free_semaphores(self.held)
            self.nc.all_engine_barrier()
        return out

    def sb(self, name, shape, dt=F32):
        return self.stack.enter_context(self.nc.sbuf_tensor(f"{self.tag}_{name}", shape, dt))

    def ps(self, name, shape, dt=F32):
        return self.stack.enter_context(self.nc.psum_tensor(f"{self.tag}_{name}", shape, dt))

    def sem(self, name):
        self.held.append(self.nc.alloc_semaphore(f"{self.tag}_{name}"))
        return self.held[-1]

    def sems(self, name, n=2):
        return [self.sem(f"{name}{i}") for i in range(n)]

    def block(self):
        return self.stack.enter_context(self.nc.Block())


def node_pass(nc, a, k):
    with Scope(nc, "na") as s:
        w1 = s.sb("w1", [P, 2, 512])
        wkv = s.sb("wkv", [P, 2, 512])
        wq = s.sb("wq", [P, 2, D])
        alr = s.sb("alr", [P, 2, 512])
        prod = s.sb("prod", [P, 512])
        wlr = s.sb("wlr", [P, 2, 16])
        io_i = s.sb("io_i", [P, P], I32)
        iop_i = s.sb("iop_i", [P, 1], I32)
        zero = s.sb("zero", [P, 2 * (P + 1) + P])
        hi_i = s.sb("hi_i", [P, T], I32)
        lo_i = s.sb("lo_i", [P, T], I32)
        hi = s.sb("hi", [P, T])
        lo = s.sb("lo", [P, T])
        oneh = s.sb("oneh", [P, 2, G, NB], BF16)
        onel = s.sb("onel", [P, 2, G, P], BF16)
        x = s.sb("x", [P, NB, D])
        qt = s.sb("qt", [P, 2, D])
        q_out, passed_sp = s.sems("q_out"), s.sem("passed_sp")
        blank = s.sb("blank", [P, T // GB * 8])
        stats = s.sb("stats", [P, NB, 6])
        mv = s.sb("mv", [P, NB, 2])
        sd = s.sb("sd", [P, NB])
        rstd = s.sb("rstd", [P, NB])
        xn = s.sb("xn", [P, 2, D])
        xt = s.sb("xt", [P, 2, 2, P])
        frow = s.sb("frow", [P, 2, L1.table])
        kmin = s.sb("kmin", [P, 2, D])
        kexp = s.sb("kexp", [P, 2, D])
        kphi = s.sb("kphi", [P, 2, D])
        vext = s.sb("vext", [P, 2, 2, P + 1])
        qmin = s.sb("qmin", [P, 2, D])
        qexp = s.sb("qexp", [P, 2, D])
        p_t = [s.ps(f"p_t{i}", [P, 512]) for i in range(2)]
        p_f = [s.ps(f"p_f{i}", [P, 512]) for i in range(2)]
        p_kv = [s.ps(f"p_kv{i}", [P, 512]) for i in range(2)]
        p_q = s.ps("p_q", [P, 512])
        p_acc = s.ps("p_acc", [P, 512])
        CW = 2 * (P + 1)
        p_c, p_h = p_acc[:, 0:CW], p_acc[0:NB, CW:CW + P]
        loaded, edges_in = s.sem("loaded"), s.sem("edges_in")
        iota_made, step = s.sem("iota_made"), s.sem("step")
        const_ready, wlr_ready = s.sem("const_ready"), s.sem("wlr_ready")
        x_in = s.sems("x_in", GB)
        passed, mv_ready, rstd_ready = s.sem("passed"), s.sem("mv_ready"), s.sem("rstd_ready")
        xn_ready, t_ready, xt_ready = s.sem("xn_ready"), s.sem("t_ready"), s.sem("xt_ready")
        proj_ready, q_ready = s.sem("proj_ready"), s.sem("q_ready")
        row_copied, row_out = s.sem("row_copied"), s.sems("row_out")
        kmin_ready, kexp_ready, kv_ready = s.sem("kmin_ready"), s.sem("kexp_ready"), s.sem("kv_ready")
        qmin_ready, qexp_ready, q_kept = s.sem("qmin_ready"), s.sem("qexp_ready"), s.sem("q_kept")
        ctx_added, onehot_ready, counted = s.sem("ctx_added"), s.sem("onehot_ready"), s.sem("counted")
        lr_copied, acc_ready, er_out = s.sem("lr_copied"), s.sem("acc_ready"), s.sem("er_out")
        blanked, blank_out = s.sem("blanked"), s.sem("blank_out")
        block = s.block()

        @block.sync
        def _(sp):
            for i in range(GB):
                n = i * GB
                sp.dma_start(x[:, n:n + GB, :], a["x"][n * P:(n + GB) * P, :].rearrange("(n p) d -> p n d", p=P)
                             ).then_inc(x_in[i], 16)
            sp.dma_start(k.dst[:, :], a["dst"]).then_inc(edges_in, 16)
            sp.dma_start(k.src[:, :], a["src"]).then_inc(edges_in, 16)
            sp.dma_start(w1[:, :, :], a["w1"].rearrange("(k p) n -> p k n", p=P)).then_inc(loaded, 16)
            sp.dma_start(wkv[:, :, :], a["wkv"].rearrange("(k p) n -> p k n", p=P)).then_inc(loaded, 16)
            sp.dma_start(wq[:, :, :], a["wq"].rearrange("(k p) n -> p k n", p=P)).then_inc(loaded, 16)
            sp.dma_start(alr[:, 0, :], a["al1"].to_broadcast([P, 512])).then_inc(loaded, 16)
            sp.dma_start(alr[:, 1, :], a["ar1"].to_broadcast([P, 512])).then_inc(loaded, 16)
            sp.wait_ge(blanked, 1)
            starts = a["starts"].rearrange("(p c t) h -> p c (t h)", p=P, c=GB)
            for i in range(GB):
                sp.dma_start(starts[:, i, :], blank[:, :]).then_inc(blank_out, 16)
            sp.wait_ge(blank_out, 16 * GB)

            def keep_queries(n, b, use):
                wait_apart(sp, nc.sync, q_kept, n + 1, passed_sp)
                sp.dma_start(a["qt"][bass.ds(n * P, P), :], qt[:, b, :]).then_inc(q_out[b], 16)

            sweep(sp, keep_queries)
            sp.wait_ge(q_out[0], 16 * (NB // 2 + 1))
            sp.wait_ge(q_out[1], 16 * (NB // 2))

        @block.gpsimd
        def _(pool):
            nc.gpsimd.iota(io_i[:, :], [[1, P]], base=0, channel_multiplier=0).then_inc(iota_made, 1)
            nc.gpsimd.iota(iop_i[:, :], [[0, 1]], base=0, channel_multiplier=1).then_inc(iota_made, 1)
            nc.gpsimd.memset(blank[:, :], 0.0).then_inc(blanked, 1)

        @block.vector
        def _(dve):
            c = Steps(dve, step, passed)
            dve.wait_ge(iota_made, 2)
            c(nc.vector.tensor_copy(k.iota[:, :], io_i[:, :]))
            c(nc.vector.tensor_copy(k.iop[:, :], iop_i[:, :]))
            c(nc.vector.memset(zero[:, :], 0.0))
            c(nc.vector.memset(vext[:, :, :, P:P + 1], 1.0))
            c.done()
            nc.vector.tensor_scalar(k.ident[:, :], k.iota[:, :], k.iop[:, 0:1], None, ALU.is_equal).then_inc(const_ready, 1)
            dve.wait_ge(edges_in, 32)
            c(nc.vector.tensor_scalar(hi_i[:, :], k.dst[:, :], 7, None, ALU.logical_shift_right))
            c(nc.vector.tensor_scalar(lo_i[:, :], k.dst[:, :], 127, None, ALU.bitwise_and))
            c.done()
            c(nc.vector.tensor_copy(hi[:, :], hi_i[:, :]))
            c(nc.vector.tensor_copy(lo[:, :], lo_i[:, :]))
            dve.wait_ge(loaded, 5 * 16)
            for kt in range(2):
                for lr in range(2):
                    c(nc.vector.tensor_tensor(prod[:, :], w1[:, kt, :], alr[:, lr, :], ALU.mult))
                    c.done()
                    c(nc.vector.tensor_reduce(wlr[:, kt, 8 * lr:8 * lr + 8],
                                              prod[:, :].rearrange("p (h d) -> p h d", h=8), AX.X, ALU.add))
                    c.done()
            nc.vector.memset(prod[:, 0:1], 0.0).then_inc(wlr_ready, 1)
            for n in range(NB):
                if n % GB == 0:
                    dve.wait_ge(x_in[n // GB], 16)
                c(nc.vector.bn_stats(stats[:, n, :], x[:, n, :]))
            c.done()
            nc.vector.sem_inc(passed)
            for n in range(NB):
                c(nc.vector.bn_aggr(mv[:, n, :], stats[:, n, :]))
            c.done()
            nc.vector.tensor_scalar(rstd[:, :], mv[:, :, 1], 1e-5, None, ALU.add).then_inc(mv_ready, 1)
            dve.wait_ge(rstd_ready, 1)
            c(nc.vector.reciprocal(rstd[:, :], sd[:, :]))
            c.done()
            start = c.n

            def norm(n, b):
                wait(dve, t_ready, n - 1)
                nc.vector.tensor_scalar(xn[:, b, :], x[:, bass.ds(n, 1), :].rearrange("p a d -> p (a d)"),
                                        mv[:, bass.ds(n, 1), 0:1].rearrange("p a d -> p (a d)"),
                                        rstd[:, bass.ds(n, 1)], ALU.subtract, ALU.mult).then_inc(xn_ready, 1)

            norm(0, 0)

            def vec(n, b, use):
                if not (isinstance(n, int) and n == NB - 1):
                    norm(n + 1, 1 - b)
                wait(dve, counted, n - 1)
                nc.vector.tensor_tensor(oneh[:, b, :, :], broad(hi[:, bass.ds(n * G, G)], NB),
                                        k.iota[:, 0:NB].unsqueeze(1).to_broadcast([P, G, NB]), ALU.is_equal)
                nc.vector.tensor_tensor(onel[:, b, :, :], broad(lo[:, bass.ds(n * G, G)], P),
                                        k.iota[:, :].unsqueeze(1).to_broadcast([P, G, P]),
                                        ALU.is_equal).then_inc(onehot_ready, 1)
                dve.wait_ge(proj_ready, n + 1)
                wait(dve, ctx_added, n - 1)
                if isinstance(n, int) and n == NB - 1:
                    nc.vector.tensor_scalar(vext[:, b, :, P:P + 1], k.iop[:, :].unsqueeze(1).to_broadcast([P, 2, 1]),
                                            float(NODES - n * P), None, ALU.is_lt)
                nc.vector.tensor_scalar(kmin[:, b, :], p_kv[b][:, 0:D], 0.0, None, ALU.min).then_inc(kmin_ready, 1)
                dve.wait_ge(q_ready, n + 1)
                nc.vector.tensor_scalar(qmin[:, b, :], p_q[:, 0:D], 0.0, None, ALU.min).then_inc(qmin_ready, 1)
                nc.vector.tensor_copy(vext[:, b, :, 0:P], p_kv[b][:, D:2 * D].rearrange("p (m v) -> p m v", m=2))
                wait(dve, row_out[b], use * 16)
                nc.vector.tensor_copy(frow[:, b, 512:520], p_q[:, D:D + 8])
                nc.vector.tensor_copy(k.er[:, bass.ds(n, 1), :].rearrange("p a h -> p (a h)"),
                                      p_q[:, D + 8:D + 16]).then_inc(lr_copied, 1)
                dve.wait_ge(kexp_ready, n + 1)
                nc.vector.scalar_tensor_tensor(kphi[:, b, :], p_kv[b][:, 0:D], 0.0, kexp[:, b, :],
                                               ALU.max, ALU.add).then_inc(kv_ready, 1)
                dve.wait_ge(qexp_ready, n + 1)
                wait(dve, q_out[b], use * 16)
                nc.vector.scalar_tensor_tensor(
                    qt[:, b, :], p_q[:, 0:D], 0.0, qexp[:, b, :], ALU.max, ALU.add).then_inc(q_kept, 1)

            sweep(dve, vec)
            dve.wait_ge(acc_ready, 1)
            c.base, c.n = start, 0
            c(nc.vector.memset(k.cbd[:, :, :], 0.0))
            c(nc.vector.memset(k.kbd[:, :, :], 0.0))
            c.done()
            for m in range(2):
                at = m * (P + 1)
                for h in range(P // MH):
                    r = slice(h * MH, (h + 1) * MH)
                    nc.vector.tensor_copy(k.cbd[r, m, r], p_c[r, at + h * MH:at + (h + 1) * MH])
                    c(nc.vector.tensor_copy(k.kbd[r, m, r], p_c[r, at + P:at + P + 1].to_broadcast([MH, MH])))
            c(nc.vector.tensor_copy(k.hist[:, :], p_h))
            c.done()

        @block.scalar
        def _(act):
            act.wait_ge(mv_ready, 1)
            nc.scalar.activation(sd[:, :], rstd[:, :], ACT.Sqrt).then_inc(rstd_ready, 1)

            def sca(n, b, use):
                act.wait_ge(t_ready, n + 1)
                wait(act, proj_ready, n - 1)
                nc.scalar.copy(xt[:, b, :, :], p_t[b][:, 0:D].rearrange("p (m v) -> p m v", m=2)).then_inc(xt_ready, 1)
                act.wait_ge(kmin_ready, n + 1)
                nc.scalar.activation(kexp[:, b, :], kmin[:, b, :], ACT.Exp).then_inc(kexp_ready, 1)
                act.wait_ge(qmin_ready, n + 1)
                nc.scalar.activation(qexp[:, b, :], qmin[:, b, :], ACT.Exp).then_inc(qexp_ready, 1)
                wait(act, row_out[b], use * 16)
                nc.scalar.copy(frow[:, b, 0:512], p_f[b][:, :]).then_inc(row_copied, 1)
                act.wait_ge(row_copied, n + 1)
                act.wait_ge(lr_copied, n + 1)
                act.dma_start(a["table1"][bass.ds(n * P, P), :], frow[:, b, :]).then_inc(row_out[b], 16)

            sweep(act, sca)
            act.dma_start(a["er1"].rearrange("(n p) h -> p n h", p=P), k.er[:, :, :]).then_inc(er_out, 16)
            act.wait_ge(er_out, 16)
            act.wait_ge(row_out[0], 16 * (NB // 2 + 1))
            act.wait_ge(row_out[1], 16 * (NB // 2))

        @block.tensor
        def _(pe):
            def transposes(n, b):
                pe.wait_ge(xn_ready, n + 1)
                wait(pe, xt_ready, n - 1)
                for m in range(2):
                    last = nc.tensor.transpose(p_t[b][:, m * P:(m + 1) * P], xn[:, b, m * P:(m + 1) * P], k.ident[:, :])
                last.then_inc(t_ready, 1)

            def products(n, b):
                pe.wait_ge(xt_ready, n + 1)
                wait(pe, row_copied, n - 1)
                for kt in range(2):
                    nc.tensor.matmul(p_f[b][:, :], xt[:, b, kt, :], w1[:, kt, :], start=kt == 0, stop=kt == 1)
                wait(pe, kv_ready, n - 1)
                for kt in range(2):
                    last = nc.tensor.matmul(p_kv[b][:, :], xt[:, b, kt, :], wkv[:, kt, :], start=kt == 0, stop=kt == 1)
                last.then_inc(proj_ready, 1)
                wait(pe, q_kept, n)
                wait(pe, lr_copied, n)
                for m in range(2):
                    for kt in range(2):
                        nc.tensor.matmul(p_q[:, m * P:(m + 1) * P], wq[:, kt, m * P:(m + 1) * P], xt[:, b, kt, :],
                                         start=kt == 0, stop=kt == 1)
                for kt in range(2):
                    last = nc.tensor.matmul(p_q[:, D:D + 16], xt[:, b, kt, :], wlr[:, kt, :], start=kt == 0, stop=kt == 1)
                last.then_inc(q_ready, 1)

            def context(n, b):
                pe.wait_ge(kv_ready, n + 1)
                pe.wait_ge(lr_copied, n + 1)
                for m in range(2):
                    last = nc.tensor.matmul(p_c[:, m * (P + 1):(m + 1) * (P + 1)], kphi[:, b, m * P:(m + 1) * P],
                                            vext[:, b, m, :], start=False, stop=False, skip_group_check=True)
                last.then_inc(ctx_added, 1)

            def count(n, b):
                pe.wait_ge(onehot_ready, n + 1)
                for g in range(G):
                    last = nc.tensor.matmul(p_h, oneh[:, b, g, :], onel[:, b, g, :],
                                            start=False, stop=False, skip_group_check=True)
                last.then_inc(counted, 1)

            pe.wait_ge(const_ready, 1)
            pe.wait_ge(wlr_ready, 1)
            pe.wait_ge(loaded, 5 * 16)
            nc.tensor.matmul(p_acc[:, 0:CW + P], zero[:, 0:P], zero[:, :], start=True, stop=False, skip_group_check=True)
            transposes(0, 0)

            def mat(n, b, use):
                products(n, b)
                if not (isinstance(n, int) and n == NB - 1):
                    transposes(n + 1, 1 - b)
                count(n, b)
                if not (isinstance(n, int) and n == 0):
                    context(n - 1, 1 - b)

            sweep(pe, mat)
            context(NB - 1, 0)
            nc.tensor.matmul(p_acc[:, 0:CW + P], zero[:, 0:P], zero[:, :], start=False, stop=True,
                             skip_group_check=True).then_inc(acc_ready, 1)


def scatter_starts(nc, a, k, pool, done):
    for n in range(NB):
        nc.gpsimd.indirect_dma_start(
            out=a["starts"], out_offset=bass.IndirectOffsetOnAxis(ap=k.first[:, n:n + 1], axis=0),
            in_=k.er[:, n, :], in_offset=None, bounds_check=P * T - 1, oob_is_err=False).then_inc(done, 16)
    pool.wait_ge(done, 16 * NB)


def index_pass(nc, a, k):
    with Scope(nc, "at") as s:
        nxt = s.sb("nxt", [P, 1], I32)
        own = s.sb("own", [P, 1])
        own_row = s.sb("own_row", [P, P])
        ones = s.sb("ones", [P, P])
        below = s.sb("below", [NB, NB])
        cum = s.sb("cum", [NB, P])
        lead = s.sb("lead", [NB, 1])
        place = s.sb("place", [NB, 3, P])
        pl = s.sb("pl", [P, 3, NB])
        strip = s.sb("strip", [P, 2, NB])
        cross = s.sb("cross", [P, NB])
        p_s = s.ps("p_s", [P, 512])
        p_r = s.ps("p_r", [P, 512])
        step, nxt_in, nxt_set = s.sem("step"), s.sem("nxt_in"), s.sem("nxt_set")
        sum_asked, summed = s.sem("sum_asked"), s.sem("summed")
        turn_asked, turned = s.sem("turn_asked"), s.sem("turned")
        index_ready, scattered = s.sem("index_ready"), s.sem("scattered")
        block = s.block()

        @block.sync
        def _(sp):
            sp.wait_ge(nxt_set, 1)
            sp.dma_start(nxt[0:P - 1, :], a["dst"][1:P, 0:1],
                         allow_slow_non_contiguous=True).then_inc(nxt_in, 16)

        @block.gpsimd
        def _(pool):
            pool.wait_ge(index_ready, 1)
            scatter_starts(nc, a, k, pool, scattered)

        @block.vector
        def _(dve):
            c = Steps(dve, step)
            nc.vector.memset(nxt[:, :], -1).then_inc(nxt_set, 1)
            c(nc.vector.memset(ones[:, :], 1.0))
            c(nc.vector.tensor_scalar(below[:, :], k.iota[0:NB, 0:NB], k.iop[0:NB, 0:1], None, ALU.is_gt))
            c.done()
            c(nc.vector.tensor_tensor_scan(cum[:, :], ones[0:NB, :], k.hist[:, :], 0.0, ALU.mult, ALU.add))
            c.done()
            c(nc.vector.tensor_copy(own[:, :], k.dst[:, T - 1:T]))
            c(nc.vector.memset(k.same[:, 0:1], 0.0))
            c(nc.vector.tensor_tensor(k.same[:, 1:T], k.dst[:, 1:T], k.dst[:, 0:T - 1], ALU.is_equal))
            c.done()
            c(nc.vector.tensor_scalar(k.restart[:, :], k.same[:, :], -1.0, BIG, ALU.add, ALU.mult))
            nc.vector.tensor_scalar(own_row[:, :], k.ident[:, :], own[:, 0:1], None, ALU.mult).then_inc(sum_asked, 1)
            dve.wait_ge(nxt_in, 16)
            c(nc.vector.tensor_tensor(k.open[:, :], k.dst[:, T - 1:T], nxt[:, :], ALU.is_equal))
            dve.wait_ge(summed, 1)
            c(nc.vector.tensor_scalar(k.group[:, :], p_s[:, 0:P], own[:, 0:1], None, ALU.is_equal))
            c(nc.vector.tensor_copy(lead[:, :], p_s[0:NB, P:P + 1]))
            c.done()
            c(nc.vector.tensor_scalar(cum[:, :], cum[:, :], lead[:, 0:1], None, ALU.add))
            c(nc.vector.tensor_copy(place[:, 0, :], k.hist[:, :]))
            c.done()
            c(nc.vector.tensor_tensor(place[:, 1, :], cum[:, :], k.hist[:, :], ALU.subtract))
            nc.vector.tensor_scalar(place[:, 2, :], cum[:, :], -1.0, None, ALU.add).then_inc(turn_asked, 1)
            dve.wait_ge(turned, 1)
            c(nc.vector.tensor_copy(pl[:, :, :], p_r[:, 0:3 * NB].rearrange("p (a n) -> p a n", a=3)))
            c.done()
            c(nc.vector.tensor_scalar(k.has[:, :], pl[:, 0, :], 1.0, None, ALU.min))
            c.done()
            c(nc.vector.tensor_scalar(cross[:, :], k.has[:, :], -NONE, NONE, ALU.mult, ALU.add))
            c(nc.vector.tensor_tensor(pl[:, 2, :], pl[:, 2, :], k.has[:, :], ALU.mult))
            c.done()
            c(nc.vector.tensor_tensor(k.first[:, :], pl[:, 1, :], cross[:, :], ALU.add))
            c(nc.vector.tensor_copy(k.last[:, :], pl[:, 2, :]))
            c(nc.vector.tensor_scalar(strip[:, :, :], pl[:, 1:3, :], 0.5, 1.0 / T, ALU.add, ALU.mult))
            c.done()
            c(nc.vector.tensor_scalar(strip[:, :, :], strip[:, :, :], -0.5, ROUND, ALU.add, ALU.add))
            c.done()
            c(nc.vector.tensor_scalar(strip[:, :, :], strip[:, :, :], -ROUND, None, ALU.add))
            c.done()
            c(nc.vector.tensor_tensor(cross[:, :], strip[:, 0, :], strip[:, 1, :], ALU.is_lt))
            c.done()
            c(nc.vector.tensor_tensor(cross[:, :], cross[:, :], k.has[:, :], ALU.mult))
            c(nc.vector.tensor_scalar(strip[:, 0, :], strip[:, 0, :], -float(P), None, ALU.add))
            c.done()
            c(nc.vector.tensor_tensor(strip[:, 0, :], strip[:, 0, :], cross[:, :], ALU.mult))
            c.done()
            nc.vector.tensor_scalar(k.tail[:, :], strip[:, 0, :], float(P), None, ALU.add).then_inc(index_ready, 1)

        @block.tensor
        def _(pe):
            pe.wait_ge(sum_asked, 1)
            nc.tensor.matmul(p_s[:, 0:P], ones[:, :], own_row[:, :], start=True, stop=True)
            nc.tensor.matmul(p_s[0:NB, P:P + 1], below[:, :], cum[:, P - 1:P], start=True, stop=True).then_inc(summed, 1)
            pe.wait_ge(turn_asked, 1)
            for i in range(3):
                last = nc.tensor.transpose(p_r[:, i * NB:(i + 1) * NB], place[:, i, :], k.ident[0:NB, 0:NB])
            last.then_inc(turned, 1)


class Attention:

    def __init__(self, nc, a, k, s):
        self.nc, self.a, self.k = nc, a, k
        self.wproj = s.sb("wproj", [P, 2, D])
        self.bproj = s.sb("bproj", [P, D])
        self.q = s.sb("q", [P, 2, D])
        self.x = s.sb("x", [P, 2, D])
        self.xb = s.sb("xb", [P, 2, D])
        self.dmax = s.sb("dmax", [P, 2, D])
        self.att = s.sb("att", [P, 2, 2, P])
        self.res = s.sb("res", [P, 2, D])
        self.p_ad = [s.ps(f"p_ad{i}", [P, 512]) for i in range(2)]
        self.p_o = [s.ps(f"p_o{i}", [P, 512]) for i in range(2)]
        self.loaded, self.step, self.passed = s.sem("mix_loaded"), s.sem("mix_step"), s.sem("mix_passed")
        self.q_in, self.x_in, self.res_out = s.sems("q_in"), s.sems("x_in"), s.sems("res_out")
        self.ad_ready, self.att_ready, self.o_ready = s.sem("ad_ready"), s.sem("att_ready"), s.sem("o_ready")
        self.res_ready, self.x_added = s.sem("res_ready"), s.sem("x_added")

    def load_weights(self, sp):
        a = self.a
        sp.dma_start(self.wproj[:, :, :], a["wproj"].rearrange("(k p) n -> p k n", p=P)).then_inc(self.loaded, 16)
        sp.dma_start(self.bproj[:, :], a["bproj"].to_broadcast([P, D])).then_inc(self.loaded, 16)

    def load(self, sp, n, b):
        at = bass.ds(n * P, P)
        if not isinstance(n, int) or n >= 2:
            wait_apart(sp, self.nc.sync, self.ad_ready, n - 1, self.passed)
            wait_apart(sp, self.nc.sync, self.res_ready, n - 1, self.passed)
        sp.dma_start(self.q[:, b, :], self.a["qt"][at, :]).then_inc(self.q_in[b], 16)
        sp.dma_start(self.x[:, b, :], self.a["x"][at, :]).then_inc(self.x_in[b], 16)

    def store(self, sp, n, b):
        wait_apart(sp, self.nc.sync, self.res_ready, n + 1, self.passed)
        sp.dma_start(self.a["res"][bass.ds(n * P, P), :], self.res[:, b, :]).then_inc(self.res_out[b], 16)

    def stored(self, sp):
        sp.wait_ge(self.res_out[0], 16 * (NB // 2 + 1))
        sp.wait_ge(self.res_out[1], 16 * (NB // 2))

    def quotient(self, dve, n, b, use):
        nc, c = self.nc, Steps(dve, self.step)
        c.base = n * 2
        dve.wait_ge(self.ad_ready, n + 1)
        c(nc.vector.tensor_scalar(self.dmax[:, b, :], self.p_ad[b][:, D:2 * D], 1e-6, None, ALU.max))
        c.done()
        c(nc.vector.reciprocal(self.dmax[:, b, :], self.dmax[:, b, :]))
        c.done()
        nc.vector.tensor_tensor(self.att[:, b, :, :].rearrange("p m v -> p (m v)"), self.p_ad[b][:, 0:D],
                                self.dmax[:, b, :], ALU.mult).then_inc(self.att_ready, 1)

    def residual(self, dve, n, b, use):
        nc = self.nc
        if isinstance(n, int) and n == 0:
            dve.wait_ge(self.loaded, 32)
        dve.wait_ge(self.o_ready, n + 1)
        dve.wait_ge(self.x_in[b], use * 16 + 16)
        wait(dve, self.res_out[b], use * 16)
        nc.vector.tensor_tensor(self.xb[:, b, :], self.p_o[b][:, 0:D], self.x[:, b, :], ALU.add).then_inc(self.x_added, 1)
        dve.wait_ge(self.x_added, n + 1)
        nc.vector.tensor_tensor(self.res[:, b, :], self.xb[:, b, :], self.bproj[:, :], ALU.add).then_inc(self.res_ready, 1)

    def products(self, pe, n, b, use):
        nc, k = self.nc, self.k
        if isinstance(n, int) and n == 0:
            pe.wait_ge(self.loaded, 32)
        pe.wait_ge(self.q_in[b], use * 16 + 16)
        wait(pe, self.att_ready, n - 1)
        for m in range(2):
            q = self.q[:, b, m * P:(m + 1) * P]
            nc.tensor.matmul(self.p_ad[b][:, m * P:(m + 1) * P], k.cbd[:, m, :], q, start=True, stop=True)
            last = nc.tensor.matmul(self.p_ad[b][:, D + m * P:D + (m + 1) * P], k.kbd[:, m, :], q, start=True, stop=True)
        last.then_inc(self.ad_ready, 1)
        pe.wait_ge(self.att_ready, n + 1)
        wait(pe, self.res_ready, n - 1)
        for m in range(2):
            last = nc.tensor.matmul(self.p_o[b][:, 0:D], self.att[:, b, m, :], self.wproj[:, m, :], start=m == 0, stop=m == 1)
        last.then_inc(self.o_ready, 1)


def edge_pass(nc, a, k, L):
    H, W, R, dim, AH = L.heads, L.width, L.row, L.dim, L.act_heads
    i_ = L.name[1]
    table, er_table, sums, tails = a["table" + i_], a["er" + i_], a["sums" + i_], a["tails" + i_]
    G1 = G + 1
    with Scope(nc, "e" + i_) as s:
        er = s.sb("er", [P, T, 8])
        er0 = s.sb("er0", [P, 8])
        idx = s.sb("idx", [P, 2, G], I32)
        rows = s.sb("rows", [P, 2, G, L.table])
        ring = s.sb("ring", [P, 2, 9, R])
        z = s.sb("z", [P, H, G])
        eext = s.sb("eext", [P, H, G1])
        rflat = s.sb("rflat", [P, H * G1 + 1])
        rext = rflat[:, 0:H * G1].rearrange("p (h j) -> p h j", h=H)
        kext = s.sb("kext", [P, H, G1])
        fext = s.sb("fext", [P, H, G1])
        mext = s.sb("mext", [P, 2, H, G1])
        d = s.sb("d", [P, H, G1])
        wr = s.sb("wr", [P, 2, H, G1])
        dext = s.sb("dext", [P, 2, H, G1])
        om = s.sb("om", [P, 1])
        pen = s.sb("pen", [P, P])
        mm = s.sb("mm", [P, H])
        diag = s.sb("diag", [P, H, P])
        cand = s.sb("cand", [P, H, P])
        gm = s.sb("gm", [P, H])
        ts = s.sb("ts", [P, R])
        sc = s.sb("sc", [P, 2, H])
        tl = s.sb("tl", [P, R])
        none = s.sb("none", [1, R])
        ones = s.sb("ones", [P, P])
        p_m = [s.ps(f"p_m{i}", [P, 512]) for i in range(2)]
        p_t = s.ps("p_t", [P, 512])
        p_d = s.ps("p_d", [P, 512])
        er_in, er0_in, step, er_ready = s.sem("er_in"), s.sem("er0_in"), s.sem("step"), s.sem("er_ready")
        idx_ready, rows_in = s.sem("idx_ready"), s.sems("rows_in")
        passed, passed_sp, d_ready, wr_ready = s.sem("passed"), s.sem("passed_sp"), s.sem("d_ready"), s.sem("wr_ready")
        scaled, summed = s.sem("scaled"), s.sem("summed")
        dm_ready, den_ready = s.sems("dm_ready"), s.sem("den_ready")
        stored = s.sems("stored")
        max_asked, max_spread = s.sem("max_asked"), s.sem("max_spread")
        exp_asked, exp_done = s.sem("exp_asked"), s.sem("exp_done")
        tail_asked, tail_summed = s.sem("tail_asked"), s.sem("tail_summed")
        tail_ready, tail_out = s.sem("tail_ready"), s.sem("tail_out")
        mix = Attention(nc, a, k, s) if L is L2 else None
        block = s.block()

        @block.sync
        def _(sp):
            sp.dma_start(er[:, :, :], a["starts"].rearrange("(p t) h -> p t h", p=P)).then_inc(er_in, 16)
            out = sums.rearrange("(p t) r -> p t r", p=P)

            if mix:
                mix.load_weights(sp)
                mix.load(sp, 0, 0)

            def store(n, b, use):
                if mix and not (isinstance(n, int) and n == NB - 1):
                    mix.load(sp, n + 1, 1 - b)
                for i, (c0, c1) in enumerate(HALVES):
                    wait_apart(sp, nc.sync, summed, n * G + c1, passed_sp)
                    wait_apart(sp, nc.sync, dm_ready[i], n + 1, passed_sp)
                    sp.dma_start(out[:, bass.ds(n * G + c0, c1 - c0), :], ring[:, i, 0:c1 - c0, :]).then_inc(stored[i], 16)
                if mix:
                    mix.store(sp, n, b)

            sweep(sp, store)
            if mix:
                mix.stored(sp)
            sp.wait_ge(tail_ready, 1)
            sp.dma_start(tails[0:P, :], tl[:, :]).then_inc(tail_out, 16)
            sp.dma_start(tails[P:P + 1, :], none[:, :]).then_inc(tail_out, 16)
            sp.wait_ge(tail_out, 32)
            sp.wait_ge(stored[0], 16 * NB)
            sp.wait_ge(stored[1], 16 * NB)

        @block.gpsimd
        def _(pool):
            nc.gpsimd.indirect_dma_start(out=er0[:, :], out_offset=None, in_=er_table,
                                         in_offset=bass.IndirectOffsetOnAxis(ap=k.dst[:, 0:1], axis=0)).then_inc(er0_in, 16)

            def gather(n, b, use):
                wait(pool, summed, (n - 1) * G)
                nc.gpsimd.sem_inc(passed)
                nc.gpsimd.tensor_copy(idx[:, b, :], k.src[:, bass.ds(n * G, G)]).then_inc(idx_ready, 1)
                pool.wait_ge(idx_ready, n + 1)
                nc.gpsimd.sem_inc(passed)
                for g in range(G):
                    nc.gpsimd.indirect_dma_start(out=rows[:, b, g, :], out_offset=None, in_=table,
                                                 in_offset=bass.IndirectOffsetOnAxis(ap=idx[:, b, g:g + 1], axis=0)
                                                 ).then_inc(rows_in[b], 16)

            sweep(pool, gather)

        @block.vector
        def _(dve):
            c = Steps(dve, step)
            c(nc.vector.memset(ring[:, :, :, :], 0.0))
            c(nc.vector.memset(mext[:, 1, :, G:G1], -BIG))
            c(nc.vector.memset(dext[:, 1, :, G:G1], 0.0))
            c(nc.vector.memset(rflat[:, :], -BIG))
            c(nc.vector.memset(kext[:, :, 0:1], 0.0))
            c(nc.vector.memset(kext[:, :, 1:2], 1.0))
            c(nc.vector.memset(ones[:, :], 1.0))
            c(nc.vector.memset(none[:, :], 0.0))
            c.done()
            c(nc.vector.memset(none[:, L.max:R], -BIG))
            dve.wait_ge(er_in, 16)
            dve.wait_ge(er0_in, 16)
            c(nc.vector.tensor_copy(er[:, 0, 0:H], er0[:, 0:H]))
            c.done()
            for h in range(H):
                c(nc.vector.tensor_tensor_scan(er[:, :, h], k.same[:, :], er[:, :, h], 0.0, ALU.mult, ALU.add))
            c.done()
            nc.vector.memset(om[:, :], 0.0).then_inc(er_ready, 1)
            start = c.n

            per = 11 if AH < H else 10
            flat = "p h j -> p (h j)"

            def batch(n, b, use):
                c.block(n, per)
                c.base = n * per + start
                dve.wait_ge(rows_in[b], use * (16 * G) + 16 * G)
                c(nc.vector.tensor_tensor(z[:, :, :], rows[:, b, :, W:W + H].rearrange("p j h -> p h j"),
                                          er[:, bass.ds(n * G, G), 0:H].rearrange("p j h -> p h j"), ALU.add))
                c(nc.vector.tensor_copy(eext[:, :, 0:1], mext[:, 1 - b, :, G:G1]))
                c(nc.vector.tensor_copy(rext[:, :, 1:G1],
                                        k.restart[:, bass.ds(n * G, G)].unsqueeze(1).to_broadcast([P, H, G])))
                c.done()
                c(nc.vector.scalar_tensor_tensor(eext[:, :, 1:G1], z[:, :, :], 0.2, z[:, :, :], ALU.mult, ALU.max))
                c.done()
                c(nc.vector.tensor_tensor_scan(fext[:, :, :].rearrange(flat), rflat[:, 0:H * G1],
                                               eext[:, :, :].rearrange(flat), 0.0, ALU.add, ALU.max))
                c.done()
                wait(dve, dm_ready[1], n - 1)
                c(nc.vector.tensor_tensor_scan(mext[:, b, :, :].rearrange(flat)[:, ::-1], rflat[:, 1:H * G1 + 1][:, ::-1],
                                               fext[:, :, :].rearrange(flat)[:, ::-1], 0.0, ALU.add, ALU.max))
                c(nc.vector.tensor_tensor(eext[:, :, 0:1], eext[:, :, 0:1], rext[:, :, 1:2], ALU.add))
                c.done()
                wait(dve, wr_ready, n)
                nc.vector.tensor_tensor(d[:, :, 0:1], eext[:, :, 0:1], mext[:, b, :, 1:2], ALU.subtract)
                nc.vector.tensor_tensor(d[:, :, 1:G1], eext[:, :, 1:G1], mext[:, b, :, 1:G1], ALU.subtract).then_inc(d_ready, 1)
                dve.wait_ge(wr_ready, n + 1)
                if AH < H:
                    v = rows[:, b, :, AH * dim:W].rearrange("p j (h e) -> p j h e", h=H - AH)
                    c(nc.vector.tensor_tensor(v, v, broad(wr[:, b, AH:H, 1:G1].rearrange("p h j -> p j h"), dim), ALU.mult))
                wait(dve, stored[0], n * 16)
                wait(dve, summed, n * G)
                c(nc.vector.tensor_copy(kext[:, :, 2:G1],
                                        k.same[:, bass.ds(n * G + 1, G - 1)].unsqueeze(1).to_broadcast([P, H, G - 1])))
                by_head = "p (h e) -> p h e"
                c(nc.vector.tensor_tensor(ring[:, 0, 0, 0:W].rearrange(by_head, h=H),
                                          ring[:, 1, LENGTH[1] - 1, 0:W].rearrange(by_head, h=H),
                                          broad(wr[:, b, :, 0], dim), ALU.mult))
                wait(dve, den_ready, n)
                c.done()
                c(nc.vector.tensor_tensor(wr[:, b, :, 0:1], wr[:, b, :, 0:1], dext[:, 1 - b, :, G:G1], ALU.mult))
                dve.wait_ge(scaled, n * G + 1)
                nc.vector.tensor_tensor(ring[:, 0, 0, 0:W], ring[:, 0, 0, 0:W], rows[:, b, 0, 0:W], ALU.add).then_inc(summed, 1)
                c.done()
                nc.vector.tensor_tensor_scan(dext[:, b, :, :].rearrange(flat), kext[:, :, :].rearrange(flat),
                                             wr[:, b, :, :].rearrange(flat), 0.0, ALU.mult, ALU.add).then_inc(den_ready, 1)
                for i, (c0, c1) in enumerate(HALVES):
                    if i == 1:
                        wait(dve, stored[1], n * 16)
                    for j in range(max(c0, 1), c1):
                        if mix and j == 3:
                            mix.quotient(dve, n, b, use)
                        if mix and j == 12:
                            mix.residual(dve, n, b, use)
                        prev = ring[:, i, j - c0 - 1, 0:W] if j > c0 else ring[:, 1 - i, LENGTH[1 - i] - 1, 0:W]
                        dve.wait_ge(scaled, n * G + (j + 1))
                        dve.wait_ge(summed, n * G + j)
                        nc.vector.scalar_tensor_tensor(ring[:, i, j - c0, 0:W], prev, kext[:, 0, j + 1:j + 2],
                                                       rows[:, b, j, 0:W], ALU.mult, ALU.add).then_inc(summed, 1)
                c.end()

            sweep(dve, batch)
            c.base, c.n = NB * per + start, 0
            final = ring[:, 1, LENGTH[1] - 1, :]
            dve.wait_ge(dm_ready[1], NB)
            dve.wait_ge(summed, T)
            c(nc.vector.tensor_scalar(om[:, :], k.open[:, :], -1.0, BIG, ALU.add, ALU.mult))
            c(nc.vector.tensor_scalar(pen[:, :], k.group[:, :], -1.0, BIG, ALU.add, ALU.mult))
            c.done()
            c(nc.vector.tensor_scalar(mm[:, :], final[:, L.max:R], om[:, 0:1], None, ALU.add))
            c.done()
            for h in range(H):
                last = nc.vector.tensor_scalar(diag[:, h, :], k.ident[:, :], mm[:, h:h + 1], None, ALU.mult)
            last.then_inc(max_asked, 1)
            dve.wait_ge(max_spread, 1)
            for h in range(H):
                c(nc.vector.tensor_tensor(cand[:, h, :], p_m[h // 4][:, h % 4 * P:(h % 4 + 1) * P], pen[:, :], ALU.add))
            c.done()
            c(nc.vector.tensor_reduce(gm[:, :], cand[:, :, :], AX.X, ALU.max))
            c.done()
            nc.vector.tensor_tensor(sc[:, 0, :], mm[:, :], gm[:, :], ALU.subtract).then_inc(exp_asked, 1)
            dve.wait_ge(exp_done, 1)
            c(nc.vector.tensor_scalar(sc[:, 1, :], sc[:, 1, :], k.open[:, 0:1], None, ALU.mult))
            c.done()
            nc.vector.tensor_tensor(ts[:, 0:W].rearrange("p (h e) -> p h e", h=H),
                                    final[:, 0:W].rearrange("p (h e) -> p h e", h=H), broad(sc[:, 1, :], dim), ALU.mult)
            nc.vector.tensor_tensor(ts[:, W:W + H], final[:, W:W + H], sc[:, 1, :], ALU.mult).then_inc(tail_asked, 1)
            dve.wait_ge(tail_summed, 1)
            nc.vector.tensor_copy(tl[:, 0:W], p_t[:, 0:W])
            nc.vector.tensor_copy(tl[:, W:W + H], p_d[:, 0:H])
            nc.vector.tensor_copy(tl[:, L.max:R], gm[:, :]).then_inc(tail_ready, 1)

        @block.scalar
        def _(act):
            def weights(n, b, use):
                act.wait_ge(d_ready, n + 1)
                wait(act, summed, (n - 1) * G)
                nc.scalar.activation(wr[:, b, :, :].rearrange("p h j -> p (h j)"),
                                     d[:, :, :].rearrange("p h j -> p (h j)"), ACT.Exp).then_inc(wr_ready, 1)
                act.wait_ge(wr_ready, n + 1)
                for i, (c0, c1) in enumerate(HALVES):
                    for j in range(c0, c1):
                        for h in range(AH):
                            at = slice(h * dim, (h + 1) * dim)
                            last = nc.scalar.activation(rows[:, b, j, at], rows[:, b, j, at], ACT.Copy,
                                                        scale=wr[:, b, h, j + 1:j + 2])
                        last.then_inc(scaled, 1)
                    act.wait_ge(den_ready, n + 1)
                    wait(act, stored[i], n * 16)
                    nc.scalar.copy(ring[:, i, 0:c1 - c0, W:W + H], dext[:, b, :, 1 + c0:1 + c1].rearrange("p h j -> p j h"))
                    nc.scalar.copy(ring[:, i, 0:c1 - c0, L.max:R],
                                   mext[:, b, :, 1 + c0:1 + c1].rearrange("p h j -> p j h")).then_inc(dm_ready[i], 1)

            act.wait_ge(er_ready, 1)
            sweep(act, weights)
            act.wait_ge(exp_asked, 1)
            nc.scalar.activation(sc[:, 1, :], sc[:, 0, :], ACT.Exp).then_inc(exp_done, 1)

        @block.tensor
        def _(pe):
            if mix:
                sweep(pe, lambda n, b, use: mix.products(pe, n, b, use))
            pe.wait_ge(max_asked, 1)
            for i in range((H + 3) // 4):
                w = min(4, H) * P
                last = nc.tensor.matmul(p_m[i][:, 0:w], ones[:, :], diag[:, 4 * i:min(4 * i + 4, H), :].rearrange("p h v -> p (h v)"),
                                        start=True, stop=True)
            last.then_inc(max_spread, 1)
            pe.wait_ge(tail_asked, 1)
            nc.tensor.matmul(p_t[:, 0:W], k.group[:, :], ts[:, 0:W], start=True, stop=True)
            nc.tensor.matmul(p_d[:, 0:H], k.group[:, :], ts[:, W:W + H], start=True, stop=True).then_inc(tail_summed, 1)


def hidden_pass(nc, a, k):
    L = L1
    with Scope(nc, "hi") as s:
        w2 = s.sb("w2", [P, 4, D + 16])
        alr = s.sb("alr", [P, 2, D])
        prod = s.sb("prod", [P, 4, D])
        rows = s.sb("rows", [P, 2 * GB, 2, L.row])
        m = s.sb("m", [P, GB, 8])
        d = s.sb("d", [P, GB, 2, 8])
        sc = s.sb("sc", [P, 2, GB, 2, 8])
        q = s.sb("q", [P, 2, GB, 2, 8])
        rec = s.sb("rec", [P, GB, 8])
        agg = s.sb("agg", [P, 2, 512])
        pos = s.sb("pos", [P, 2, 512])
        neg = s.sb("neg", [P, 2, 512])
        ex = s.sb("ex", [P, 2, 512])
        hid = s.sb("hid", [P, 2, 512])
        ht = s.sb("ht", [P, 2, 4, P])
        frow = s.sb("frow", [P, 2, L2.table])
        p_t = [s.ps(f"p_t{i}", [P, 512]) for i in range(2)]
        p_f = [s.ps(f"p_f{i}", [P, 512]) for i in range(2)]
        loaded, step, wlr_ready = s.sem("loaded"), s.sem("step"), s.sem("wlr_ready")
        rows_in, d_ready, sc_ready = s.sems("rows_in", 2 * GB), s.sem("d_ready"), s.sem("sc_ready")
        agg_ready, neg_ready, pos_ready, ex_ready = s.sem("agg_ready"), s.sem("neg_ready"), s.sem("pos_ready"), s.sem("ex_ready")
        hid_ready, t_ready, ht_ready, f_ready = s.sem("hid_ready"), s.sem("t_ready"), s.sem("ht_ready"), s.sem("f_ready")
        er_kept, row_copied, row_out, er_out = s.sem("er_kept"), s.sem("row_copied"), s.sems("row_out"), s.sem("er_out")
        scattered, step1, step2 = s.sem("scattered"), s.sem("step1"), s.sem("step2")
        block = s.block()

        @block.sync
        def _(sp):
            sp.dma_start(w2[:, :, 0:D], a["w2"].rearrange("(k p) n -> p k n", p=P)).then_inc(loaded, 16)
            sp.dma_start(alr[:, 0, :], a["al2"].to_broadcast([P, D])).then_inc(loaded, 16)
            sp.dma_start(alr[:, 1, :], a["ar2"].to_broadcast([P, D])).then_inc(loaded, 16)

        def scatter(pool, n):
            pool.wait_ge(er_kept, n + 1)
            nc.gpsimd.indirect_dma_start(
                out=a["starts"], out_offset=bass.IndirectOffsetOnAxis(ap=k.first[:, n:n + 1], axis=0),
                in_=k.er[:, n, :], in_offset=None, bounds_check=P * T - 1, oob_is_err=False).then_inc(scattered, 16)

        @block.gpsimd
        def _(pool):
            for n in range(NB):
                b = n % (2 * GB)
                wait(pool, agg_ready, n - 2 * GB + 1)
                for i, (at, src) in enumerate([(k.last, a["sums1"]), (k.tail, a["tails1"])]):
                    nc.gpsimd.indirect_dma_start(out=rows[:, b, i, :], out_offset=None, in_=src,
                                                 in_offset=bass.IndirectOffsetOnAxis(ap=at[:, n:n + 1], axis=0)
                                                 ).then_inc(rows_in[b], 16)
                if n >= 2 * GB:
                    scatter(pool, n - 2 * GB)
            for n in range(NB - 2 * GB, NB):
                scatter(pool, n)
            pool.wait_ge(scattered, 16 * NB)

        @block.vector
        def _(dve):
            c, c1, c2 = Steps(dve, step), Steps(dve, step1), Steps(dve, step2)
            c(nc.vector.memset(w2[:, :, D:D + 16], 0.0))
            c.done()
            dve.wait_ge(loaded, 48)
            for lr in range(2):
                c(nc.vector.tensor_tensor(prod[:, :, :], w2[:, :, 0:D], alr[:, lr:lr + 1, :].to_broadcast([P, 4, D]), ALU.mult))
                c.done()
                c(nc.vector.tensor_reduce(w2[:, :, D + 8 * lr:D + 8 * lr + 1], prod[:, :, :], AX.X, ALU.add))
                c.done()
            nc.vector.memset(prod[:, 0, 0:1], 0.0).then_inc(wlr_ready, 1)

            def shares(g, gb):
                c1.block(g, 6)
                at = rows[:, gb * GB:(gb + 1) * GB, :, :]
                for i in range(GB):
                    if not isinstance(g, int):
                        dve.wait_ge(rows_in[gb * GB + i], (g - gb) * 16 + 32)
                    else:
                        dve.wait_ge(rows_in[gb * GB + i], g // 2 * 32 + 32)
                c1(nc.vector.tensor_tensor(m[:, :, :], at[:, :, 0, L.max:L.row], at[:, :, 1, L.max:L.row], ALU.max))
                c1.done()
                wait(dve, sc_ready, g)
                nc.vector.tensor_tensor(d[:, :, :, :], at[:, :, :, L.max:L.row],
                                        m[:, :, :].unsqueeze(2).to_broadcast([P, GB, 2, 8]), ALU.subtract).then_inc(d_ready, 1)
                dve.wait_ge(sc_ready, g + 1)
                c1(nc.vector.tensor_tensor(q[:, gb, :, :, :], at[:, :, :, L.den:L.max], sc[:, gb, :, :, :], ALU.mult))
                c1.done()
                c1(nc.vector.tensor_tensor(rec[:, :, :], q[:, gb, :, 0, :], q[:, gb, :, 1, :], ALU.add))
                c1.done()
                c1(nc.vector.reciprocal(rec[:, :, :], rec[:, :, :]))
                c1.done()
                c1(nc.vector.tensor_tensor(rec[:, :, :], rec[:, :, :], broad(k.has[:, bass.ds(g * GB, GB)], 8), ALU.mult))
                c1.done()
                c1(nc.vector.tensor_tensor(q[:, gb, :, :, :], sc[:, gb, :, :, :],
                                           rec[:, :, :].unsqueeze(2).to_broadcast([P, GB, 2, 8]), ALU.mult))
                c1.done()
                c1.end()

            def elu(n, b):
                dve.wait_ge(ex_ready, n + 1)
                wait(dve, t_ready, n - 1)
                nc.vector.scalar_tensor_tensor(hid[:, b, :], ex[:, b, :], -1.0, pos[:, b, :], ALU.add,
                                               ALU.add).then_inc(hid_ready, 1)

            def main(g, gb, gu, more):
                for i in range(GB):
                    n, b = g * GB + i, (gb + i) % 2
                    at = rows[:, gb * GB + i, :, :]
                    for j in range(2):
                        v = at[:, j, 0:512].rearrange("p (h e) -> p h e", h=8)
                        last = nc.vector.tensor_tensor(v, v, broad(q[:, gb, i, j, :], L.dim), ALU.mult)
                    last.then_inc(step2, 1)
                    dve.wait_ge(step2, n + 1)
                    wait(dve, ex_ready, n - 1)
                    nc.vector.tensor_tensor(agg[:, b, :], at[:, 0, 0:512], at[:, 1, 0:512], ALU.add).then_inc(agg_ready, 1)
                    if not (isinstance(n, int) and n == 0):
                        elu(n - 1, 1 - b)
                    dve.wait_ge(agg_ready, n + 1)
                    nc.vector.tensor_scalar(neg[:, b, :], agg[:, b, :], 0.0, None, ALU.min).then_inc(neg_ready, 1)
                    if more and i == 5:
                        shares(g + 1, 1 - gb)

            groups(dve, lambda: shares(0, 0), main)
            elu(NB - 1, 0)

        @block.scalar
        def _(act):
            def exponents(g, gb):
                act.wait_ge(d_ready, g + 1)
                wait(act, agg_ready, (g - 1) * GB)
                nc.scalar.activation(sc[:, gb, :, :, :], d[:, :, :, :], ACT.Exp).then_inc(sc_ready, 1)

            def turned(n, b):
                act.wait_ge(t_ready, n + 1)
                wait(act, f_ready, n - 1)
                nc.scalar.copy(ht[:, b, :, :].rearrange("p k v -> p (k v)"), p_t[b][:, :]).then_inc(ht_ready, 1)

            def out(n, b, use):
                act.wait_ge(f_ready, n + 1)
                wait(act, row_out[b], use * 16)
                nc.scalar.copy(frow[:, b, :], p_f[b][:, 0:L2.table]).then_inc(row_copied, 1)
                nc.scalar.copy(k.er[:, bass.ds(n, 1), :].rearrange("p a h -> p (a h)"),
                               p_f[b][:, D + 8:D + 16]).then_inc(er_kept, 1)
                act.wait_ge(row_copied, n + 1)
                act.dma_start(a["table2"][bass.ds(n * P, P), :], frow[:, b, :]).then_inc(row_out[b], 16)

            def main(g, gb, gu, more):
                for i in range(GB):
                    n, b = g * GB + i, (gb + i) % 2
                    act.wait_ge(agg_ready, n + 1)
                    wait(act, hid_ready, n - 1)
                    nc.scalar.activation(pos[:, b, :], agg[:, b, :], ACT.Relu)
                    act.wait_ge(neg_ready, n + 1)
                    nc.scalar.activation(ex[:, b, :], neg[:, b, :], ACT.Exp).then_inc(ex_ready, 1)
                    if more and i == 5:
                        exponents(g + 1, 1 - gb)
                    if not (isinstance(n, int) and n < 1):
                        turned(n - 1, 1 - b)
                    if not (isinstance(n, int) and n < 2):
                        out(n - 2, b, gu * GB + (gb * GB + i - 2) // 2)

            groups(act, lambda: exponents(0, 0), main)
            turned(NB - 1, 0)
            out(NB - 2, 1, NB // 2 - 1)
            out(NB - 1, 0, NB // 2)
            act.wait_ge(er_kept, NB)
            act.dma_start(a["er2"].rearrange("(n p) h -> p n h", p=P), k.er[:, :, :]).then_inc(er_out, 16)
            act.wait_ge(er_out, 16)
            act.wait_ge(row_out[0], 16 * (NB // 2 + 1))
            act.wait_ge(row_out[1], 16 * (NB // 2))

        @block.tensor
        def _(pe):
            pe.wait_ge(loaded, 48)
            pe.wait_ge(wlr_ready, 1)

            def transposes(n, b):
                pe.wait_ge(hid_ready, n + 1)
                wait(pe, ht_ready, n - 1)
                for kt in range(4):
                    last = nc.tensor.transpose(p_t[b][:, kt * P:(kt + 1) * P], hid[:, b, kt * P:(kt + 1) * P], k.ident[:, :])
                last.then_inc(t_ready, 1)

            def product(n, b):
                pe.wait_ge(ht_ready, n + 1)
                wait(pe, er_kept, n - 1)
                for kt in range(4):
                    last = nc.tensor.matmul(p_f[b][:, 0:D + 16], ht[:, b, kt, :], w2[:, kt, :], start=kt == 0, stop=kt == 3)
                last.then_inc(f_ready, 1)

            def mat(n, b, use):
                transposes(n, b)
                if not (isinstance(n, int) and n == 0):
                    product(n - 1, 1 - b)

            sweep(pe, mat)
            product(NB - 1, 0)


def final_pass(nc, a, k):
    L = L2
    GR = NB // GB
    FILLS = 9 * 4
    HI, LO = 0, 1
    PARTS = ((HI, HI), (HI, LO), (LO, HI))
    with Scope(nc, "fi") as s:
        SLOTS, PIECE = 3, 2
        PIECES = 3 * E // PIECE
        stage = s.sb("stage", [P, SLOTS, PIECE, 2, D])
        stage_r = s.sb("stage_r", [P, 2, E])
        wf = [s.sb(f"wf{i}", [P, 2, E, 2, D], F32R) for i in range(3)]
        bn = s.sb("bn", [P, 10, E * 2])
        scale = s.sb("scale", [P, 2, E * 2])
        shift = s.sb("shift", [P, 2, E * 2])
        wr = s.sb("wr", [P, 2, 2, E], F32R)
        br = s.sb("br", [P, E])
        bo = s.sb("bo", [E, D])
        rows = s.sb("rows", [P, GB, 2, L.row])
        m = s.sb("m", [P, GB])
        d = s.sb("d", [P, GB, 2])
        sc = s.sb("sc", [P, GB, 2])
        q = s.sb("q", [P, GB, 2])
        rec = s.sb("rec", [P, GB])
        y = s.sb("y", [P, 2, GB, D])
        stats = s.sb("stats", [P, GB, 6])
        mv = s.sb("mv", [P, GB, 2])
        var = s.sb("var", [P, GB])
        sd = s.sb("sd", [P, GB])
        rstd = s.sb("rstd", [P, GB])
        xn = s.sb("xn", [P, GB, D])
        xt = s.sb("xt", [P, 2, 2, GB * P], F32R)
        lg = s.sb("lg", [P, GB, E])
        top = s.sb("top", [P, GB])
        lge = s.sb("lge", [P, GB, E])
        tot = s.sb("tot", [P, GB])
        w = s.sb("w", [P, 2, GB, E])
        wt = s.sb("wt", [E, GB * P])
        full = s.sb("full", [P, 4, GN])
        h = [s.sb(f"h{i}", [P, 2, 2, GB * P], F32R) for i in range(2)]
        p_h = [s.ps(f"p_h{i}", [P, 512]) for i in range(4)]
        p_y = [s.ps(f"p_y{i}", [P, 512]) for i in range(2)]
        p_t = [s.ps(f"p_t{i}", [P, 512]) for i in range(2)]
        loaded, bn_in, step, bn_ready = s.sems("loaded", SLOTS), s.sem("bn_in"), s.sem("step"), s.sem("bn_ready")
        sd_asked, sd_done, passed = s.sem("sd_asked"), s.sem("sd_done"), s.sem("passed")
        wf_hi, wf_split, gate_step = s.sem("wf_hi"), s.sem("wf_split"), s.sem("gate_step")
        rows_in, res_in, joined = s.sems("rows_in", GB), s.sem("res_in"), s.sem("joined")
        d_ready, sc_ready, x_ready = s.sem("d_ready"), s.sem("sc_ready"), s.sem("x_ready")
        xn_ready, t_ready, xt_hi, xt_ready = s.sem("xn_ready"), s.sem("t_ready"), s.sem("xt_hi"), s.sem("xt_ready")
        gate_ready, lg_ready, lge_ready = s.sem("gate_ready"), s.sem("lg_ready"), s.sem("lge_ready")
        w_ready, wt_turned, wt_ready = s.sem("w_ready"), s.sem("wt_turned"), s.sem("wt_ready")
        h_filled, h_kept, h_ready = s.sem("h_filled"), s.sem("h_kept"), s.sem("h_ready")
        y_filled, y_added, y_out = s.sem("y_filled"), s.sem("y_added"), s.sems("y_out")
        small_in, wr_in = s.sem("small_in"), s.sem("wr_in")
        block = s.block()

        def piece(j):
            i, e = j * PIECE // E, slice(j * PIECE % E, j * PIECE % E + PIECE)
            return ("f1", "f2", "fo")[i], e, stage[:, j % SLOTS, :, :, :], wf[i][:, HI, e, :, :], wf[i][:, LO, e, :, :]

        @block.sync
        def _(sp):
            def load(g, b, use):
                wait(sp, y_out[b], use * 16)
                if not isinstance(use, int):
                    nc.sync.sem_inc(passed)
                sp.dma_start(y[:, b, :, :], a["res"][bass.ds(g * (GB * P), GB * P), :].rearrange("(n p) d -> p n d", p=P)
                             ).then_inc(res_in, 16)

            def first():
                load(0, 0, 0)
                for i, name in enumerate(("b1", "g1", "be1", "m1", "v1", "b2", "g2", "be2", "m2", "v2")):
                    sp.dma_start(bn[:, i, :], a[name].rearrange("p e k -> p (e k)")).then_inc(bn_in, 16)
                sp.dma_start(stage_r[:, :, :], a["wr"].rearrange("(k p) n -> p k n", p=P)).then_inc(wr_in, 16)
                sp.dma_start(br[:, :], a["br"].to_broadcast([P, E])).then_inc(small_in, 16)
                sp.dma_start(bo[:, :], a["bo"]).then_inc(small_in, 16)
                for j in range(PIECES):
                    name, e, place, hi, lo = piece(j)
                    wait(sp, wf_split, j - SLOTS + 2)
                    sp.dma_start(place, a[name][e, :, :].rearrange("e (k p) n -> p e k n", p=P)
                                 ).then_inc(loaded[j % SLOTS], 16)

            def main(g, b, use, more):
                if more:
                    load(g + 1, 1 - b, use + b)
                wait_apart(sp, nc.sync, y_added, (g + 1) * FILLS, passed)
                sp.dma_start(a["out"][bass.ds(g * (GB * P), GB * P), :].rearrange("(n p) d -> p n d", p=P),
                             y[:, b, :, :]).then_inc(y_out[b], 16)

            groups(sp, first, main)
            sp.wait_ge(y_out[0], 16 * (GR // 2 + 1))
            sp.wait_ge(y_out[1], 16 * (GR // 2))

        @block.gpsimd
        def _(pool):
            for n in range(NB):
                wait(pool, joined, n - GB + 1)
                for i, (at, src) in enumerate([(k.last, a["sums2"]), (k.tail, a["tails2"])]):
                    nc.gpsimd.indirect_dma_start(out=rows[:, n % GB, i, :], out_offset=None, in_=src,
                                                 in_offset=bass.IndirectOffsetOnAxis(ap=at[:, n:n + 1], axis=0)
                                                 ).then_inc(rows_in[n % GB], 16)

        @block.vector
        def _(dve):
            c, cg = Steps(dve, step, passed), Steps(dve, gate_step)
            dve.wait_ge(bn_in, 160)
            for i in range(2):
                last = nc.vector.tensor_scalar(shift[:, i, :], bn[:, 5 * i + 4, :], 1e-3, None, ALU.add)
            last.then_inc(sd_asked, 1)
            dve.wait_ge(sd_done, 1)
            c(nc.vector.reciprocal(scale[:, :, :], scale[:, :, :]))
            c.done()
            for i in range(2):
                c(nc.vector.tensor_tensor(scale[:, i, :], scale[:, i, :], bn[:, 5 * i + 1, :], ALU.mult))
                c(nc.vector.tensor_tensor(shift[:, i, :], bn[:, 5 * i, :], bn[:, 5 * i + 3, :], ALU.subtract))
            c.done()
            for i in range(2):
                c(nc.vector.tensor_tensor(shift[:, i, :], shift[:, i, :], scale[:, i, :], ALU.mult))
            c.done()
            for i in range(2):
                last = nc.vector.tensor_tensor(shift[:, i, :], shift[:, i, :], bn[:, 5 * i + 2, :], ALU.add)
            last.then_inc(bn_ready, 1)
            dve.wait_ge(small_in, 32)
            start = c.n
            SHARES, SUMS = 6, 2 * GB + GB - 1
            PER = SHARES + SUMS + GB + 1

            def low(pieces):
                for j in pieces:
                    name, e, place, hi, lo = piece(j)
                    dve.wait_ge(wf_hi, j + 2)
                    nc.vector.tensor_tensor(lo, place, hi.bitcast(F32), ALU.subtract).then_inc(wf_split, 1)

            def below(g):
                for i in range(GB):
                    dve.wait_ge(rows_in[i], g * 32 + 32)
                c(nc.vector.tensor_tensor(m[:, :], rows[:, :, 0, L.max], rows[:, :, 1, L.max], ALU.max))
                c.done()
                nc.vector.tensor_tensor(d[:, :, :], rows[:, :, :, L.max], broad(m[:, :], 2), ALU.subtract).then_inc(d_ready, 1)

            def shares(g):
                dve.wait_ge(sc_ready, g + 1)
                c(nc.vector.tensor_tensor(q[:, :, :], rows[:, :, :, L.den], sc[:, :, :], ALU.mult))
                c.done()
                c(nc.vector.tensor_tensor(rec[:, :], q[:, :, 0], q[:, :, 1], ALU.add))
                c.done()
                c(nc.vector.reciprocal(rec[:, :], rec[:, :]))
                c.done()
                c(nc.vector.tensor_tensor(rec[:, :], rec[:, :], k.has[:, bass.ds(g * GB, GB)], ALU.mult))
                c.done()
                c(nc.vector.tensor_tensor(q[:, :, :], sc[:, :, :], broad(rec[:, :], 2), ALU.mult))
                c.done()

            def weigh(i):
                c(nc.vector.tensor_tensor(rows[:, i, :, 0:D], rows[:, i, :, 0:D], broad(q[:, i, :], D), ALU.mult))

            def join(g, b, i):
                c.done()
                if i == 0:
                    dve.wait_ge(res_in, g * 16 + 16)
                c(nc.vector.tensor_tensor(y[:, b, i, :], rows[:, i, 0, 0:D], y[:, b, i, :], ALU.add))
                c.done()
                nc.vector.tensor_tensor(y[:, b, i, :], rows[:, i, 1, 0:D], y[:, b, i, :], ALU.add).then_inc(joined, 1)
                dve.wait_ge(joined, g * GB + i + 1)
                ins = nc.vector.bn_stats(stats[:, i, :], y[:, b, i, :])
                if i < GB - 1:
                    c(ins)
                else:
                    ins.then_inc(x_ready, 1)

            def spread(g):
                dve.wait_ge(x_ready, g + 1)
                nc.vector.sem_inc(passed)
                for i in range(GB):
                    c(nc.vector.bn_aggr(mv[:, i, :], stats[:, i, :]))
                c.done()
                nc.vector.tensor_scalar(var[:, :], mv[:, :, 1], 1e-5, None, ALU.add).then_inc(sd_asked, 1)

            def inverse(g):
                dve.wait_ge(sd_done, g + 2)
                c(nc.vector.reciprocal(rstd[:, :], sd[:, :]))
                c.done()
                wait(dve, t_ready, g * GB)

            def norm(b, i):
                nc.vector.tensor_scalar(xn[:, i, :], y[:, b, i, :], mv[:, i, 0:1], rstd[:, i:i + 1],
                                        ALU.subtract, ALU.mult).then_inc(xn_ready, 1)

            def turned_low(g, i):
                dve.wait_ge(xt_hi, g * GB + (i + 1))
                at = slice(i * P, (i + 1) * P)
                nc.vector.tensor_tensor(xt[:, LO, :, at], p_t[i % 2][:, 0:D].rearrange("p (m v) -> p m v", m=2),
                                        xt[:, HI, :, at].bitcast(F32), ALU.subtract).then_inc(xt_ready, 1)

            def gates(g, b):
                cg.block(g, 4)
                dve.wait_ge(gate_ready, g + 1)
                cg(nc.vector.tensor_tensor(lg[:, :, :], p_t[0][:, 0:GB * E].rearrange("p (n e) -> p n e", n=GB),
                                           br[:, :].unsqueeze(1).to_broadcast([P, GB, E]), ALU.add))
                cg.done()
                cg(nc.vector.tensor_reduce(top[:, :], lg[:, :, :], AX.X, ALU.max))
                cg.done()
                nc.vector.tensor_tensor(lg[:, :, :], lg[:, :, :], broad(top[:, :], E), ALU.subtract).then_inc(lg_ready, 1)
                dve.wait_ge(lge_ready, g + 1)
                cg(nc.vector.tensor_reduce(tot[:, :], lge[:, :, :], AX.X, ALU.add))
                cg.done()
                cg(nc.vector.reciprocal(tot[:, :], tot[:, :]))
                cg.done()
                cg.end()
                nc.vector.tensor_tensor(w[:, b, :, :], lge[:, :, :], broad(tot[:, :], E), ALU.mult).then_inc(w_ready, 1)

            def low_part(g, e, layer, r):
                mt, half = r // 2, r % 2
                at = slice(half * GN, (half + 1) * GN)
                dve.wait_ge(h_kept, g * (E * 8) + ((e * 2 + layer) * 4 + r + 1))
                nc.vector.tensor_tensor(h[layer][:, LO, mt, at], full[:, r, :], h[layer][:, HI, mt, at].bitcast(F32),
                                        ALU.subtract).then_inc(h_ready, 1)

            def add(g, b, e, v):
                dve.wait_ge(y_filled, g * FILLS + ((e + 1) * 4 + v + 1))
                wait(dve, y_added, g * FILLS + e * 4 + v + 1 if e >= 0 else 0)
                for i in range(2 * v, min(2 * v + 2, GB)):
                    out = p_y[v % 2][:, i % 2 * D:(i % 2 + 1) * D]
                    if e < 0:
                        ins = nc.vector.tensor_tensor(y[:, b, i, :], out, y[:, b, i, :], ALU.add)
                    else:
                        ins = nc.vector.scalar_tensor_tensor(y[:, b, i, :], out, w[:, b, i, e:e + 1], y[:, b, i, :],
                                                             ALU.mult, ALU.add)
                ins.then_inc(y_added, 1)

            def first():
                dve.wait_ge(wf_hi, 1)
                nc.vector.tensor_tensor(wr[:, LO, :, :], stage_r[:, :, :], wr[:, HI, :, :].bitcast(F32),
                                        ALU.subtract).then_inc(wf_split, 1)
                c.base, c.n = start, 0
                below(0)
                shares(0)
                low(range(0, 3))
                for i in range(GB):
                    weigh(i)
                    join(0, 0, i)
                low(range(3, 6))
                spread(0)
                inverse(0)
                for i in range(GB):
                    norm(0, i)
                assert c.n == PER, c.n
                low(range(6, 9))
                for i in range(GB):
                    turned_low(0, i)
                low(range(9, PIECES))

            def main(g, b, use, more):
                gates(g, b)
                for r in range(4):
                    low_part(g, 0, 0, r)
                c.base, c.n = (g + 1) * PER + start, 0
                for e in range(E):
                    for r in range(4):
                        low_part(g, e, 1, r)
                        i = 2 * e - 2 + r // 2
                        if more and 1 <= e < 5 and i < GB:
                            if r % 2 == 0:
                                weigh(i)
                            else:
                                join(g + 1, 1 - b, i)
                    if more and e == 0:
                        below(g + 1)
                    if more and e == 5:
                        inverse(g + 1)
                    for v in range(4):
                        if e < E - 1:
                            for r in ((0, 1, 2), (3,), (), ())[v]:
                                low_part(g, e + 1, 0, r)
                                if more and e == 5:
                                    for i in range(2 * r, min(2 * r + 2, GB)):
                                        norm(1 - b, i)
                        elif more:
                            for i in range(2 * v, min(2 * v + 2, GB)):
                                turned_low(g + 1, i)
                        if e == 0:
                            add(g, b, -1, v)
                        else:
                            add(g, b, e, v)
                    if e == 0:
                        for v in range(4):
                            add(g, b, 0, v)
                    if more and e == 0:
                        shares(g + 1)
                    if more and e == 4:
                        spread(g + 1)

            groups(dve, first, main)

        @block.scalar
        def _(act):
            act.wait_ge(sd_asked, 1)
            nc.scalar.activation(scale[:, :, :], shift[:, :, :], ACT.Sqrt).then_inc(sd_done, 1)

            def high(pieces):
                for j in pieces:
                    name, e, place, hi, lo = piece(j)
                    act.wait_ge(loaded[j % SLOTS], 16 * (j // SLOTS + 1))
                    nc.scalar.copy(hi, place).then_inc(wf_hi, 1)

            def exponents(g):
                act.wait_ge(d_ready, g + 1)
                wait(act, joined, g * GB)
                nc.scalar.activation(sc[:, :, :], d[:, :, :], ACT.Exp).then_inc(sc_ready, 1)

            def root(g):
                act.wait_ge(sd_asked, g + 2)
                nc.scalar.activation(sd[:, :], var[:, :], ACT.Sqrt).then_inc(sd_done, 1)

            def turned(g):
                for i in range(GB):
                    act.wait_ge(t_ready, g * GB + (i + 1))
                    nc.scalar.copy(xt[:, HI, :, i * P:(i + 1) * P],
                                   p_t[i % 2][:, 0:D].rearrange("p (m v) -> p m v", m=2)).then_inc(xt_hi, 1)

            def gates(g):
                act.wait_ge(lg_ready, g + 1)
                wait(act, w_ready, g)
                nc.scalar.activation(lge[:, :, :], lg[:, :, :], ACT.Exp).then_inc(lge_ready, 1)

            def weights(g):
                act.wait_ge(wt_turned, g + 1)
                nc.scalar.copy(wt[:, 0:4 * P], p_t[0][0:E, 0:4 * P])
                nc.scalar.copy(wt[:, 4 * P:GB * P], p_t[1][0:E, 0:(GB - 4) * P]).then_inc(wt_ready, 1)

            def keep(g, e, layer):
                for r in range(4):
                    mt, half = r // 2, r % 2
                    fill = (e * 2 + layer) * 4 + r
                    act.wait_ge(h_filled, g * (E * 8) + (fill + 1))
                    wait(act, h_ready, g * (E * 8) + (fill - 3))
                    for out in (h[layer][:, HI, mt, half * GN:(half + 1) * GN], full[:, r, :]):
                        last = nc.scalar.activation(out, p_h[r][:, 0:GN], ACT.Relu,
                                                    bias=shift[:, layer, 2 * e + mt:2 * e + mt + 1],
                                                    scale=scale[:, layer, 2 * e + mt:2 * e + mt + 1])
                    last.then_inc(h_kept, 1)

            def first():
                act.wait_ge(wr_in, 16)
                nc.scalar.copy(wr[:, HI, :, :], stage_r[:, :, :]).then_inc(wf_hi, 1)
                exponents(0)
                high(range(0, 6))
                root(0)
                high(range(6, 9))
                turned(0)
                high(range(9, PIECES))
                act.wait_ge(bn_ready, 1)

            def main(g, b, use, more):
                gates(g)
                keep(g, 0, 0)
                weights(g)
                for e in range(E):
                    keep(g, e, 1)
                    if more and e == 5:
                        root(g + 1)
                    if e < E - 1:
                        keep(g, e + 1, 0)
                        if more and e == 0:
                            exponents(g + 1)
                    elif more:
                        turned(g + 1)

            groups(act, first, main)

        @block.tensor
        def _(pe):
            def transposes(g, i):
                pe.wait_ge(xn_ready, g * GB + (i + 1))
                if i > 1:
                    pe.wait_ge(xt_ready, g * GB + (i - 1))
                for mt in range(2):
                    last = nc.tensor.transpose(p_t[i % 2][:, mt * P:(mt + 1) * P], xn[:, i, mt * P:(mt + 1) * P],
                                               k.ident[:, :])
                last.then_inc(t_ready, 1)

            def product(out, left, right):
                for kt in range(2):
                    for pl, pr in PARTS:
                        last = nc.tensor.matmul(out, left(pl, kt), right(pr, kt), start=kt == 0 and (pl, pr) == PARTS[0],
                                                stop=kt == 1 and (pl, pr) == PARTS[-1])
                return last

            def gate(g):
                pe.wait_ge(xt_ready, g * GB + GB)
                for i in range(GB):
                    last = product(p_t[0][:, i * E:(i + 1) * E], lambda part, kt: xt[:, part, kt, i * P:(i + 1) * P],
                                   lambda part, kt: wr[:, part, kt, :])
                last.then_inc(gate_ready, 1)

            def turn_weights(g, b):
                pe.wait_ge(w_ready, g + 1)
                for i in range(GB):
                    last = nc.tensor.transpose(p_t[i // 4][0:E, i % 4 * P:(i % 4 + 1) * P], w[:, b, i, :], k.ident[:, :])
                last.then_inc(wt_turned, 1)

            def layer(g, e, lay):
                src = (xt, h[0])[lay]
                if lay == 1:
                    pe.wait_ge(h_ready, g * (E * 8) + (e * 8 + 4))
                for r in range(4):
                    mt, half = r // 2, r % 2
                    fill = (e * 2 + lay) * 4 + r
                    wait(pe, h_kept, g * (E * 8) + (fill - 3))
                    product(p_h[r][:, 0:GN], lambda part, kt: wf[lay][:, part, e, kt, mt * P:(mt + 1) * P],
                            lambda part, kt: src[:, part, kt, half * GN:(half + 1) * GN]).then_inc(h_filled, 1)

            def outputs(g, e, v):
                if e < 0:
                    pe.wait_ge(wt_ready, g + 1)
                elif v == 0:
                    pe.wait_ge(h_ready, g * (E * 8) + (e * 8 + 8))
                wait(pe, y_added, g * FILLS + ((e + 1) * 4 + v - 1))
                for i in range(2 * v, min(2 * v + 2, GB)):
                    out = p_y[v % 2][:, i % 2 * D:(i % 2 + 1) * D]
                    if e < 0:
                        last = nc.tensor.matmul(out, wt[:, i * P:(i + 1) * P], bo[:, :], start=True, stop=True)
                    else:
                        last = product(out, lambda part, kt: h[1][:, part, kt, i * P:(i + 1) * P],
                                       lambda part, kt: wf[2][:, part, e, kt, :])
                last.then_inc(y_filled, 1)

            def first():
                for i in range(GB):
                    transposes(0, i)
                pe.wait_ge(small_in, 32)
                pe.wait_ge(wf_split, 1)
                gate(0)
                pe.wait_ge(wf_split, 1 + PIECES)

            def main(g, b, use, more):
                layer(g, 0, 0)
                turn_weights(g, b)
                for e in range(E):
                    layer(g, e, 1)
                    if e < E - 1:
                        layer(g, e + 1, 0)
                    if e == 0:
                        for v in range(4):
                            outputs(g, -1, v)
                    for v in range(4):
                        if more and e == E - 1:
                            for i in range(2 * v, min(2 * v + 2, GB)):
                                transposes(g + 1, i)
                        outputs(g, e, v)
                if more:
                    gate(g + 1)

            groups(pe, first, main)


def gps_kernel(nc, a):
    with Scope(nc, "k") as k:
        k.iota = k.sb("iota", [P, P])
        k.iop = k.sb("iop", [P, 1])
        k.ident = k.sb("ident", [P, P])
        k.er = k.sb("er", [P, NB, 8])
        k.hist = k.sb("hist", [NB, P])
        k.first = k.sb("first", [P, NB], I32)
        k.last = k.sb("last", [P, NB], I32)
        k.tail = k.sb("tail", [P, NB], I32)
        k.has = k.sb("has", [P, NB])
        k.group = k.sb("group", [P, P])
        k.open = k.sb("open", [P, 1])
        k.cbd = k.sb("cbd", [P, 2, P])
        k.kbd = k.sb("kbd", [P, 2, P])
        with Scope(nc, "ed") as edges:
            k.src = edges.sb("src", [P, T], I32)
            k.dst = edges.sb("dst", [P, T], I32)
            k.restart = edges.sb("restart", [P, T])
            k.same = edges.sb("same", [P, T])
            node_pass(nc, a, k)
            index_pass(nc, a, k)
            edge_pass(nc, a, k, L1)
            hidden_pass(nc, a, k)
            edge_pass(nc, a, k, L2)
        final_pass(nc, a, k)


_SHAPES = {
    "table1": (NP, L1.table), "table2": (NP, L2.table), "er1": (NP, 8), "er2": (NP, 8), "qt": (NP, D), "res": (NP, D),
    "starts": (P * T, 8), "sums1": (P * T, L1.row), "sums2": (P * T, L2.row),
    "tails1": (P + 1, L1.row), "tails2": (P + 1, L2.row),
}


def kernel(**inputs):
    import numpy as np
    import concourse.bacc as bacc
    from concourse.bass_utils import run_bass_kernel_spmd as run

    v = {name: np.asarray(x) for name, x in inputs.items()}

    def edges(name, fill):
        out = np.full(P * T, fill, np.int32)
        out[:EDGES] = v[name]
        return out.reshape(P, T)

    def by_feature(name):
        return np.ascontiguousarray(v["L0_ffn_" + name].reshape(E, 2, P).transpose(2, 0, 1))

    x = np.zeros((NP, D), np.float32)
    x[:NODES] = v["x"]
    given = {
        "x": x, "src": edges("src", 0), "dst": edges("dst", NODES),
        "w1": v["L0_gnn_W1"], "al1": v["L0_gnn_attn_l1"].reshape(1, -1), "ar1": v["L0_gnn_attn_r1"].reshape(1, -1),
        "w2": v["L0_gnn_W2"], "al2": v["L0_gnn_attn_l2"], "ar2": v["L0_gnn_attn_r2"],
        "wq": v["L0_mix_Wq"].T, "wkv": v["L0_mix_Wkv"].T, "wproj": v["L0_mix_Wproj"].T,
        "bproj": v["L0_mix_bproj"].reshape(1, -1),
        "wr": v["L0_ffn_Wr"], "br": v["L0_ffn_br"].reshape(1, -1),
        "f1": v["L0_ffn_W1"], "f2": v["L0_ffn_W2"], "fo": v["L0_ffn_Wo"], "bo": v["L0_ffn_bo"],
        **{name: by_feature(name) for name in ("b1", "g1", "be1", "m1", "v1", "b2", "g2", "be2", "m2", "v2")},
    }
    nc = bacc.Bacc("TRN2", target_bir_lowering=False, num_devices=1)
    arrays, a = {}, {}
    for name, array in given.items():
        array = np.ascontiguousarray(array)
        arrays[f"in_{name}"] = array
        a[name] = nc.dram_tensor(f"in_{name}", array.shape, mybir.dt.from_np(array.dtype), kind="ExternalInput").ap()
    for name, shape in _SHAPES.items():
        a[name] = nc.dram_tensor(f"scratch_{name}", shape, F32, kind="Internal").ap()
    a["out"] = nc.dram_tensor("out", (NP, D), F32, kind="ExternalOutput").ap()
    gps_kernel(nc, a)
    r = run(nc, [arrays], core_ids=[0])
    return r.results[0]["out"][:NODES]
```
